# Optimizing a Trainium2 kernel written in Bass

```python
import numpy as np
import jax
import jax.numpy as jnp

def _softmax(x, axis=-1):
    return jax.nn.softmax(x, axis=axis)

def _gelu(x):
    return jax.nn.gelu(x, approximate=True)

def _silu(x):
    return jax.nn.silu(x)

def _sigmoid(x):
    return jax.nn.sigmoid(x)

def _layernorm(x, axis=-1, eps=1e-05):
    m = jnp.mean(x, axis=axis, keepdims=True)
    v = jnp.var(x, axis=axis, keepdims=True)
    return (x - m) / jnp.sqrt(v + eps)

def _scatter_add(tgt, idx, src, axis=0):
    return tgt.at[idx].add(src)

def _segment_sum(src, seg, n):
    return jax.ops.segment_sum(src, seg, n)
kernel_name = 'mk_decoder_preln_d2_seqx_r8_17c77f'

def setup_inputs(seed: int=0):
    np.random.seed(seed)
    _w = jnp.asarray

    def _rec_inputs():
        import jax
        import jax.numpy as jnp
        _rk = jax.random.key(seed)
        x = 2.818e-05 + 1 * jax.random.normal(jax.random.fold_in(_rk, 1), (32, 128, 128), jnp.float32)
        _lenS = 128 - jax.random.randint(jax.random.fold_in(_rk, 7), (32,), 0, max(1, 128 // 4) + 1, jnp.int32)
        _lenS2 = 128 - jax.random.randint(jax.random.fold_in(_rk, 8), (32,), 0, max(1, 128 // 4) + 1, jnp.int32)
        _ctx_2048P = jax.random.normal(jax.random.fold_in(_rk, 11), (32, 16, 256), jnp.float32)
        _ctx_2048c = jax.random.dirichlet(jax.random.fold_in(_rk, 511), 0.3 * jnp.ones((16,), jnp.float32), (32, 128))
        _ctx_2048t = jnp.einsum('bsk,bkd->bsd', _ctx_2048c, _ctx_2048P)
        _ctx_2048t = _ctx_2048t * jax.lax.rsqrt(jnp.mean(jnp.square(_ctx_2048t)) + 1e-12) * 0.953939
        ctx_2048 = -0.000125008 + 0.999885 * (_ctx_2048t + 0.3 * jax.random.normal(jax.random.fold_in(_rk, 611), (32, 128, 256), jnp.float32))
        _validS = jnp.arange(128)[None, :] < _lenS[:, None]
        _validS2 = jnp.arange(128)[None, :] < _lenS2[:, None]
        _causal = jnp.tril(jnp.ones((128, 128), dtype=bool))
        mask_BxS2_fk1 = jnp.where(jnp.broadcast_to(_validS2[:, :], (32, 128)), 1.0, 0.0).astype(jnp.float32)
        mask_BxS2_if0 = jnp.where(jnp.ones((32, 128), dtype=bool), 4, 0).astype(jnp.int32)
        return (x, ctx_2048, mask_BxS2_fk1, mask_BxS2_if0)
    x, ctx_2048, mask_BxS2_fk1, mask_BxS2_if0 = _rec_inputs()

    def _L0_attn_setup():
        import jax, jax.numpy as jnp
        import numpy as np
        DIM = 128
        NUM_HEADS = 16
        NUM_GROUPS = 8

        def grouped_linear(x, w, b):
            B, N, Cin = x.shape
            G = w.shape[0]
            xg = x.reshape(B, N, G, Cin // G)
            out = jnp.einsum('bngi,gio->bngo', xg, w)
            out = out.reshape(B, N, -1)
            if b is not None:
                out = out + b
            return out
        key = jax.random.key(seed)
        k1, k2, k3, k4 = jax.random.split(key, 4)
        G = NUM_GROUPS
        x = jax.random.normal(k1, (2, 256, DIM), dtype=jnp.float32)
        w_qkv = jax.random.normal(k2, (G, DIM // G, 3 * DIM // G), dtype=jnp.float32) * (DIM // G) ** (-0.5)
        w_proj = jax.random.normal(k3, (G, DIM // G, DIM // G), dtype=jnp.float32) * (DIM // G) ** (-0.5)
        b_proj = jax.random.normal(k4, (DIM,), dtype=jnp.float32) * 0.02
        return {'x': x, 'w_qkv': w_qkv, 'w_proj': w_proj, 'b_proj': b_proj}
    _L0_attn_all = _L0_attn_setup()
    _L0_attn_in = {k: v for k, v in _L0_attn_all.items() if k in ('w_qkv', 'w_proj', 'b_proj')}
    del _L0_attn_all

    def _L0_xattn_setup():
        import jax, jax.numpy as jnp
        import numpy as np
        B, S, T = (32, 64, 64)
        SRC_SIZE, TGT_SIZE, OUT_SIZE, NUM_HEAD = (256, 128, 128, 8)
        HEAD_DIM = OUT_SIZE // NUM_HEAD
        key = jax.random.key(seed)
        ks = jax.random.split(key, 12)
        src = jax.random.normal(ks[0], (B, S, SRC_SIZE), dtype=jnp.float32)
        tgt = jax.random.normal(ks[1], (B, T, TGT_SIZE), dtype=jnp.float32)
        src_mask = (jax.random.uniform(ks[2], (B, S)) > 0.3).astype(jnp.float32)
        src_mask = src_mask.at[:, 0].set(1.0)
        tgt_mask = (jax.random.uniform(ks[3], (B, T)) > 0.3).astype(jnp.float32)
        tgt_mask = tgt_mask.at[:, 0].set(1.0)

        def lin(k, out_f, in_f):
            return jax.random.normal(k, (out_f, in_f), dtype=jnp.float32) / np.sqrt(in_f)
        W_src = lin(ks[4], 2 * OUT_SIZE, SRC_SIZE)
        b_src = jnp.zeros((2 * OUT_SIZE,), jnp.float32)
        W_tgt = lin(ks[5], OUT_SIZE, TGT_SIZE)
        b_tgt = jnp.zeros((OUT_SIZE,), jnp.float32)
        W_out = lin(ks[6], OUT_SIZE, OUT_SIZE + TGT_SIZE)
        b_out = jnp.zeros((OUT_SIZE,), jnp.float32)
        return {'src': src, 'tgt': tgt, 'src_mask': src_mask, 'tgt_mask': tgt_mask, 'W_src': W_src, 'b_src': b_src, 'W_tgt': W_tgt, 'b_tgt': b_tgt, 'W_out': W_out, 'b_out': b_out}
    _L0_xattn_all = _L0_xattn_setup()
    _L0_xattn_in = {k: v for k, v in _L0_xattn_all.items() if k in ('W_src', 'b_src', 'W_tgt', 'b_tgt', 'W_out', 'b_out')}
    del _L0_xattn_all

    def _L0_ffn_setup():
        import jax, jax.numpy as jnp
        import numpy as np
        D = 128
        E = 8
        H = 256
        TOP_K = 2
        ALPHA = 0.5
        LN_EPS = 1e-05

        def _experts_all(x, W1, b1, W2, b2):
            h = jax.nn.relu(jnp.einsum('bld,edh->eblh', x, W1) + b1[:, None, None, :])
            return jnp.einsum('eblh,ehd->ebld', h, W2) + b2[:, None, None, :]

        def _selected_expert(x, expert_idx, W1, b1, W2, b2):
            oh = jax.nn.one_hot(expert_idx, E, dtype=x.dtype)
            return jnp.einsum('ebld,ble->bld', _experts_all(x, W1, b1, W2, b2), oh)

        def _layer_norm(x, gamma, beta):
            mu = jnp.mean(x, axis=-1, keepdims=True)
            var = jnp.mean(jnp.square(x - mu), axis=-1, keepdims=True)
            return (x - mu) * jax.lax.rsqrt(var + LN_EPS) * gamma + beta
        key = jax.random.key(seed)
        ks = jax.random.split(key, 8)
        x = jax.random.normal(ks[0], (2, 256, D), dtype=jnp.float32)
        gate_W = jax.random.normal(ks[1], (D, E), dtype=jnp.float32) * 0.02
        gate_b = jnp.zeros((E,), dtype=jnp.float32)
        W1 = jax.random.normal(ks[2], (E, D, H), dtype=jnp.float32) * 0.02
        b1 = jnp.zeros((E, H), dtype=jnp.float32)
        W2 = jax.random.normal(ks[3], (E, H, D), dtype=jnp.float32) * 0.02
        b2 = jnp.zeros((E, D), dtype=jnp.float32)
        ln_gamma = jnp.ones((D,), dtype=jnp.float32)
        ln_beta = jnp.zeros((D,), dtype=jnp.float32)
        return {'x': x, 'gate_W': gate_W, 'gate_b': gate_b, 'W1': W1, 'b1': b1, 'W2': W2, 'b2': b2, 'ln_gamma': ln_gamma, 'ln_beta': ln_beta}
    _L0_ffn_all = _L0_ffn_setup()
    _L0_ffn_in = {k: v for k, v in _L0_ffn_all.items() if k in ('gate_W', 'gate_b', 'W1', 'b1', 'W2', 'b2', 'ln_gamma', 'ln_beta')}
    del _L0_ffn_all

    def _L1_attn_setup():
        import jax, jax.numpy as jnp
        import numpy as np
        from jax import lax
        D_MODEL = 128
        D_STATE = 16
        D_CONV = 4
        EXPAND = 2
        HEADDIM = 64
        CHUNK = 64
        D_INNER = EXPAND * D_MODEL
        NHEADS = D_INNER // HEADDIM
        CONV_DIM = D_INNER + 2 * D_STATE
        D_IN_PROJ = 2 * D_INNER + 2 * D_STATE + NHEADS
        B_SZ = 4
        SEQ = 256

        def _ssd(x, A, B, C):
            b, l, h, p = x.shape
            c = l // CHUNK
            xc = x.reshape(b, c, CHUNK, h, p)
            Ac = A.reshape(b, c, CHUNK, h).transpose(0, 3, 1, 2)
            Bc = B.reshape(b, c, CHUNK, -1)
            Cc = C.reshape(b, c, CHUNK, -1)
            A_cs = jnp.cumsum(Ac, axis=-1)
            idx = jnp.arange(CHUNK)
            mask = idx[:, None] >= idx[None, :]
            seg = jnp.where(mask, A_cs[..., :, None] - A_cs[..., None, :], -jnp.inf)
            L = jnp.exp(seg)
            Y_diag = jnp.einsum('bcln,bcsn,bhcls,bcshp->bclhp', Cc, Bc, L, xc)
            decay_states = jnp.exp(A_cs[..., -1:] - A_cs)
            states = jnp.einsum('bcln,bhcl,bclhp->bchpn', Bc, decay_states, xc)
            states = jnp.concatenate([jnp.zeros_like(states[:, :1]), states], axis=1)
            A_last = jnp.pad(A_cs[..., -1], ((0, 0), (0, 0), (1, 0)))
            cs2 = jnp.cumsum(A_last, axis=-1)
            idx2 = jnp.arange(c + 1)
            m2 = idx2[:, None] >= idx2[None, :]
            decay_chunk = jnp.exp(jnp.where(m2, cs2[..., :, None] - cs2[..., None, :], -jnp.inf))
            new_states = jnp.einsum('bhzc,bchpn->bzhpn', decay_chunk, states)
            st = new_states[:, :-1]
            Y_off = jnp.einsum('bcln,bchpn,bhcl->bclhp', Cc, st, jnp.exp(A_cs))
            return (Y_diag + Y_off).reshape(b, l, h, p)
        key = jax.random.key(seed)
        ks = jax.random.split(key, 8)

        def n(k, shape, s=1.0):
            return jax.random.normal(k, shape, dtype=jnp.float32) * jnp.float32(s)
        return {'x': n(ks[0], (B_SZ, SEQ, D_MODEL)), 'W_in': n(ks[1], (D_IN_PROJ, D_MODEL), D_MODEL ** (-0.5)), 'conv_w': n(ks[2], (CONV_DIM, D_CONV), 0.2), 'conv_b': n(ks[3], (CONV_DIM,), 0.02), 'dt_bias': n(ks[4], (NHEADS,), 0.5), 'A_log': jnp.log(jnp.float32(1.0) + jax.random.uniform(ks[5], (NHEADS,), dtype=jnp.float32) * jnp.float32(15.0)), 'D': n(ks[6], (NHEADS,), 1.0), 'norm_w': jnp.ones((D_INNER,), jnp.float32), 'W_out': n(ks[7], (D_MODEL, D_INNER), D_INNER ** (-0.5))}
    _L1_attn_all = _L1_attn_setup()
    _L1_attn_in = {k: v for k, v in _L1_attn_all.items() if k in ('W_in', 'conv_w', 'conv_b', 'dt_bias', 'A_log', 'D', 'norm_w', 'W_out')}
    del _L1_attn_all

    def _L1_xattn_setup():
        import jax, jax.numpy as jnp
        import numpy as np
        B, L, P = (4, 512, 128)
        D_MODEL = 128
        D_GLOBAL = 256
        HEADDIM = 32
        EPSILON = 0.001
        RMS_EPS = 1e-05

        def rmsnorm(x, g, eps=RMS_EPS):
            var = jnp.mean(jnp.square(x), axis=-1, keepdims=True)
            return x * jax.lax.rsqrt(var + eps) * g

        def _hnet_depool(h, h_patch_full, patch_lens):
            h_patch = h_patch_full[..., :D_MODEL]
            bsz, plen = (h_patch.shape[0], h_patch.shape[1])
            seqlen = h.shape[1]
            logp = jnp.full((bsz, plen), -EPSILON, dtype=jnp.float32)
            bidx = jnp.cumsum(patch_lens, axis=1) - 1
            boundary_mask = jnp.zeros((bsz, seqlen), dtype=jnp.int32)
            boundary_mask = boundary_mask.at[jnp.arange(bsz)[:, None], bidx].set(1)
            dt = (-jnp.log(-jnp.expm1(logp))).astype(h_patch.dtype)
            x = h_patch / dt[..., None]
            n_heads = D_MODEL // HEADDIM
            A = -jnp.ones((n_heads,), dtype=jnp.float32)
            bcoef = jnp.exp(logp).astype(h_patch.dtype)
            x4 = x.reshape(bsz, plen, n_heads, HEADDIM)
            a = jnp.exp(dt[:, :, None] * A[None, None, :])
            u = (dt * bcoef)[:, :, None, None] * x4
            a_b = jnp.broadcast_to(a[..., None], u.shape)

            def comb(lft, rgt):
                aL, uL = lft
                aR, uR = rgt
                return (aL * aR, uL * aR + uR)
            _, s = jax.lax.associative_scan(comb, (a_b, u), axis=1)
            depool = s.reshape(bsz, plen, D_MODEL)
            plug = jnp.clip(jnp.cumsum(boundary_mask, axis=1) - 1, 0, plen - 1)
            depool_out = depool[jnp.arange(bsz)[:, None], plug]
            return depool_out + h
        key = jax.random.key(seed)
        k1, k2, k3, k4 = jax.random.split(key, 4)
        embeds = jax.random.normal(k1, (B, L, D_MODEL), dtype=jnp.float32)
        patch_embeds = jax.random.normal(k2, (B, P, D_GLOBAL), dtype=jnp.float32)
        patch_lens = jnp.full((B, P), L // P, dtype=jnp.int64)
        W_in = jax.random.normal(k3, (D_MODEL, D_MODEL), dtype=jnp.float32) * 0.02
        b_in = jnp.zeros((D_MODEL,), dtype=jnp.float32)
        g_res = jnp.ones((D_MODEL,), dtype=jnp.float32)
        g_init = jnp.ones((D_GLOBAL,), dtype=jnp.float32)
        return {'embeds': embeds, 'patch_embeds': patch_embeds, 'patch_lens': patch_lens, 'W_in': W_in, 'b_in': b_in, 'g_res': g_res, 'g_init': g_init}
    _L1_xattn_all = _L1_xattn_setup()
    _L1_xattn_in = {k: v for k, v in _L1_xattn_all.items() if k in ('W_in', 'b_in', 'g_res', 'g_init')}
    del _L1_xattn_all

    def _L1_ffn_setup():
        import jax, jax.numpy as jnp
        import numpy as np
        D_MODEL, D_FF, RANK = (128, 512, 32)
        B, S = (4, 512)
        key = jax.random.key(seed)
        ks = jax.random.split(key, 7)
        return {'x': jax.random.normal(ks[0], (B, S, D_MODEL), dtype=jnp.float32), 'U1': jax.random.normal(ks[1], (D_MODEL, RANK), dtype=jnp.float32) * 0.02, 'V1': jax.random.normal(ks[2], (RANK, D_FF), dtype=jnp.float32) * 0.02, 'b1': jnp.zeros((D_FF,), dtype=jnp.float32), 'U2': jax.random.normal(ks[3], (D_FF, RANK), dtype=jnp.float32) * 0.02, 'V2': jax.random.normal(ks[4], (RANK, D_MODEL), dtype=jnp.float32) * 0.02, 'b2': jnp.zeros((D_MODEL,), dtype=jnp.float32)}
    _L1_ffn_all = _L1_ffn_setup()
    _L1_ffn_in = {k: v for k, v in _L1_ffn_all.items() if k in ('U1', 'V1', 'b1', 'U2', 'V2', 'b2')}
    del _L1_ffn_all
    return {'x': x, 'ctx_2048': ctx_2048, 'mask_BxS2_fk1': mask_BxS2_fk1, 'mask_BxS2_if0': mask_BxS2_if0, 'L0_attn_w_qkv': _L0_attn_in['w_qkv'], 'L0_attn_w_proj': _L0_attn_in['w_proj'], 'L0_attn_b_proj': _L0_attn_in['b_proj'], 'L0_xattn_W_src': _L0_xattn_in['W_src'], 'L0_xattn_b_src': _L0_xattn_in['b_src'], 'L0_xattn_W_tgt': _L0_xattn_in['W_tgt'], 'L0_xattn_b_tgt': _L0_xattn_in['b_tgt'], 'L0_xattn_W_out': _L0_xattn_in['W_out'], 'L0_xattn_b_out': _L0_xattn_in['b_out'], 'L0_ffn_gate_W': _L0_ffn_in['gate_W'], 'L0_ffn_gate_b': _L0_ffn_in['gate_b'], 'L0_ffn_W1': _L0_ffn_in['W1'], 'L0_ffn_b1': _L0_ffn_in['b1'], 'L0_ffn_W2': _L0_ffn_in['W2'], 'L0_ffn_b2': _L0_ffn_in['b2'], 'L0_ffn_ln_gamma': _L0_ffn_in['ln_gamma'], 'L0_ffn_ln_beta': _L0_ffn_in['ln_beta'], 'L1_attn_W_in': _L1_attn_in['W_in'], 'L1_attn_conv_w': _L1_attn_in['conv_w'], 'L1_attn_conv_b': _L1_attn_in['conv_b'], 'L1_attn_dt_bias': _L1_attn_in['dt_bias'], 'L1_attn_A_log': _L1_attn_in['A_log'], 'L1_attn_D': _L1_attn_in['D'], 'L1_attn_norm_w': _L1_attn_in['norm_w'], 'L1_attn_W_out': _L1_attn_in['W_out'], 'L1_xattn_W_in': _L1_xattn_in['W_in'], 'L1_xattn_b_in': _L1_xattn_in['b_in'], 'L1_xattn_g_res': _L1_xattn_in['g_res'], 'L1_xattn_g_init': _L1_xattn_in['g_init'], 'L1_ffn_U1': _L1_ffn_in['U1'], 'L1_ffn_V1': _L1_ffn_in['V1'], 'L1_ffn_b1': _L1_ffn_in['b1'], 'L1_ffn_U2': _L1_ffn_in['U2'], 'L1_ffn_V2': _L1_ffn_in['V2'], 'L1_ffn_b2': _L1_ffn_in['b2']}

def reference(x, ctx_2048, mask_BxS2_fk1, mask_BxS2_if0, L0_attn_w_qkv, L0_attn_w_proj, L0_attn_b_proj, L0_xattn_W_src, L0_xattn_b_src, L0_xattn_W_tgt, L0_xattn_b_tgt, L0_xattn_W_out, L0_xattn_b_out, L0_ffn_gate_W, L0_ffn_gate_b, L0_ffn_W1, L0_ffn_b1, L0_ffn_W2, L0_ffn_b2, L0_ffn_ln_gamma, L0_ffn_ln_beta, L1_attn_W_in, L1_attn_conv_w, L1_attn_conv_b, L1_attn_dt_bias, L1_attn_A_log, L1_attn_D, L1_attn_norm_w, L1_attn_W_out, L1_xattn_W_in, L1_xattn_b_in, L1_xattn_g_res, L1_xattn_g_init, L1_ffn_U1, L1_ffn_V1, L1_ffn_b1, L1_ffn_U2, L1_ffn_V2, L1_ffn_b2):
    import jax
    import jax.numpy as jnp

    def _L0_attn_ref(x, w_qkv, w_proj, b_proj):
        import jax, jax.numpy as jnp
        import numpy as np
        DIM = 128
        NUM_HEADS = 16
        NUM_GROUPS = 8

        def grouped_linear(x, w, b):
            B, N, Cin = x.shape
            G = w.shape[0]
            xg = x.reshape(B, N, G, Cin // G)
            out = jnp.einsum('bngi,gio->bngo', xg, w)
            out = out.reshape(B, N, -1)
            if b is not None:
                out = out + b
            return out
        B, N, C = x.shape
        H = NUM_HEADS
        D = C // H
        scale = D ** (-0.5)
        qkv = grouped_linear(x, w_qkv, None)
        qkv = qkv.reshape(B, N, 3, H, D)
        qkv = jnp.transpose(qkv, (2, 0, 3, 1, 4))
        q, k, v = (qkv[0] * scale, qkv[1], qkv[2])
        attn = jnp.einsum('bhnd,bhmd->bhnm', q, k)
        attn = jax.nn.softmax(attn, axis=-1)
        out = jnp.einsum('bhnm,bhmd->bhnd', attn, v)
        out = jnp.transpose(out, (0, 2, 1, 3)).reshape(B, N, C)
        out = grouped_linear(out, w_proj, b_proj)
        return out

    def _L0_xattn_ref(src, tgt, src_mask, tgt_mask, W_src, b_src, W_tgt, b_tgt, W_out, b_out):
        import jax, jax.numpy as jnp
        import numpy as np
        B, S, T = (32, 64, 64)
        SRC_SIZE, TGT_SIZE, OUT_SIZE, NUM_HEAD = (256, 128, 128, 8)
        HEAD_DIM = OUT_SIZE // NUM_HEAD
        b, s, _ = src.shape
        t = tgt.shape[1]
        src_trans = jnp.einsum('bsf,of->bso', src, W_src) + b_src
        tgt_trans = jnp.einsum('btf,of->bto', tgt, W_tgt) + b_tgt
        src_trans = src_trans * src_mask[:, :, None]
        tgt_trans = tgt_trans * tgt_mask[:, :, None]
        src_key, src_val = jnp.split(src_trans, 2, axis=2)
        k = src_key.reshape(b, s, NUM_HEAD, HEAD_DIM)
        v = src_val.reshape(b, s, NUM_HEAD, HEAD_DIM)
        q = tgt_trans.reshape(b, t, NUM_HEAD, HEAD_DIM)
        scores = jnp.einsum('bthd,bshd->bhts', q, k) / np.sqrt(HEAD_DIM)
        scores = jnp.where(src_mask[:, None, None, :] == 0, -jnp.inf, scores)
        attn = jax.nn.softmax(scores, axis=-1)
        tgt_update = jnp.einsum('bhts,bshd->bthd', attn, v).reshape(b, t, OUT_SIZE)
        cat_tgt = jnp.concatenate([tgt, tgt_update], axis=2)
        return jnp.einsum('btf,of->bto', cat_tgt, W_out) + b_out

    def _L0_ffn_ref(x, gate_W, gate_b, W1, b1, W2, b2, ln_gamma, ln_beta):
        import jax, jax.numpy as jnp
        import numpy as np
        D = 128
        E = 8
        H = 256
        TOP_K = 2
        ALPHA = 0.5
        LN_EPS = 1e-05

        def _experts_all(x, W1, b1, W2, b2):
            h = jax.nn.relu(jnp.einsum('bld,edh->eblh', x, W1) + b1[:, None, None, :])
            return jnp.einsum('eblh,ehd->ebld', h, W2) + b2[:, None, None, :]

        def _selected_expert(x, expert_idx, W1, b1, W2, b2):
            oh = jax.nn.one_hot(expert_idx, E, dtype=x.dtype)
            return jnp.einsum('ebld,ble->bld', _experts_all(x, W1, b1, W2, b2), oh)

        def _layer_norm(x, gamma, beta):
            mu = jnp.mean(x, axis=-1, keepdims=True)
            var = jnp.mean(jnp.square(x - mu), axis=-1, keepdims=True)
            return (x - mu) * jax.lax.rsqrt(var + LN_EPS) * gamma + beta
        residual = x
        gate_logits = jnp.einsum('bld,de->ble', x, gate_W) + gate_b
        gate_weights = jax.nn.softmax(gate_logits, axis=-1)
        topk_vals, topk_idx = jax.lax.top_k(gate_weights, TOP_K)
        boost = jax.lax.stop_gradient(x)
        outs = []
        for i in range(TOP_K):
            eo = _selected_expert(boost, topk_idx[:, :, i], W1, b1, W2, b2)
            outs.append(eo)
            if i < TOP_K - 1:
                boost = boost + ALPHA * jax.lax.stop_gradient(eo)
        fused = sum((topk_vals[:, :, i:i + 1] * outs[i] for i in range(TOP_K)))
        return _layer_norm(residual + fused, ln_gamma, ln_beta)

    def _L1_attn_ref(x, W_in, conv_w, conv_b, dt_bias, A_log, D, norm_w, W_out):
        import jax, jax.numpy as jnp
        import numpy as np
        from jax import lax
        D_MODEL = 128
        D_STATE = 16
        D_CONV = 4
        EXPAND = 2
        HEADDIM = 64
        CHUNK = 64
        D_INNER = EXPAND * D_MODEL
        NHEADS = D_INNER // HEADDIM
        CONV_DIM = D_INNER + 2 * D_STATE
        D_IN_PROJ = 2 * D_INNER + 2 * D_STATE + NHEADS
        B_SZ = 4
        SEQ = 256

        def _ssd(x, A, B, C):
            b, l, h, p = x.shape
            c = l // CHUNK
            xc = x.reshape(b, c, CHUNK, h, p)
            Ac = A.reshape(b, c, CHUNK, h).transpose(0, 3, 1, 2)
            Bc = B.reshape(b, c, CHUNK, -1)
            Cc = C.reshape(b, c, CHUNK, -1)
            A_cs = jnp.cumsum(Ac, axis=-1)
            idx = jnp.arange(CHUNK)
            mask = idx[:, None] >= idx[None, :]
            seg = jnp.where(mask, A_cs[..., :, None] - A_cs[..., None, :], -jnp.inf)
            L = jnp.exp(seg)
            Y_diag = jnp.einsum('bcln,bcsn,bhcls,bcshp->bclhp', Cc, Bc, L, xc)
            decay_states = jnp.exp(A_cs[..., -1:] - A_cs)
            states = jnp.einsum('bcln,bhcl,bclhp->bchpn', Bc, decay_states, xc)
            states = jnp.concatenate([jnp.zeros_like(states[:, :1]), states], axis=1)
            A_last = jnp.pad(A_cs[..., -1], ((0, 0), (0, 0), (1, 0)))
            cs2 = jnp.cumsum(A_last, axis=-1)
            idx2 = jnp.arange(c + 1)
            m2 = idx2[:, None] >= idx2[None, :]
            decay_chunk = jnp.exp(jnp.where(m2, cs2[..., :, None] - cs2[..., None, :], -jnp.inf))
            new_states = jnp.einsum('bhzc,bchpn->bzhpn', decay_chunk, states)
            st = new_states[:, :-1]
            Y_off = jnp.einsum('bcln,bchpn,bhcl->bclhp', Cc, st, jnp.exp(A_cs))
            return (Y_diag + Y_off).reshape(b, l, h, p)
        b, l, _ = x.shape
        zxbcdt = jnp.einsum('bld,ed->ble', x, W_in)
        z = zxbcdt[..., :D_INNER]
        xBC = zxbcdt[..., D_INNER:D_INNER + CONV_DIM]
        dt = jax.nn.softplus(zxbcdt[..., D_INNER + CONV_DIM:] + dt_bias)
        xp = jnp.pad(xBC, ((0, 0), (D_CONV - 1, 0), (0, 0)))
        kern = conv_w.T[:, None, :]
        xconv = lax.conv_general_dilated(xp, kern, (1,), 'VALID', dimension_numbers=('NWC', 'WIO', 'NWC'), feature_group_count=CONV_DIM)
        xBC = jax.nn.silu(xconv + conv_b)
        xh = xBC[..., :D_INNER].reshape(b, l, NHEADS, HEADDIM)
        Bm = xBC[..., D_INNER:D_INNER + D_STATE]
        Cm = xBC[..., D_INNER + D_STATE:]
        A = -jnp.exp(A_log)
        y = _ssd(xh * dt[..., None], A * dt, Bm, Cm)
        y = y + xh * D[:, None]
        y = y.reshape(b, l, D_INNER)
        y = y * jax.nn.silu(z)
        y = y * lax.rsqrt(jnp.mean(y * y, axis=-1, keepdims=True) + jnp.float32(1e-05)) * norm_w
        return jnp.einsum('ble,de->bld', y, W_out)

    def _L1_xattn_ref(embeds, patch_embeds, patch_lens, W_in, b_in, g_res, g_init):
        import jax, jax.numpy as jnp
        import numpy as np
        B, L, P = (4, 512, 128)
        D_MODEL = 128
        D_GLOBAL = 256
        HEADDIM = 32
        EPSILON = 0.001
        RMS_EPS = 1e-05

        def rmsnorm(x, g, eps=RMS_EPS):
            var = jnp.mean(jnp.square(x), axis=-1, keepdims=True)
            return x * jax.lax.rsqrt(var + eps) * g

        def _hnet_depool(h, h_patch_full, patch_lens):
            h_patch = h_patch_full[..., :D_MODEL]
            bsz, plen = (h_patch.shape[0], h_patch.shape[1])
            seqlen = h.shape[1]
            logp = jnp.full((bsz, plen), -EPSILON, dtype=jnp.float32)
            bidx = jnp.cumsum(patch_lens, axis=1) - 1
            boundary_mask = jnp.zeros((bsz, seqlen), dtype=jnp.int32)
            boundary_mask = boundary_mask.at[jnp.arange(bsz)[:, None], bidx].set(1)
            dt = (-jnp.log(-jnp.expm1(logp))).astype(h_patch.dtype)
            x = h_patch / dt[..., None]
            n_heads = D_MODEL // HEADDIM
            A = -jnp.ones((n_heads,), dtype=jnp.float32)
            bcoef = jnp.exp(logp).astype(h_patch.dtype)
            x4 = x.reshape(bsz, plen, n_heads, HEADDIM)
            a = jnp.exp(dt[:, :, None] * A[None, None, :])
            u = (dt * bcoef)[:, :, None, None] * x4
            a_b = jnp.broadcast_to(a[..., None], u.shape)

            def comb(lft, rgt):
                aL, uL = lft
                aR, uR = rgt
                return (aL * aR, uL * aR + uR)
            _, s = jax.lax.associative_scan(comb, (a_b, u), axis=1)
            depool = s.reshape(bsz, plen, D_MODEL)
            plug = jnp.clip(jnp.cumsum(boundary_mask, axis=1) - 1, 0, plen - 1)
            depool_out = depool[jnp.arange(bsz)[:, None], plug]
            return depool_out + h
        h = rmsnorm(embeds, g_res)
        h = jnp.einsum('bld,ed->ble', h, W_in) + b_in
        h_patch = rmsnorm(patch_embeds, g_init)
        return _hnet_depool(h, h_patch, patch_lens)

    def _L1_ffn_ref(x, U1, V1, b1, U2, V2, b2):
        import jax, jax.numpy as jnp
        import numpy as np
        D_MODEL, D_FF, RANK = (128, 512, 32)
        B, S = (4, 512)
        P = jnp.einsum('bsd,dr->bsr', x, U1)
        H = jax.nn.gelu(jnp.einsum('bsr,rf->bsf', P, V1) + b1)
        Q = jnp.einsum('bsf,fr->bsr', H, U2)
        return jnp.einsum('bsr,rd->bsd', Q, V2) + b2
    x = x + _L0_attn_ref(_layernorm(x, axis=-1), L0_attn_w_qkv, L0_attn_w_proj, L0_attn_b_proj)
    x = x + _L0_xattn_ref(ctx_2048, _layernorm(x, axis=-1), mask_BxS2_fk1, mask_BxS2_fk1, L0_xattn_W_src, L0_xattn_b_src, L0_xattn_W_tgt, L0_xattn_b_tgt, L0_xattn_W_out, L0_xattn_b_out)
    x = x + _L0_ffn_ref(_layernorm(x, axis=-1), L0_ffn_gate_W, L0_ffn_gate_b, L0_ffn_W1, L0_ffn_b1, L0_ffn_W2, L0_ffn_b2, L0_ffn_ln_gamma, L0_ffn_ln_beta)
    x = x + _L1_attn_ref(_layernorm(x, axis=-1), L1_attn_W_in, L1_attn_conv_w, L1_attn_conv_b, L1_attn_dt_bias, L1_attn_A_log, L1_attn_D, L1_attn_norm_w, L1_attn_W_out)
    x = x + _L1_xattn_ref(_layernorm(x, axis=-1), ctx_2048, mask_BxS2_if0, L1_xattn_W_in, L1_xattn_b_in, L1_xattn_g_res, L1_xattn_g_init)
    x = x + _L1_ffn_ref(_layernorm(x, axis=-1), L1_ffn_U1, L1_ffn_V1, L1_ffn_b1, L1_ffn_U2, L1_ffn_V2, L1_ffn_b2)
    return x

_drawn_inputs = setup_inputs


def setup_inputs(seed=0):
    import zlib

    import numpy as np

    out = dict(_drawn_inputs(seed))
    spreads = {'L0_xattn_b_src': (0.0, 0.1),
     'L0_xattn_b_tgt': (0.0, 0.656),
     'L0_xattn_b_out': (0.0, 0.1),
     'L0_ffn_gate_b': (0.0, 0.8),
     'L0_ffn_b1': (0.0, 0.8),
     'L0_ffn_b2': (0.0, 0.8),
     'L0_ffn_ln_gamma': (1.0, 0.2),
     'L0_ffn_ln_beta': (0.0, 0.1),
     'L1_attn_norm_w': (1.0, 0.2),
     'L1_xattn_b_in': (0.0, 0.1),
     'L1_xattn_g_res': (1.0, 0.6),
     'L1_xattn_g_init': (1.0, 0.2),
     'L1_ffn_b1': (0.0, 0.8),
     'L1_ffn_b2': (0.0, 0.363)}
    factors = {'L0_attn_b_proj': 2.967,
     'L0_ffn_gate_W': 5.611,
     'L0_ffn_W1': 8.0,
     'L0_ffn_W2': 8.0,
     'L1_attn_conv_b': 2.711,
     'L1_attn_dt_bias': 8.0,
     'L1_attn_A_log': 8.0,
     'L1_ffn_U1': 8.0,
     'L1_ffn_V1': 8.0,
     'L1_ffn_U2': 8.0,
     'L1_ffn_V2': 8.0}
    for name, (base, spread) in spreads.items():
        noise = np.random.default_rng([zlib.crc32(name.encode()), seed]).standard_normal(out[name].shape)
        drawn = base * np.exp(spread * noise) if base else spread * noise
        out[name] = jnp.asarray(drawn.astype(out[name].dtype))
    for name, factor in factors.items():
        out[name] = (out[name] * factor).astype(out[name].dtype)
    return out
```

```python
from contextlib import ExitStack

import numpy as np

import concourse.bass as bass
from concourse import mybir

F32 = mybir.dt.float32
BF16 = mybir.dt.bfloat16
I32 = mybir.dt.int32
U32 = mybir.dt.uint32
ACT = mybir.ActivationFunctionType
ALU = mybir.AluOpType
AX = mybir.AxisListType

B, S, D, DC = 32, 128, 128, 256
G = 4
NG = B // G
GT = G * S
Q = 32
H0, D0 = 16, 8
H1, D1 = 8, 16
E, HID = 8, 256
EC = HID // 128
DI, NS, HM, HP = 256, 16, 4, 64
TAPS = 4
FF, RANK = 512, 32
LN_EPS = 1e-5
PATCH_EPS = 1e-3
BIG = 1e30

W_COLS = [("q0", 4 * 128), ("k0", 4 * 128), ("v0", 128), ("proj", 128),
          ("k1", 2 * 2 * 128), ("v1", 2 * 128), ("q1", 2 * 128), ("out1", 2 * 128), ("gate", E),
          ("w1", E * HID), ("w2", E * EC * 128), ("z", DI), ("xs", DI), ("bc", 128), ("dt", HM),
          ("mout", 2 * 128), ("win", 128), ("u1", RANK), ("u2", 4 * RANK)]
P_COLS = [("bk1", 2), ("bq1", 2), ("b1", E * EC), ("cw", 3 * TAPS), ("cb", 3), ("bff1", 4),
          ("normw", 2), ("gres", 1)]
R_COLS = [("bproj", 128), ("bv1", 128), ("bout", 128), ("gateb", E), ("gamma", 128), ("beta", 128),
          ("dtb", HM), ("alog", HM), ("dskip", HM), ("bin", 128), ("ginit", 128), ("bff2", 128)]


def places(cols):
    at, out = 0, {}
    for name, n in cols:
        out[name] = (at, at + n)
        at += n
    return out, at


W_AT, W_N = places(W_COLS)
P_AT, P_N = places(P_COLS)
R_AT, R_N = places(R_COLS)


def build(nc, x, ctx_in, mask, m_t, l_t, w_in, w_p, w_r, w_b2, w_v1, w_v2, out):
    x_t = x.rearrange("b t d -> t b d")
    c_t = ctx_in.rearrange("b t d -> t b d")
    o_t = out.rearrange("b t d -> t b d")

    stack = ExitStack()
    with stack:
        def sb(name, shape, dt=F32):
            return stack.enter_context(nc.sbuf_tensor(name, shape, dt))

        per = {}

        def sem(name, n=1):
            s = stack.enter_context(nc.semaphore(name))
            per[name] = n
            by_sem.append((s, n))
            return s

        by_sem = []

        def counter(g):
            def at(s, c):
                n = [k for t, k in by_sem if t is s][0]
                return g * n + c
            return at

        bank = [stack.enter_context(nc.psum_tensor(f"bank{i}", [128, 512], F32)) for i in range(8)]

        W = sb("W", [128, W_N])
        WP = sb("WP", [128, P_N])
        WR = sb("WR", [128, R_N])
        B2 = sb("B2", [E, 128])
        V1w = sb("V1w", [RANK, FF])
        V2w = sb("V2w", [RANK, 128])
        ident = sb("ident", [128, 128])
        tri = sb("tri", [128, 128])
        after = sb("after", [128, 128])
        tri_bf = sb("tri_bf", [128, 128], BF16)
        decay = sb("decay", [128, 128])
        ones = sb("ones", [128, 128])
        ones_bf = sb("ones_bf", [128, 128], BF16)
        iota_row = sb("iota_row", [128, 128])
        iota_part1 = sb("iota_part1", [128, 1])
        big_e = sb("big_e", [E, E, 128], BF16)
        halfneg = sb("halfneg", [128, 16])
        eps = sb("eps", [128, 16])
        mark = sb("mark", [1, 16])
        base = sb("base", [128, 128])
        neg_a = sb("neg_a", [128, HM])
        gb = sb("gb", [128, 128])
        woutn = sb("woutn", [128, 2, 128])
        winn = sb("winn", [128, 128])

        def w(name, k=None, n=128):
            a, b = W_AT[name]
            return W[:, a:b] if k is None else W[:, a + k * n:a + (k + 1) * n]

        def wp(name, k=0):
            return WP[:, P_AT[name][0] + k:P_AT[name][0] + k + 1]

        def wr(name):
            return WR[:, R_AT[name][0]:R_AT[name][1]]

        def over_g(row, n=128):
            return row.unsqueeze(1).broadcast_to([128, G, n])

        X = sb("X", [128, G, D])
        C = sb("C", [128, G, DC])
        MT = sb("MT", [128, G])
        LT = sb("LT", [128, G], I32)
        MB = sb("MB", [128, G, 128])
        negrow = sb("negrow", [128, GT], BF16)
        xb = sb("xb", [128, G, D])
        bst = sb("bst", [128, G, 6])
        mv = sb("mv", [128, G, 2])
        vs = sb("vs", [128, G])
        rstd = sb("rstd", [128, G])
        XN = sb("XN", [128, G, D])
        XT = sb("XT", [128, GT])
        QT = sb("QT", [128, 4, GT])
        KT = sb("KT", [128, 4, GT])
        V0 = sb("V0", [128, G, H0, D0 + 1])
        V1 = sb("V1", [128, G, H1, D1 + 1])
        mx = sb("mx", [128, 16, 4])
        SM = sb("SM", [128, 2, 4, 128])
        PT = sb("PT", [128, 2, 4, 128])
        rs = sb("rs", [128, G, H0])
        AO = sb("AO", [128, G, D])
        AT = sb("AT", [128, GT])
        CT = sb("CT", [128, 2, GT])
        bm = sb("bm", [128, G, 128])
        vtmp = sb("vtmp", [128, G, 128])
        X1 = sb("X1", [128, G, D])
        X1b = sb("X1b", [128, G, D])
        X2 = sb("X2", [128, G, D])
        X2b = sb("X2b", [128, G, D])
        XL = sb("XL", [128, G, D])
        lg = sb("lg", [128, G, E])
        top = sb("top", [128, G, 8])
        topi = sb("topi", [128, G, 8], U32)
        topf = sb("topf", [128, G, 8])
        lsh = sb("lsh", [128, G, E])
        lex = sb("lex", [128, G, E])
        lsum = sb("lsum", [128, G])
        l2 = sb("l2", [128, G])
        gv = sb("gv", [128, 2, G])
        oh = sb("oh", [128, 2, G, E])
        ohT = sb("ohT", [E, 2, GT])
        ohM = sb("ohM", [E, 2, GT], BF16)
        HS = sb("HS", [128, 3, GT])
        boost = sb("boost", [128, G, D])
        boostT = sb("boostT", [128, GT])
        f1 = sb("f1", [128, G, D])
        X3 = sb("X3", [128, G, D])
        xp = sb("xp", [128, 3, G, S + TAPS - 1])
        u = sb("u", [128, 3, G, S])
        th = sb("th", [128, 3, G, S])
        xs = sb("xs", [128, 2, G, S])
        Bm = sb("Bm", [NS, G, S])
        Cm = sb("Cm", [NS, G, S])
        xh = sb("xh", [128, G, 2, 128])
        xd = sb("xd", [128, G, 2, 128])
        tz = sb("tz", [128, G, DI])
        sz = sb("sz", [128, G, DI])
        dtr = sb("dtr", [128, G, HM])
        dta = sb("dta", [128, G, HM])
        dte = sb("dte", [128, G, HM])
        dtw = sb("dtw", [128, G, HM])
        dtl = sb("dtl", [128, G, HM])
        dtd = sb("dtd", [128, G, HM])
        dtz = sb("dtz", [128, G, HM])
        dtm = sb("dtm", [128, G, HM])
        dt = sb("dt", [128, G, HM])
        dA = sb("dA", [128, G, HM])
        R = QT[:].rearrange("p b (h t) -> p b h t", h=HM)
        EX = KT[:].rearrange("p b (h t) -> p b h t", h=HM)
        Gm = sb("Gm", [128, G, 128])
        M = sb("M", [128, G, HM, 128])
        Y = CT[:].rearrange("p k (b c) -> p (k b) c", c=DI)
        Yz = tz
        ysq = Y
        yss = sb("yss", [128, G])
        yr = sb("yr", [128, G])
        YT = th[:, 0:2, :, :].rearrange("p k b t -> p k (b t)")
        X4 = sb("X4", [128, G, D])
        X4b = sb("X4b", [128, G, D])
        q6 = sb("q6", [128, G])
        lf = sb("lf", [128, G])
        bi = sb("bi", [128, G])
        bw = sb("bw", [128, G])
        OH = sb("OH", [128, G, 128], BF16)
        bnd = sb("bnd", [128, G, 128], BF16)
        sel = sb("sel", [128, G, 128])
        csq = tz
        css = sb("css", [128, G])
        cr = sb("cr", [128, G])
        cu = vtmp
        dp = sb("dp", [128, G, 128])
        X5 = X1
        X5b = X1b
        Pt = QT[0:RANK, 0, :]
        HF = M[:].rearrange("p b h t -> p b (h t)")
        Qt = QT[0:RANK, 1, :]
        X6 = sb("X6", [128, G, D])

        once = stack.enter_context(nc.semaphore("weights_loaded"))
        const_pool = stack.enter_context(nc.semaphore("pool_constants"))
        const_vec = stack.enter_context(nc.semaphore("vector_constants"))
        const_act = stack.enter_context(nc.semaphore("scalar_constants"))
        x_loaded, c_loaded, m_loaded, l_loaded = (sem(n, 16) for n in ("x_loaded", "c_loaded", "m_loaded", "l_loaded"))
        mt_loaded = sem("mt_loaded", 16)
        stored = sem("stored", 16)
        NLN = 7
        bn_done, mv_ready, ve_ready, rstd_ready = (sem(n, NLN * k) for n, k in
                                                   (("bn_done", G), ("mv_ready", G), ("ve_ready", 1), ("rstd_ready", 1)))
        xn_ready = sem("xn_ready", NLN)
        xt_psum, xt_ready = sem("xt_psum", 6), sem("xt_ready", 6)
        xb_ready = sem("xb_ready", 6)
        q_psum, k_psum, q_ready, k_ready = (sem(n, 4) for n in ("q_psum", "k_psum", "q_ready", "k_ready"))
        v_psum, v_ready = sem("v_psum"), sem("v_ready")
        NJ = H0 + H1
        s_psum, max_ready, sm_ready, pt_psum, pt_ready, pv_done = (
            sem(n, NJ) for n in ("s_psum", "max_ready", "sm_ready", "pt_psum", "pt_ready", "pv_done"))
        rs_ready, ao_ready = sem("rs_ready", 4), sem("ao_ready", 4)
        at_psum, at_ready, att_psum = sem("at_psum", 2), sem("at_ready", 2), sem("att_psum", 2)
        x1_ready, x2_ready = sem("x1_ready"), sem("x2_ready")
        ct_psum, ct_ready = sem("ct_psum", 2), sem("ct_ready", 2)
        neg_ready, bm_ready = sem("neg_ready"), sem("bm_ready")
        k1_psum, k1_ready, q1_psum, q1_ready = (sem(n, 2) for n in ("k1_psum", "k1_ready", "q1_psum", "q1_ready"))
        v1_psum, v1_part, v1_ready = sem("v1_psum"), sem("v1_part"), sem("v1_ready")
        gate_psum, gate_step = sem("gate_psum"), sem("gate_step", 0)
        lsh_ready, lex_ready, oh_ready = sem("lsh_ready"), sem("lex_ready"), sem("oh_ready")
        oh_psum, ohm_ready = sem("oh_psum", 2), sem("ohm_ready", 2)
        h_psum, h_act, h_vec = sem("h_psum", 32), sem("h_act", 16), sem("h_vec", 16)
        hs_used = sem("hs_used", 32)
        eo_psum = sem("eo_psum", 2)
        boost_ready, f_ready = sem("boost_ready", 2), sem("f_ready", 2)
        bt_psum, bt_ready = sem("bt_psum"), sem("bt_ready")
        y_norm, x3_ready = sem("y_norm", 2), sem("x3_ready")
        z_psum, xp_psum, xp_ready, dt_psum = sem("z_psum", 2), sem("xp_psum", 3), sem("xp_ready", 3), sem("dt_psum")
        tz_ready, sz_ready = sem("tz_ready", 2), sem("sz_ready", 2)
        conv_step, th_ready, xs_ready = sem("conv_step", 12), sem("th_ready", 3), sem("xs_ready", 4)
        xh_psum, xh_ready, xd_ready = sem("xh_psum", 2), sem("xh_ready", 2), sem("xd_ready")
        dt_step, dte_ready, dtw_ready, dtl_ready, dt_ready = (
            sem("dt_step", 7), sem("dte_ready"), sem("dtw_ready"), sem("dtl_ready"), sem("dt_ready"))
        dA_ready, r_ready, seg_psum, ex_ready = sem("dA_ready"), sem("r_ready", G), sem("seg_psum", G), sem("ex_ready", G)
        g_psum, gm_ready, m_ready, y_psum = sem("g_psum"), sem("gm_ready"), sem("m_ready", G), sem("y_psum", 2)
        y_step, yss_ready, yr_ready, yt_psum, yt_ready = (
            sem("y_step", 4), sem("yss_ready", G), sem("yr_ready", 2), sem("yt_psum", 2), sem("yt_ready", 2))
        mo_psum, x4_ready = sem("mo_psum"), sem("x4_ready")
        lf_ready, lf_copied, bi_step, ohj_ready, cs_psum, nb_psum, bnd_ready, plug_psum = (
            sem(n, k) for n, k in (("lf_ready", 1), ("lf_copied", 1), ("bi_step", 3), ("ohj_ready", 1), ("cs_psum", 1),
                                   ("nb_psum", 1), ("bnd_ready", 1), ("plug_psum", 1)))
        css_ready, cr_ready, cu_ready, dp_psum, dp_ready = (
            sem(n, k) for n, k in (("css_ready", G), ("cr_ready", 2), ("cu_ready", 1), ("dp_psum", 1), ("dp_ready", 1)))
        r6_step = sem("r6_step", 4)
        x5_psum, x5_ready = sem("x5_psum"), sem("x5_ready")
        p_psum, p_ready, hf_psum, hf_ready = sem("p_psum"), sem("p_ready"), sem("hf_psum", 4), sem("hf_ready", 4)
        qf_psum, qf_ready, x6_psum, x6_ready = sem("qf_psum"), sem("qf_ready"), sem("x6_psum"), sem("x6_ready")
        sel_ready = sem("sel_ready")
        LINKS = 7
        link_sem = sem("gate_link", LINKS)

        block = stack.enter_context(nc.Block())

        @block.sync
        def _(sp):
            for dst, src in ((W, w_in), (WP, w_p), (WR, w_r), (B2, w_b2), (V1w, w_v1), (V2w, w_v2)):
                sp.dma_start(dst[:], src).then_inc(once, 16)
            sp.sem_inc(stored, 1)

            def load_x(g):
                sp.dma_start(X[:], x_t[:, bass.ds(g * G, G), :]).then_inc(x_loaded, 16)

            def load_rest(g):
                sp.dma_start(C[:], c_t[:, bass.ds(g * G, G), :]).then_inc(c_loaded, 16)
                sp.dma_start(MT[:], m_t[:, bass.ds(g * G, G)]).then_inc(mt_loaded, 16)
                sp.dma_start(MB[:], mask[bass.ds(g * G, G), :].unsqueeze(0).broadcast_to([128, G, S])
                             ).then_inc(m_loaded, 16)
                sp.dma_start(LT[:], l_t[:, bass.ds(g * G, G)]).then_inc(l_loaded, 16)

            def store(g, at):
                sp.wait_ge(x6_ready, at(x6_ready, 1))
                sp.dma_start(o_t[:, bass.ds(g * G, G), :], X6[:]).then_inc(stored, 16)

            load_x(0)
            load_rest(0)
            with sp.Fori(0, NG - 1) as g:
                at = counter(g)
                sp.wait_ge(xn_ready, at(xn_ready, 1))
                sp.wait_ge(xb_ready, at(xb_ready, 1))
                load_x(g + 1)
                sp.wait_ge(cu_ready, at(cu_ready, 1))
                load_rest(g + 1)
                store(g, at)
            store(NG - 1, counter(NG - 1))
            sp.wait_ge(stored, 16 * NG + 1)

        @block.gpsimd
        def _(pool):
            pg = nc.gpsimd
            nconst = [0]

            def const(ins):
                nconst[0] += 1
                ins.then_inc(const_pool, 1)
                pool.wait_ge(const_pool, nconst[0])

            const(pg.memset(ones[:], 1.0))
            const(pg.memset(ones_bf[:], 1.0))
            const(pg.memset(halfneg[:], -0.5))
            const(pg.memset(eps[:], LN_EPS))
            const(pg.affine_select(out=ident[:], in_=ones[:], pattern=[[1, 128]], compare_op=ALU.is_equal,
                                   fill=0.0, base=0, channel_multiplier=-1))
            const(pg.affine_select(out=tri[:], in_=ones[:], pattern=[[1, 128]], compare_op=ALU.is_ge,
                                   fill=0.0, base=0, channel_multiplier=-1))
            const(pg.affine_select(out=tri_bf[:], in_=ones[:], pattern=[[1, 128]], compare_op=ALU.is_ge,
                                   fill=0.0, base=0, channel_multiplier=-1))
            const(pg.affine_select(out=after[:], in_=ones[:], pattern=[[-1, 128]], compare_op=ALU.is_gt,
                                   fill=0.0, base=0, channel_multiplier=1))
            const(pg.iota(iota_row[:], pattern=[[1, 128]], base=0, channel_multiplier=0,
                          allow_small_or_imprecise_dtypes=True))
            const(pg.iota(iota_part1[:], pattern=[[0, 1]], base=1, channel_multiplier=1,
                          allow_small_or_imprecise_dtypes=True))
            const(pg.iota(base[:], pattern=[[1, 128]], base=0, channel_multiplier=-1,
                          allow_small_or_imprecise_dtypes=True))
            const(pg.tensor_scalar(base[:], base[:], 0.0, None, ALU.max))
            const(pg.memset(decay[:], float(-np.expm1(-PATCH_EPS))))
            const(pg.tensor_tensor(base[:], decay[:], base[:], ALU.pow))
            const(pg.affine_select(out=decay[:], in_=base[:], pattern=[[1, 128]], compare_op=ALU.is_ge,
                                   fill=0.0, base=0, channel_multiplier=-1))
            const(pg.memset(big_e[:], BIG))
            const(pg.affine_select(out=big_e[:], in_=big_e[:], pattern=[[1, E], [0, 128]], compare_op=ALU.is_equal,
                                   fill=0.0, base=0, channel_multiplier=-1))
            pg.memset(V0[:], 1.0)
            pg.memset(V1[:], 1.0)
            const(pg.memset(xp[:], 0.0))
            with pool.Fori(0, NG) as g:
                at = counter(g)

                def plus_eps(k):
                    pool.wait_ge(mv_ready, at(mv_ready, G * (k + 1)))
                    pg.tensor_tensor(vs[:], mv[:, :, 1], eps[:, 0:G], ALU.add).then_inc(ve_ready, 1)
                    pool.wait_ge(ve_ready, at(ve_ready, k + 1))
                    ins = pg.tensor_tensor(rstd[:], vs[:], halfneg[:, 0:G], ALU.pow)
                    return ins

                pool.wait_ge(x_loaded, at(x_loaded, 16))
                pg.tensor_tensor(xb[:], X[:], over_g(wr("bproj")), ALU.add).then_inc(xb_ready, 1)
                plus_eps(0).then_inc(rstd_ready, 1)
                pool.wait_ge(mt_loaded, at(mt_loaded, 16))
                pg.tensor_tensor(bm[:], over_g(wr("bv1")), MT[:].unsqueeze(2).broadcast_to([128, G, 128]), ALU.mult
                                 ).then_inc(bm_ready, 1)
                pool.wait_ge(x1_ready, at(x1_ready, 1))
                pg.tensor_tensor(X1b[:], X1[:], over_g(wr("bout")), ALU.add).then_inc(xb_ready, 1)
                plus_eps(1).then_inc(rstd_ready, 1)
                pool.wait_ge(css_ready, at(css_ready, G))
                pg.tensor_tensor(cr[:], css[:], eps[:, 0:G], ALU.add).then_inc(cr_ready, 1)
                pool.wait_ge(cr_ready, at(cr_ready, 1))
                pg.tensor_tensor(cr[:], cr[:], halfneg[:, 0:G], ALU.pow).then_inc(cr_ready, 1)
                pool.wait_ge(x2_ready, at(x2_ready, 1))
                pg.tensor_tensor(X2b[:], X2[:], over_g(wr("beta")), ALU.add).then_inc(xb_ready, 1)
                plus_eps(2).then_inc(rstd_ready, 1)
                plus_eps(3).then_inc(rstd_ready, 1)
                plus_eps(4).then_inc(rstd_ready, 1)
                pool.wait_ge(dA_ready, at(dA_ready, 1))
                for b in range(G):
                    pg.tensor_tensor(R[:, b, :, :], tri[:, :].unsqueeze(1).broadcast_to([128, HM, 128]),
                                     dA[:, b, :].unsqueeze(2).broadcast_to([128, HM, 128]),
                                     ALU.mult).then_inc(r_ready, 1)
                pool.wait_ge(xh_ready, at(xh_ready, 2))
                for b in range(G):
                    ins = pg.tensor_tensor(xd[:, b, :, :].rearrange("t k (h p) -> t (k h) p", p=HP),
                                           xh[:, b, :, :].rearrange("t k (h p) -> t (k h) p", p=HP),
                                           wr("dskip").unsqueeze(2).broadcast_to([128, HM, HP]), ALU.mult)
                ins.then_inc(xd_ready, 1)
                pool.wait_ge(yss_ready, at(yss_ready, G))
                pg.tensor_tensor(yr[:], yss[:], eps[:, 0:G], ALU.add).then_inc(yr_ready, 1)
                pool.wait_ge(yr_ready, at(yr_ready, 1))
                pg.tensor_tensor(yr[:], yr[:], halfneg[:, 0:G], ALU.pow).then_inc(yr_ready, 1)
                pool.wait_ge(x4_ready, at(x4_ready, 1))
                pg.tensor_tensor(X4b[:], X4[:], over_g(wr("bin")), ALU.add).then_inc(xb_ready, 1)
                plus_eps(5).then_inc(r6_step, 1)
                pool.wait_ge(r6_step, at(r6_step, 1))
                pg.tensor_tensor(q6[:], rstd[:], rstd[:], ALU.mult).then_inc(r6_step, 1)
                pool.wait_ge(r6_step, at(r6_step, 2))
                pg.tensor_tensor(vs[:], q6[:], mv[:, :, 1], ALU.mult).then_inc(r6_step, 1)
                pool.wait_ge(r6_step, at(r6_step, 3))
                pg.tensor_tensor(q6[:], vs[:], eps[:, 0:G], ALU.add).then_inc(r6_step, 1)
                pool.wait_ge(r6_step, at(r6_step, 4))
                pg.tensor_tensor(q6[:], q6[:], halfneg[:, 0:G], ALU.pow).then_inc(xb_ready, 1)
                pool.wait_ge(xb_ready, at(xb_ready, 5))
                pg.tensor_tensor(rstd[:], rstd[:], q6[:], ALU.mult).then_inc(rstd_ready, 1)
                pool.wait_ge(x5_ready, at(x5_ready, 1))
                pg.tensor_tensor(X5b[:], X5[:], over_g(wr("bff2")), ALU.add).then_inc(xb_ready, 1)
                plus_eps(6).then_inc(rstd_ready, 1)

        @block.scalar
        def _(act):
            ac = nc.scalar
            act.wait_ge(once, 96)
            ac.activation(neg_a[:], wr("alog"), ACT.Exp).then_inc(const_act, 1)
            with act.Fori(0, NG) as g:
                at = counter(g)

                def copy_xt(k, src):
                    act.wait_ge(xt_psum, at(xt_psum, k + 1))
                    ac.copy(XT[:], src[:, :]).then_inc(xt_ready, 1)

                def exps(j0, n, scale):
                    for j in range(j0, j0 + n):
                        act.wait_ge(pt_psum, at(pt_psum, j + 1))
                        if j - j0 >= 2:
                            act.wait_ge(pv_done, at(pv_done, j - 1))
                        ac.activation(PT[:, j % 2, :, :], bank[5 + j % 2][:, :], ACT.Exp,
                                      scale=scale).then_inc(pt_ready, 1)

                act.wait_ge(c_loaded, at(c_loaded, 16))
                for b in range(G):
                    ac.activation(csq[:, b, :], C[:, b, :], ACT.Square, scale=DC ** -0.5, accum_out=css[:, b:b + 1]).then_inc(css_ready, 1)
                for k in range(2):
                    act.wait_ge(ct_psum, at(ct_psum, k + 1))
                    ac.copy(CT[:, k, :], bank[4 + k][:, :]).then_inc(ct_ready, 1)
                copy_xt(0, bank[0])
                for i in range(4):
                    act.wait_ge(q_psum, at(q_psum, i + 1))
                    ac.copy(QT[:, i, :], bank[1 + i][:, :]).then_inc(q_ready, 1)
                exps(0, H0, D0 ** -0.5)
                act.wait_ge(at_psum, at(at_psum, 1))
                ac.copy(AT[:], bank[1][:, :]).then_inc(at_ready, 1)
                copy_xt(1, bank[3])
                exps(H0, H1, D1 ** -0.5)
                act.wait_ge(at_psum, at(at_psum, 2))
                ac.copy(AT[:], bank[1][:, :]).then_inc(at_ready, 1)
                copy_xt(2, bank[3])
                act.wait_ge(lsh_ready, at(lsh_ready, 1))
                ac.activation(lex[:], lsh[:], ACT.Exp).then_inc(lex_ready, 1)
                for r in range(2):
                    for n in range(0, E * EC, 2):
                        m = r * E * EC + n
                        act.wait_ge(h_psum, at(h_psum, m + 1))
                        if m >= 3:
                            act.wait_ge(hs_used, at(hs_used, m - 2))
                        ac.activation(HS[:, m % 3, :], bank[m % 3][:, :], ACT.Relu,
                                      bias=wp("b1", n)).then_inc(h_act, 1)
                    if r == 0:
                        act.wait_ge(bt_psum, at(bt_psum, 1))
                        ac.copy(boostT[:], bank[3][:, :]).then_inc(bt_ready, 1)
                copy_xt(3, bank[3])
                for k in range(3):
                    n = 128 if k < 2 else 64
                    act.wait_ge(xp_psum, at(xp_psum, k + 1))
                    ac.copy(xp[0:n, k, :, TAPS - 1:], bank[k][0:n, :].rearrange("c (b t) -> c b t", b=G)
                            ).then_inc(xp_ready, 1)
                for k in range(2):
                    act.wait_ge(z_psum, at(z_psum, k + 1))
                    ac.activation(tz[:, 2 * k:2 * k + 2, :], bank[4 + k][:, :], ACT.Tanh,
                                  scale=0.5).then_inc(tz_ready, 1)
                act.wait_ge(dt_step, at(dt_step, 2))
                ac.activation(dte[:], dta[:], ACT.Exp).then_inc(dte_ready, 1)
                act.wait_ge(dtw_ready, at(dtw_ready, 1))
                ac.activation(dtl[:], dtw[:], ACT.Ln).then_inc(dtl_ready, 1)
                for k in (2, 0, 1):
                    n = 128 if k < 2 else 64
                    act.wait_ge(conv_step, at(conv_step, 4 * [1, 2, 0][k] + 4))
                    ac.activation(th[0:n, k, :, :], u[0:n, k, :, :], ACT.Tanh, scale=0.5).then_inc(th_ready, 1)
                for b in range(G):
                    act.wait_ge(seg_psum, at(seg_psum, b + 1))
                    ac.activation(EX[:, b, :, :], bank[4 + b % 2][:, :], ACT.Exp).then_inc(ex_ready, 1)
                for k in range(2):
                    act.wait_ge(xh_psum, at(xh_psum, k + 1))
                    ac.mul(xh[:, :, k, :], bank[k][:, :].rearrange("t (b c) -> t b c", b=G), 0.5
                           ).then_inc(xh_ready, 1)
                act.wait_ge(y_step, at(y_step, 4))
                for b in range(G):
                    ac.activation(ysq[:, b, :], Yz[:, b, :], ACT.Square, scale=DI ** -0.5, accum_out=yss[:, b:b + 1]).then_inc(yss_ready, 1)
                for k in range(2):
                    act.wait_ge(yt_psum, at(yt_psum, k + 1))
                    ac.copy(YT[:, k, :], bank[2 + k][:, :]).then_inc(yt_ready, 1)
                act.wait_ge(dp_psum, at(dp_psum, 1))
                ac.copy(dp[:], bank[7][:, :].rearrange("t (b c) -> t b c", b=G)).then_inc(dp_ready, 1)
                copy_xt(4, bank[5])
                copy_xt(5, bank[1])
                for k in range(4):
                    act.wait_ge(hf_psum, at(hf_psum, k + 1))
                    ac.activation(HF[:, k, :], bank[3 + k][:, :], ACT.Gelu_apprx_tanh,
                                  bias=wp("bff1", k)).then_inc(hf_ready, 1)

        @block.vector
        def _(dve):
            v = nc.vector
            dve.wait_ge(once, 96)
            for k in range(2):
                v.tensor_scalar(woutn[:, k, :], w("mout", k), wp("normw", k), None, ALU.mult).then_inc(const_vec, 1)
            v.tensor_scalar(winn[:], w("win"), wp("gres"), None, ALU.mult).then_inc(const_vec, 1)
            v.tensor_scalar(gb[:], wr("ginit"), float(np.exp(-PATCH_EPS)), None, ALU.mult).then_inc(const_vec, 1)
            dve.wait_ge(const_act, 1)
            v.tensor_scalar(neg_a[:], neg_a[:], -1.0, None, ALU.mult).then_inc(const_vec, 1)
            dve.wait_ge(const_vec, 5)
            dve.wait_ge(const_pool, 18)
            with dve.Fori(0, NG) as g:
                at = counter(g)
                links, carried = [0], [0]

                def link(ins):
                    links[0] += 1
                    ins.then_inc(link_sem, 1)
                    dve.wait_ge(link_sem, at(link_sem, links[0]))

                def carry():
                    carried[0] += 1
                    v.memset(mark[:, carried[0]:carried[0] + 1], 0.0)

                def norm(k, src, dst):
                    for b in range(G):
                        v.bn_stats(bst[:, b, :], src[:, b, :]).then_inc(bn_done, 1)
                    dve.wait_ge(bn_done, at(bn_done, G * (k + 1)))
                    carry()
                    for b in range(G):
                        v.bn_aggr(mv[:, b, :], bst[:, b, :]).then_inc(mv_ready, 1)
                    dve.wait_ge(mv_ready, at(mv_ready, G * (k + 1)))
                    dve.wait_ge(rstd_ready, at(rstd_ready, k + 1))
                    for b in range(G):
                        ins = v.tensor_scalar(dst[:, b, :], src[:, b, :], mv[:, b, 0:1], rstd[:, b:b + 1],
                                              ALU.subtract, ALU.mult)
                    ins.then_inc(xn_ready, 1)

                def maxima(j0, n):
                    for j in range(j0, j0 + n):
                        sc = bank[2 + (j - j0) % 3][:, :].rearrange("t (h s) -> t h s", h=4)
                        m = mx[:, (j - j0) % 16, :]
                        dve.wait_ge(s_psum, at(s_psum, j + 1))
                        v.tensor_reduce(m, sc, AX.X, ALU.max).then_inc(max_ready, 1)
                        dve.wait_ge(max_ready, at(max_ready, j + 1))
                        if j - j0 >= 2:
                            dve.wait_ge(pt_psum, at(pt_psum, j - 1))
                        v.tensor_tensor(SM[:, j % 2, :, :], sc, m.unsqueeze(2).broadcast_to([128, 4, 128]),
                                        ALU.subtract).then_inc(sm_ready, 1)

                def attended(a, heads, width, jobs):
                    for k in range(2):
                        o = bank[[7, 0][k]][:, 0:2 * heads * (width + 1)].rearrange(
                            "t (b h e) -> t b h e", b=2, h=heads)
                        dve.wait_ge(pv_done, at(pv_done, jobs))
                        v.reciprocal(rs[:, 2 * k:2 * k + 2, 0:heads], o[:, :, :, width]).then_inc(rs_ready, 1)
                        dve.wait_ge(rs_ready, at(rs_ready, 2 * a + k + 1))
                        for b in range(2):
                            ins = v.tensor_tensor(
                                AO[:, 2 * k + b, :].rearrange("t (h e) -> t h e", h=heads), o[:, b, :, 0:width],
                                rs[:, 2 * k + b, 0:heads].unsqueeze(2).broadcast_to([128, heads, width]), ALU.mult)
                        ins.then_inc(ao_ready, 1)

                dve.wait_ge(x_loaded, at(x_loaded, 16))
                norm(0, X, XN)
                dve.wait_ge(m_loaded, at(m_loaded, 16))
                v.tensor_scalar(negrow[:], MB[:].rearrange("p b t -> p (b t)"), 0.0, -BIG, ALU.is_equal, ALU.mult
                                ).then_inc(neg_ready, 1)
                for i in range(4):
                    dve.wait_ge(k_psum, at(k_psum, i + 1))
                    v.tensor_copy(KT[:, i, :], bank[[5, 6, 7, 0][i]][:, :]).then_inc(k_ready, 1)
                dve.wait_ge(v_psum, at(v_psum, 1))
                v.tensor_copy(V0[:, :, :, 0:D0].rearrange("t b h e -> t (b h) e"),
                              bank[1][:, :].rearrange("t (n e) -> t n e", e=D0)).then_inc(v_ready, 1)
                maxima(0, H0)
                attended(0, H0, D0, H0)
                dve.wait_ge(att_psum, at(att_psum, 1))
                dve.wait_ge(xb_ready, at(xb_ready, 1))
                v.tensor_tensor(X1[:], bank[2][:, :].rearrange("t (b c) -> t b c", b=G), xb[:], ALU.add
                                ).then_inc(x1_ready, 1)
                dve.wait_ge(x1_ready, at(x1_ready, 1))
                norm(1, X1, XN)
                for i in range(2):
                    dve.wait_ge(k1_psum, at(k1_psum, i + 1))
                    v.scalar_tensor_tensor(KT[:, i, :], bank[6 + i][:, :], wp("bk1", i),
                                           MB[:].rearrange("p b t -> p (b t)"), ALU.add, ALU.mult).then_inc(k1_ready, 1)
                dve.wait_ge(v1_psum, at(v1_psum, 1))
                for b in range(G):
                    ins = v.tensor_scalar(vtmp[:, b, :], bank[0][:, 128 * b:128 * b + 128], MT[:, b:b + 1], None,
                                          ALU.mult)
                ins.then_inc(v1_part, 1)
                dve.wait_ge(v1_part, at(v1_part, 1))
                dve.wait_ge(bm_ready, at(bm_ready, 1))
                v.tensor_tensor(V1[:, :, :, 0:D1].rearrange("t b h e -> t (b h) e"),
                                vtmp[:].rearrange("t b (h e) -> t (b h) e", e=D1),
                                bm[:].rearrange("t b (h e) -> t (b h) e", e=D1), ALU.add).then_inc(v1_ready, 1)
                for i in range(2):
                    dve.wait_ge(q1_psum, at(q1_psum, i + 1))
                    v.scalar_tensor_tensor(QT[:, i, :], bank[1 + i][:, :], wp("bq1", i),
                                           MB[:].rearrange("p b t -> p (b t)"), ALU.add, ALU.mult).then_inc(q1_ready, 1)
                maxima(H0, H1)
                attended(1, H1, D1, NJ)
                dve.wait_ge(att_psum, at(att_psum, 2))
                dve.wait_ge(xb_ready, at(xb_ready, 2))
                v.tensor_tensor(X2[:], bank[2][:, :].rearrange("t (b c) -> t b c", b=G), X1b[:], ALU.add
                                ).then_inc(x2_ready, 1)
                dve.wait_ge(x2_ready, at(x2_ready, 1))
                norm(2, X2, XL)
                dve.wait_ge(gate_psum, at(gate_psum, 1))
                link(v.tensor_tensor(lg[:], bank[4][:, 0:G * E].rearrange("t (b e) -> t b e", b=G),
                                     over_g(wr("gateb"), E), ALU.add))
                carry()
                for b in range(G):
                    ins = v.max(top[:, b, :], lg[:, b, :])
                link(ins)
                carry()
                for b in range(G):
                    ins = v.max_index(topi[:, b, :], top[:, b, :], lg[:, b, :])
                v.tensor_tensor(lsh[:], lg[:], top[:, :, 0:1].broadcast_to([128, G, E]), ALU.subtract
                                ).then_inc(lsh_ready, 1)
                link(v.tensor_tensor(l2[:], top[:, :, 1], top[:, :, 0], ALU.subtract))
                link(v.tensor_copy(topf[:], topi[:]))
                for r in range(2):
                    for b in range(G):
                        ins = v.tensor_scalar(oh[:, r, b, :], iota_row[:, 0:E], topf[:, b, r:r + 1], None, ALU.is_equal)
                ins.then_inc(oh_ready, 1)
                for r in range(2):
                    dve.wait_ge(oh_psum, at(oh_psum, r + 1))
                    v.tensor_copy(ohT[:, r, :], bank[5 + r][0:E, :])
                    v.tensor_scalar(ohM[:, r, :], bank[5 + r][0:E, :], 1.0, None, ALU.subtract).then_inc(ohm_ready, 1)
                dve.wait_ge(lex_ready, at(lex_ready, 1))
                link(v.tensor_reduce(lsum[:], lex[:], AX.X, ALU.add))
                link(v.reciprocal(gv[:, 0, :], lsum[:]))
                link(v.tensor_tensor(lsh[:], lex[:], oh[:, 1, :, :], ALU.mult))
                v.tensor_reduce(l2[:], lsh[:], AX.X, ALU.add).then_inc(f_ready, 1)
                dve.wait_ge(f_ready, at(f_ready, 1))
                v.tensor_tensor(gv[:, 1, :], l2[:], gv[:, 0, :], ALU.mult).then_inc(f_ready, 1)
                for r in range(2):
                    for n in range(1, E * EC, 2):
                        m = r * E * EC + n
                        dve.wait_ge(h_psum, at(h_psum, m + 1))
                        if m >= 3:
                            dve.wait_ge(hs_used, at(hs_used, m - 2))
                        v.tensor_scalar(HS[:, m % 3, :], bank[m % 3][:, :], wp("b1", n), 0.0, ALU.add, ALU.max
                                        ).then_inc(h_vec, 1)
                    eo = bank[7 - r][:, :].rearrange("t (b c) -> t b c", b=G)
                    dve.wait_ge(eo_psum, at(eo_psum, r + 1))
                    if r == 0:
                        v.scalar_tensor_tensor(boost[:], eo, 0.5, XL[:], ALU.mult, ALU.add).then_inc(boost_ready, 1)
                        dve.wait_ge(f_ready, at(f_ready, 2))
                    for b in range(G):
                        ins = v.scalar_tensor_tensor(f1[:, b, :], eo[:, b, :], gv[:, r, b:b + 1],
                                                     (XL if r == 0 else f1)[:, b, :], ALU.mult, ALU.add)
                    ins.then_inc(y_norm, 1)
                    dve.wait_ge(y_norm, at(y_norm, r + 1))
                norm(3, f1, boost)
                dve.wait_ge(xn_ready, at(xn_ready, 4))
                v.tensor_tensor(f1[:], boost[:], over_g(wr("gamma")), ALU.mult).then_inc(x3_ready, 1)
                dve.wait_ge(x3_ready, at(x3_ready, 1))
                dve.wait_ge(xb_ready, at(xb_ready, 3))
                v.tensor_tensor(X3[:], f1[:], X2b[:], ALU.add).then_inc(boost_ready, 1)
                dve.wait_ge(boost_ready, at(boost_ready, 2))
                norm(4, X3, XN)
                dve.wait_ge(dt_psum, at(dt_psum, 1))
                v.tensor_tensor(dtr[:], bank[7][:, 0:G * HM].rearrange("t (b h) -> t b h", b=G),
                                over_g(wr("dtb"), HM), ALU.add).then_inc(dt_step, 1)
                dve.wait_ge(dt_step, at(dt_step, 1))
                v.scalar_tensor_tensor(dta[:], dtr[:], -1.0, dtr[:], ALU.mult, ALU.min).then_inc(dt_step, 1)
                v.tensor_scalar(dtm[:], dtr[:], 0.0, None, ALU.max)
                dve.wait_ge(dte_ready, at(dte_ready, 1))
                v.tensor_scalar(dtw[:], dte[:], 1.0, None, ALU.add).then_inc(dtw_ready, 1)
                dve.wait_ge(dtw_ready, at(dtw_ready, 1))
                v.tensor_scalar(dtd[:], dtw[:], 1.0, None, ALU.subtract).then_inc(dt_step, 1)
                dve.wait_ge(dt_step, at(dt_step, 3))
                v.tensor_scalar(dtz[:], dtd[:], 0.0, None, ALU.is_equal).then_inc(dt_step, 1)
                dve.wait_ge(dt_step, at(dt_step, 4))
                v.tensor_tensor(dtd[:], dtd[:], dtz[:], ALU.add).then_inc(dt_step, 1)
                dve.wait_ge(dt_step, at(dt_step, 5))
                v.reciprocal(dtd[:], dtd[:])
                dve.wait_ge(dtl_ready, at(dtl_ready, 1))
                v.tensor_tensor(dtl[:], dtl[:], dtz[:], ALU.add).then_inc(dt_step, 1)
                dve.wait_ge(dt_step, at(dt_step, 6))
                v.tensor_tensor(dtl[:], dtl[:], dtd[:], ALU.mult).then_inc(dt_step, 1)
                dve.wait_ge(dt_step, at(dt_step, 7))
                v.tensor_tensor(dtl[:], dtl[:], dte[:], ALU.mult).then_inc(lf_ready, 1)
                dve.wait_ge(lf_ready, at(lf_ready, 1))
                v.tensor_tensor(dt[:], dtl[:], dtm[:], ALU.add).then_inc(dt_ready, 1)
                dve.wait_ge(dt_ready, at(dt_ready, 1))
                v.tensor_tensor(dA[:], dt[:], over_g(neg_a[:, :], HM), ALU.mult).then_inc(dA_ready, 1)
                for k in range(2):
                    dve.wait_ge(tz_ready, at(tz_ready, k + 1))
                    v.scalar_tensor_tensor(sz[:, 2 * k:2 * k + 2, :], tz[:, 2 * k:2 * k + 2, :], 1.0,
                                           bank[4 + k][:, :].rearrange("t (b c) -> t b c", b=2), ALU.add, ALU.mult
                                           ).then_inc(sz_ready, 1)
                for q, k in enumerate((2, 0, 1)):
                    n = 128 if k < 2 else 64
                    dve.wait_ge(xp_ready, at(xp_ready, k + 1))
                    uk = u[0:n, k, :, :]
                    cw = P_AT["cw"][0] + TAPS * k
                    v.tensor_scalar(uk, xp[0:n, k, :, 0:S], WP[0:n, cw:cw + 1], wp("cb", k)[0:n], ALU.mult, ALU.add
                                    ).then_inc(conv_step, 1)
                    for i in range(1, TAPS):
                        dve.wait_ge(conv_step, at(conv_step, 4 * q + i))
                        v.scalar_tensor_tensor(uk, xp[0:n, k, :, i:i + S], WP[0:n, cw + i:cw + i + 1], uk,
                                               ALU.mult, ALU.add).then_inc(conv_step, 1)
                dve.wait_ge(th_ready, at(th_ready, 1))
                v.scalar_tensor_tensor(Bm[:], th[0:NS, 2, :, :], 1.0, u[0:NS, 2, :, :], ALU.add, ALU.mult
                                       ).then_inc(xs_ready, 1)
                v.scalar_tensor_tensor(Cm[:], th[32:32 + NS, 2, :, :], 1.0, u[32:32 + NS, 2, :, :], ALU.add, ALU.mult
                                       ).then_inc(xs_ready, 1)
                for k in range(2):
                    dve.wait_ge(th_ready, at(th_ready, k + 2))
                    v.scalar_tensor_tensor(xs[:, k, :, :], th[:, k, :, :], 1.0, u[:, k, :, :], ALU.add, ALU.mult
                                           ).then_inc(xs_ready, 1)
                dve.wait_ge(g_psum, at(g_psum, 1))
                v.scalar_tensor_tensor(Gm[:], bank[3][:, :].rearrange("s (b t) -> s b t", b=G), 0.25,
                                       over_g(tri[:, :]), ALU.mult, ALU.mult).then_inc(gm_ready, 1)
                dve.wait_ge(gm_ready, at(gm_ready, 1))
                for b in range(G):
                    dve.wait_ge(ex_ready, at(ex_ready, b + 1))
                    for h in range(HM):
                        ins = v.scalar_tensor_tensor(M[:, b, h, :], EX[:, b, h, :], dt[:, b, h:h + 1], Gm[:, b, :],
                                                     ALU.mult, ALU.mult)
                    ins.then_inc(m_ready, 1)
                dve.wait_ge(xd_ready, at(xd_ready, 1))
                for k in range(2):
                    dve.wait_ge(y_psum, at(y_psum, k + 1))
                    v.tensor_tensor(Y[:, 2 * k:2 * k + 2, :], bank[6 + k][:, :].rearrange("t (b c) -> t b c", b=2),
                                    xd[:, 2 * k:2 * k + 2, :, :].rearrange("t b k c -> t b (k c)"), ALU.add
                                    ).then_inc(y_step, 1)
                dve.wait_ge(sz_ready, at(sz_ready, 2))
                for k in range(2):
                    dve.wait_ge(y_step, at(y_step, k + 1))
                    v.scalar_tensor_tensor(Yz[:, 2 * k:2 * k + 2, :], Y[:, 2 * k:2 * k + 2, :], 0.5,
                                           sz[:, 2 * k:2 * k + 2, :], ALU.mult, ALU.mult).then_inc(y_step, 1)
                dve.wait_ge(l_loaded, at(l_loaded, 16))
                v.tensor_copy(lf[:], LT[:]).then_inc(lf_copied, 1)
                dve.wait_ge(cs_psum, at(cs_psum, 1))
                v.tensor_scalar(bi[:], bank[6][:, 0:G], 1.0, None, ALU.subtract).then_inc(bi_step, 1)
                dve.wait_ge(bi_step, at(bi_step, 1))
                v.tensor_scalar(bw[:], bi[:], 0.0, float(S), ALU.is_lt, ALU.mult).then_inc(bi_step, 1)
                dve.wait_ge(bi_step, at(bi_step, 2))
                v.tensor_tensor(bi[:], bi[:], bw[:], ALU.add).then_inc(bi_step, 1)
                dve.wait_ge(bi_step, at(bi_step, 3))
                for b in range(G):
                    ins = v.tensor_scalar(OH[:, b, :], iota_row[:], bi[:, b:b + 1], None, ALU.is_equal)
                ins.then_inc(ohj_ready, 1)
                dve.wait_ge(nb_psum, at(nb_psum, 1))
                v.tensor_scalar(bnd[:], bank[6][:, 8:8 + G].unsqueeze(2).broadcast_to([128, G, 128]), 1.0, None,
                                ALU.min).then_inc(bnd_ready, 1)
                dve.wait_ge(plug_psum, at(plug_psum, 1))
                v.tensor_scalar(sel[:], bank[6][:, :].rearrange("p (b t) -> p b t", b=G), 1.0, iota_part1[:, 0:1],
                                ALU.max, ALU.is_equal).then_inc(sel_ready, 1)
                dve.wait_ge(cr_ready, at(cr_ready, 2))
                for b in range(G):
                    ins = v.scalar_tensor_tensor(cu[:, b, :], C[:, b, 0:128], cr[:, b:b + 1], gb[:], ALU.mult, ALU.mult)
                ins.then_inc(cu_ready, 1)
                dve.wait_ge(mo_psum, at(mo_psum, 1))
                dve.wait_ge(yr_ready, at(yr_ready, 2))
                for b in range(G):
                    ins = v.scalar_tensor_tensor(X4[:, b, :], bank[4][:, 128 * b:128 * b + 128], yr[:, b:b + 1],
                                                 X3[:, b, :], ALU.mult, ALU.add)
                ins.then_inc(x4_ready, 1)
                dve.wait_ge(x4_ready, at(x4_ready, 1))
                norm(5, X4, XN)
                dve.wait_ge(x5_psum, at(x5_psum, 1))
                dve.wait_ge(xb_ready, at(xb_ready, 5))
                v.tensor_tensor(X5[:], bank[0][:, :].rearrange("t (b c) -> t b c", b=G), X4b[:], ALU.add
                                ).then_inc(x5_ready, 1)
                dve.wait_ge(x5_ready, at(x5_ready, 1))
                norm(6, X5, XN)
                dve.wait_ge(p_psum, at(p_psum, 1))
                v.tensor_copy(Pt, bank[2][0:RANK, :]).then_inc(p_ready, 1)
                dve.wait_ge(qf_psum, at(qf_psum, 1))
                v.tensor_copy(Qt, bank[7][0:RANK, :]).then_inc(qf_ready, 1)
                dve.wait_ge(x6_psum, at(x6_psum, 1))
                dve.wait_ge(xb_ready, at(xb_ready, 6))
                dve.wait_ge(stored, at(stored, 1))
                v.tensor_tensor(X6[:], bank[0][:, :].rearrange("t (b c) -> t b c", b=G), X5b[:], ALU.add
                                ).then_inc(x6_ready, 1)
                assert links[0] == LINKS, links

        @block.tensor
        def _(pe):
            mm = nc.tensor.matmul
            pe.wait_ge(once, 96)
            pe.wait_ge(const_vec, 5)
            pe.wait_ge(const_pool, 18)
            with pe.Fori(0, NG) as g:
                at = counter(g)

                def turn(dst, src):
                    for b in range(G):
                        ins = nc.tensor.transpose(dst[:, 128 * b:128 * b + 128], src[:, b, :], ident[:])
                    return ins

                def attention(j0, n, heads, width, values):
                    for t in range(n + 3):
                        if t < n:
                            i, q = t // 4, Q * (t % 4)
                            dst = bank[2 + t % 3]
                            if t >= 3:
                                pe.wait_ge(sm_ready, at(sm_ready, j0 + t - 2))
                            if heads == H1:
                                mm(dst[:, :], ones_bf[q:q + 1, :], negrow[q:q + 1, :], start=True, stop=False, skip_group_check=True)
                            for b in range(G):
                                ins = mm(dst[:, 128 * b:128 * b + 128],
                                         QT[q:q + Q, i, 128 * b:128 * b + 128],
                                         KT[q:q + Q, i, 128 * b:128 * b + 128],
                                         start=heads == H0, stop=True, skip_group_check=True)
                            ins.then_inc(s_psum, 1)
                        j = t - 2
                        if 0 <= j < n:
                            pe.wait_ge(sm_ready, at(sm_ready, j0 + j + 1))
                            if j >= 2:
                                pe.wait_ge(pt_ready, at(pt_ready, j0 + j - 1))
                            for b in range(G):
                                ins = nc.tensor.transpose(bank[5 + j % 2][:, 128 * b:128 * b + 128],
                                                          SM[:, j % 2, b, :], ident[:])
                            ins.then_inc(pt_psum, 1)
                        j = t - 3
                        if j >= 0:
                            pe.wait_ge(pt_ready, at(pt_ready, j0 + j + 1))
                            for b in range(G):
                                dst = bank[[7, 0][b // 2]]
                                c = ((b % 2) * heads + j) * (width + 1)
                                ins = mm(dst[:, c:c + width + 1], PT[:, j % 2, b, :], values[:, b, j, :],
                                         start=True, stop=True)
                            ins.then_inc(pv_done, 1)

                pe.wait_ge(c_loaded, at(c_loaded, 16))
                for k in range(2):
                    for b in range(G):
                        ins = nc.tensor.transpose(bank[4 + k][:, 128 * b:128 * b + 128],
                                                  C[:, b, 128 * k:128 * k + 128], ident[:])
                    ins.then_inc(ct_psum, 1)
                pe.wait_ge(xn_ready, at(xn_ready, 1))
                turn(bank[0], XN).then_inc(xt_psum, 1)
                pe.wait_ge(xt_ready, at(xt_ready, 1))
                pe.wait_ge(ct_ready, at(ct_ready, 2))
                for i in range(4):
                    mm(bank[1 + i][:, :], w("q0", i), XT[:], start=True, stop=True).then_inc(q_psum, 1)
                    mm(bank[[5, 6, 7, 0][i]][:, :], w("k0", i), XT[:], start=True, stop=True).then_inc(k_psum, 1)
                pe.wait_ge(q_ready, at(q_ready, 1))
                for b in range(G):
                    ins = mm(bank[1][:, 128 * b:128 * b + 128], XT[:, 128 * b:128 * b + 128], w("v0"),
                             start=True, stop=True)
                ins.then_inc(v_psum, 1)
                pe.wait_ge(q_ready, at(q_ready, 4))
                pe.wait_ge(k_ready, at(k_ready, 4))
                pe.wait_ge(v_ready, at(v_ready, 1))
                attention(0, H0, H0, D0, V0)
                pe.wait_ge(ao_ready, at(ao_ready, 2))
                turn(bank[1], AO).then_inc(at_psum, 1)
                pe.wait_ge(at_ready, at(at_ready, 1))
                for b in range(G):
                    ins = mm(bank[2][:, 128 * b:128 * b + 128], AT[:, 128 * b:128 * b + 128], w("proj"),
                             start=True, stop=True)
                ins.then_inc(att_psum, 1)
                for i in range(2):
                    for k in range(2):
                        ins = mm(bank[6 + i][:, :], w("k1", 2 * i + k), CT[:, k, :], start=k == 0, stop=k == 1)
                    ins.then_inc(k1_psum, 1)
                for b in range(G):
                    for k in range(2):
                        ins = mm(bank[0][:, 128 * b:128 * b + 128], CT[:, k, 128 * b:128 * b + 128], w("v1", k),
                                 start=k == 0, stop=k == 1)
                ins.then_inc(v1_psum, 1)
                pe.wait_ge(xn_ready, at(xn_ready, 2))
                turn(bank[3], XN).then_inc(xt_psum, 1)
                pe.wait_ge(xt_ready, at(xt_ready, 2))
                for i in range(2):
                    mm(bank[1 + i][:, :], w("q1", i), XT[:], start=True, stop=True).then_inc(q1_psum, 1)
                pe.wait_ge(q1_ready, at(q1_ready, 2))
                pe.wait_ge(k1_ready, at(k1_ready, 2))
                pe.wait_ge(v1_ready, at(v1_ready, 1))
                pe.wait_ge(neg_ready, at(neg_ready, 1))
                attention(H0, H1, H1, D1, V1)
                pe.wait_ge(ao_ready, at(ao_ready, 4))
                turn(bank[1], AO).then_inc(at_psum, 1)
                pe.wait_ge(at_ready, at(at_ready, 2))
                for b in range(G):
                    mm(bank[2][:, 128 * b:128 * b + 128], XT[:, 128 * b:128 * b + 128], w("out1", 0),
                       start=True, stop=False)
                    ins = mm(bank[2][:, 128 * b:128 * b + 128], AT[:, 128 * b:128 * b + 128], w("out1", 1),
                             start=False, stop=True)
                ins.then_inc(att_psum, 1)
                pe.wait_ge(xn_ready, at(xn_ready, 3))
                turn(bank[3], XL).then_inc(xt_psum, 1)
                pe.wait_ge(xt_ready, at(xt_ready, 3))
                for b in range(G):
                    ins = mm(bank[4][:, E * b:E * b + E], XT[:, 128 * b:128 * b + 128], w("gate"),
                             start=True, stop=True)
                ins.then_inc(gate_psum, 1)
                pe.wait_ge(oh_ready, at(oh_ready, 1))
                for r in range(2):
                    for b in range(G):
                        ins = nc.tensor.transpose(bank[5 + r][0:E, 128 * b:128 * b + 128], oh[:, r, b, :], ident[:])
                    ins.then_inc(oh_psum, 1)
                for r in range(2):
                    pe.wait_ge(ohm_ready, at(ohm_ready, 2))
                    acc = bank[7 - r]
                    for b in range(G):
                        mm(acc[:, 128 * b:128 * b + 128], ohT[:, r, 128 * b:128 * b + 128], B2[:], start=b == 0,
                           stop=False, skip_group_check=True)
                    src = XT
                    if r == 1:
                        pe.wait_ge(boost_ready, at(boost_ready, 1))
                        turn(bank[3], boost).then_inc(bt_psum, 1)
                        pe.wait_ge(bt_ready, at(bt_ready, 1))
                        src = boostT
                    for t in range(E * EC + 2):
                        if t < E * EC:
                            m = r * E * EC + t
                            if m >= 3:
                                odd = (m - 3) % 2
                                pe.wait_ge(h_vec if odd else h_act, at(h_vec if odd else h_act, (m - 3) // 2 + 1))
                            mm(bank[m % 3][:, :], w("w1", t), src[:], start=True, stop=False, skip_group_check=True)
                            mm(bank[m % 3][:, :], big_e[:, t // EC, :], ohM[:, r, :], start=False, stop=True,
                               skip_group_check=True).then_inc(h_psum, 1)
                        if t >= 2:
                            n = t - 2
                            m = r * E * EC + n
                            pe.wait_ge(h_vec if m % 2 else h_act, at(h_vec if m % 2 else h_act, m // 2 + 1))
                            for b in range(G):
                                ins = mm(acc[:, 128 * b:128 * b + 128], HS[:, m % 3, 128 * b:128 * b + 128],
                                         w("w2", n), start=False, stop=n == E * EC - 1, skip_group_check=True)
                            ins.then_inc(hs_used, 1)
                    pe.wait_ge(hs_used, at(hs_used, (r + 1) * E * EC))
                    nc.tensor.matmul(bank[3][0:1, 0:1], ones[:, 0:1], ones[:, 0:1], start=True, stop=True
                                     ).then_inc(eo_psum, 1)
                pe.wait_ge(xn_ready, at(xn_ready, 5))
                turn(bank[3], XN).then_inc(xt_psum, 1)
                pe.wait_ge(xt_ready, at(xt_ready, 4))
                for b in range(G):
                    ins = mm(bank[7][:, HM * b:HM * b + HM], XT[:, 128 * b:128 * b + 128], w("dt"),
                             start=True, stop=True)
                ins.then_inc(dt_psum, 1)
                for k in range(2):
                    mm(bank[k][:, :], w("xs", k), XT[:], start=True, stop=True).then_inc(xp_psum, 1)
                mm(bank[2][:, :], w("bc"), XT[:], start=True, stop=True).then_inc(xp_psum, 1)
                for k in range(2):
                    for b in range(2):
                        ins = mm(bank[4 + k][:, DI * b:DI * b + DI],
                                 XT[:, 128 * (2 * k + b):128 * (2 * k + b) + 128], w("z"), start=True, stop=True)
                    ins.then_inc(z_psum, 1)
                pe.wait_ge(xs_ready, at(xs_ready, 2))
                for b in range(G):
                    ins = mm(bank[3][:, 128 * b:128 * b + 128], Bm[:, b, :], Cm[:, b, :], start=True, stop=True)
                ins.then_inc(g_psum, 1)
                pe.wait_ge(sz_ready, at(sz_ready, 2))
                for b in range(G):
                    pe.wait_ge(r_ready, at(r_ready, b + 1))
                    if b >= 2:
                        pe.wait_ge(ex_ready, at(ex_ready, b - 1))
                    mm(bank[4 + b % 2][:, :], after[:], R[:, b, :, :].rearrange("u h t -> u (h t)"), start=True,
                       stop=True).then_inc(seg_psum, 1)
                for k in range(2):
                    pe.wait_ge(xs_ready, at(xs_ready, 3 + k))
                    turn(bank[k], xs[:, k, :, :]).then_inc(xh_psum, 1)
                pe.wait_ge(xh_ready, at(xh_ready, 2))
                for b in range(G):
                    pe.wait_ge(m_ready, at(m_ready, b + 1))
                    for h in range(HM):
                        c = 256 * (b % 2) + HP * h
                        ins = mm(bank[6 + b // 2][:, c:c + HP], M[:, b, h, :],
                                 xh[:, b, h // 2, HP * (h % 2):HP * (h % 2) + HP], start=True, stop=True)
                    if b % 2:
                        ins.then_inc(y_psum, 1)
                pe.wait_ge(y_step, at(y_step, 4))
                for k in range(2):
                    turn(bank[2 + k], Yz[:, :, 128 * k:128 * k + 128]).then_inc(yt_psum, 1)
                pe.wait_ge(yt_ready, at(yt_ready, 2))
                for b in range(G):
                    for k in range(2):
                        ins = mm(bank[4][:, 128 * b:128 * b + 128], YT[:, k, 128 * b:128 * b + 128], woutn[:, k, :],
                                 start=k == 0, stop=k == 1)
                ins.then_inc(mo_psum, 1)
                pe.wait_ge(lf_copied, at(lf_copied, 1))
                mm(bank[6][:, 0:G], tri[:], lf[:], start=True, stop=True).then_inc(cs_psum, 1)
                pe.wait_ge(ohj_ready, at(ohj_ready, 1))
                for b in range(G):
                    ins = mm(bank[6][:, 8 + b:9 + b], OH[:, b, :], ones_bf[:, 0:1], start=True, stop=True)
                ins.then_inc(nb_psum, 1)
                pe.wait_ge(bnd_ready, at(bnd_ready, 1))
                for b in range(G):
                    ins = mm(bank[6][:, 128 * b:128 * b + 128], bnd[:, b, :], tri_bf[:], start=True, stop=True)
                ins.then_inc(plug_psum, 1)
                pe.wait_ge(cu_ready, at(cu_ready, 1))
                mm(bank[7][:, :], decay[:], cu[:].rearrange("q b c -> q (b c)"), start=True, stop=True
                   ).then_inc(dp_psum, 1)
                pe.wait_ge(xn_ready, at(xn_ready, 6))
                turn(bank[5], XN).then_inc(xt_psum, 1)
                pe.wait_ge(xt_ready, at(xt_ready, 5))
                pe.wait_ge(dp_ready, at(dp_ready, 1))
                pe.wait_ge(sel_ready, at(sel_ready, 1))
                for b in range(G):
                    mm(bank[0][:, 128 * b:128 * b + 128], XT[:, 128 * b:128 * b + 128], winn[:], start=True, stop=False)
                    ins = mm(bank[0][:, 128 * b:128 * b + 128], sel[:, b, :], dp[:, b, :], start=False, stop=True)
                ins.then_inc(x5_psum, 1)
                pe.wait_ge(xn_ready, at(xn_ready, 7))
                turn(bank[1], XN).then_inc(xt_psum, 1)
                pe.wait_ge(xt_ready, at(xt_ready, 6))
                mm(bank[2][0:RANK, :], w("u1"), XT[:], start=True, stop=True).then_inc(p_psum, 1)
                pe.wait_ge(p_ready, at(p_ready, 1))
                for k in range(4):
                    mm(bank[3 + k][:, :], V1w[:, 128 * k:128 * k + 128], Pt, start=True, stop=True
                       ).then_inc(hf_psum, 1)
                for k in range(4):
                    pe.wait_ge(hf_ready, at(hf_ready, k + 1))
                    ins = mm(bank[7][0:RANK, :], w("u2", k, RANK), HF[:, k, :], start=k == 0, stop=k == 3)
                ins.then_inc(qf_psum, 1)
                pe.wait_ge(qf_ready, at(qf_ready, 1))
                for b in range(G):
                    ins = mm(bank[0][:, 128 * b:128 * b + 128], Qt[:, 128 * b:128 * b + 128], V2w[:], start=True,
                             stop=True)
                ins.then_inc(x6_psum, 1)


def layout(i):
    f = np.float32
    Wt = np.zeros((128, W_N), f)
    Pc = np.zeros((128, P_N), f)

    def put(name, a, k=0):
        at = W_AT[name][0] + k
        Wt[:a.shape[0], at:at + a.shape[1]] = a

    def col(name, a, k=0):
        Pc[:a.shape[0], P_AT[name][0] + k] = a

    qkv = np.zeros((128, 384), f)
    proj = np.zeros((128, 128), f)
    for n in range(8):
        qkv[16 * n:16 * n + 16, 48 * n:48 * n + 48] = i["L0_attn_w_qkv"][n]
        proj[16 * n:16 * n + 16, 16 * n:16 * n + 16] = i["L0_attn_w_proj"][n]
    for h in range(H0):
        at = 128 * (h // 4) + Q * (h % 4)
        put("q0", qkv[:, D0 * h:D0 * h + D0], at)
        put("k0", qkv[:, 128 + D0 * h:128 + D0 * h + D0], at)
    put("v0", qkv[:, 256:384])
    put("proj", proj)
    src, tgt = i["L0_xattn_W_src"].T, i["L0_xattn_W_tgt"].T
    for h in range(H1):
        n, r = h // 4, Q * (h % 4)
        mine = slice(D1 * h, D1 * h + D1)
        for k in range(2):
            put("k1", src[128 * k:128 * k + 128, mine], 128 * (2 * n + k) + r)
        put("q1", tgt[:, mine], 128 * n + r)
        Pc[r:r + D1, P_AT["bk1"][0] + n] = i["L0_xattn_b_src"][mine]
        Pc[r:r + D1, P_AT["bq1"][0] + n] = i["L0_xattn_b_tgt"][mine]
    w_out = i["L0_xattn_W_out"].T
    for k in range(2):
        put("v1", src[128 * k:128 * k + 128, 128:], 128 * k)
        put("out1", w_out[128 * k:128 * k + 128], 128 * k)
    put("gate", i["L0_ffn_gate_W"])
    for e in range(E):
        put("w1", i["L0_ffn_W1"][e], HID * e)
        for c in range(EC):
            put("w2", i["L0_ffn_W2"][e, 128 * c:128 * c + 128], 128 * (EC * e + c))
            col("b1", i["L0_ffn_b1"][e, 128 * c:128 * c + 128], EC * e + c)
    m_in = i["L1_attn_W_in"].T
    put("z", m_in[:, 0:DI])
    put("xs", m_in[:, DI:2 * DI])
    put("bc", m_in[:, 2 * DI:2 * DI + NS], 0)
    put("bc", m_in[:, 2 * DI + NS:2 * DI + 2 * NS], 32)
    put("dt", m_in[:, 2 * DI + 2 * NS:])
    cw, cb = i["L1_attn_conv_w"], i["L1_attn_conv_b"]
    for k, (rows, at) in enumerate([(slice(0, 128), 0), (slice(128, 256), 0), (slice(256, 272), 0)]):
        n = rows.stop - rows.start
        c = P_AT["cw"][0] + TAPS * k
        Pc[at:at + n, c:c + TAPS] = cw[rows]
        Pc[at:at + n, P_AT["cb"][0] + k] = cb[rows]
    c = P_AT["cw"][0] + TAPS * 2
    Pc[32:32 + NS, c:c + TAPS] = cw[272:288]
    Pc[32:32 + NS, P_AT["cb"][0] + 2] = cb[272:288]
    m_out = i["L1_attn_W_out"].T
    for k in range(2):
        put("mout", m_out[128 * k:128 * k + 128], 128 * k)
        col("normw", i["L1_attn_norm_w"][128 * k:128 * k + 128], k)
    put("win", i["L1_xattn_W_in"].T)
    col("gres", i["L1_xattn_g_res"])
    put("u1", i["L1_ffn_U1"])
    for k in range(4):
        put("u2", i["L1_ffn_U2"][128 * k:128 * k + 128], RANK * k)
        col("bff1", i["L1_ffn_b1"][128 * k:128 * k + 128], k)
    rows = [i["L0_attn_b_proj"], i["L0_xattn_b_src"][128:], i["L0_xattn_b_out"], i["L0_ffn_gate_b"],
            i["L0_ffn_ln_gamma"], i["L0_ffn_ln_beta"], i["L1_attn_dt_bias"], i["L1_attn_A_log"], i["L1_attn_D"],
            i["L1_xattn_b_in"], i["L1_xattn_g_init"][:128], i["L1_ffn_b2"]]
    Rr = np.ascontiguousarray(np.broadcast_to(np.concatenate(rows), (128, R_N)))
    return Wt, Pc, Rr, i["L0_ffn_b2"], i["L1_ffn_V1"], i["L1_ffn_V2"]


def kernel(**inputs):
    import concourse.bacc as bacc
    from concourse.bass_utils import run_bass_kernel_spmd

    i = {k: np.asarray(a) for k, a in inputs.items()}
    arrays = [i["x"], i["ctx_2048"], i["mask_BxS2_fk1"], i["mask_BxS2_fk1"].T, i["mask_BxS2_if0"].T, *layout(i)]
    names = ["x", "ctx", "mask", "mask_t", "lens_t", "w", "wp", "wr", "b2", "v1", "v2"]
    nc = bacc.Bacc("TRN2", target_bir_lowering=False, num_devices=1)
    feed, args = {}, []
    for name, a in zip(names, arrays):
        a = np.ascontiguousarray(a)
        feed[f"in_{name}"] = a
        args.append(nc.dram_tensor(f"in_{name}", a.shape, mybir.dt.from_np(a.dtype), kind="ExternalInput").ap())
    args.append(nc.dram_tensor("out", (B, S, D), F32, kind="ExternalOutput").ap())
    build(nc, *args)
    r = run_bass_kernel_spmd(nc, [feed], core_ids=[0])
    return r.results[0]["out"]
```

```python
from contextlib import ExitStack

import numpy as np

import concourse.bass as bass
from concourse import mybir

F32 = mybir.dt.float32
BF16 = mybir.dt.bfloat16
I32 = mybir.dt.int32
U32 = mybir.dt.uint32
ACT = mybir.ActivationFunctionType
ALU = mybir.AluOpType
AX = mybir.AxisListType

B, S, D, DC = 32, 128, 128, 256
G = 4
NG = B // G
GT = G * S
Q = 32
H0, D0 = 16, 8
H1, D1 = 8, 16
E, HID = 8, 256
EC = HID // 128
DI, NS, HM, HP = 256, 16, 4, 64
TAPS = 4
FF, RANK = 512, 32
LN_EPS = 1e-5
PATCH_EPS = 1e-3
N_CONST = 18
FRONT_STAGES, BACK_STAGES = 57, 69
BIG = 1e30

W_COLS = [("q0", 4 * 128), ("k0", 4 * 128), ("v0", 128), ("proj", 128),
          ("k1", 2 * 2 * 128), ("v1", 2 * 128), ("q1", 2 * 128), ("out1", 2 * 128), ("gate", E),
          ("w1", E * HID), ("w2", E * EC * 128), ("z", DI), ("xs", DI), ("bc", 128), ("dt", HM),
          ("mout", 2 * 128), ("win", 128), ("u1", RANK), ("u2", 4 * RANK)]
P_COLS = [("bk1", 2), ("bq1", 2), ("b1", E * EC), ("cw", 3 * TAPS), ("cb", 3), ("bff1", 4),
          ("normw", 2), ("gres", 1)]
R_COLS = [("bproj", 128), ("bv1", 128), ("bout", 128), ("gateb", E), ("gamma", 128), ("beta", 128),
          ("dtb", HM), ("alog", HM), ("dskip", HM), ("bin", 128), ("ginit", 128), ("bff2", 128)]


def places(cols):
    at, out = 0, {}
    for name, n in cols:
        out[name] = (at, at + n)
        at += n
    return out, at


W_AT, W_N = places(W_COLS)
P_AT, P_N = places(P_COLS)
R_AT, R_N = places(R_COLS)


def build(nc, x, ctx_in, mask, m_t, l_t, w_in, w_p, w_r, w_b2, w_v1, w_v2, out):
    x_t = x.rearrange("b t d -> t b d")
    c_t = ctx_in.rearrange("b t d -> t b d")
    o_t = out.rearrange("b t d -> t b d")

    stack = ExitStack()
    with stack:
        def sb(name, shape, dt=F32):
            return stack.enter_context(nc.sbuf_tensor(name, shape, dt))

        by_sem = []

        def sem(name, n=1):
            s = stack.enter_context(nc.semaphore(name))
            by_sem.append((s, n))
            return s

        def counter(g):
            def at(s, c):
                n = [k for t, k in by_sem if t is s][0]
                return g * n + c
            return at

        bank = [stack.enter_context(nc.psum_tensor(f"bank{i}", [128, 512], F32)) for i in range(8)]
        FB, BB = bank[0:4], bank[4:8]

        def seqs(b):
            return b[:, :].rearrange("p (b c) -> p b c", b=G)

        def cols(b):
            return slice(128 * b, 128 * b + 128)

        W = sb("W", [128, W_N])
        WP = sb("WP", [128, P_N])
        WR = sb("WR", [128, R_N])
        B2 = sb("B2", [E, 128])
        V1w = sb("V1w", [RANK, FF])
        V2w = sb("V2w", [RANK, 128])
        ident = sb("ident", [128, 128])
        tri = sb("tri", [128, 128])
        after = sb("after", [128, 128])
        tri_bf = sb("tri_bf", [128, 128], BF16)
        decay = sb("decay", [128, 128])
        ones_bf = sb("ones_bf", [128, 128], BF16)
        iota_row = sb("iota_row", [128, 128])
        iota_part1 = sb("iota_part1", [128, 1])
        big_e = sb("big_e", [E, E, 128], BF16)
        halfneg = sb("halfneg", [128, 16])
        eps = sb("eps", [128, 16])
        mark = sb("mark", [1, 32])
        neg_a = sb("neg_a", [128, HM])
        gb = sb("gb", [128, 128])
        woutn = sb("woutn", [128, 2, 128])
        winn = sb("winn", [128, 128])

        def w(name, k=None, n=128):
            a, b = W_AT[name]
            return W[:, a:b] if k is None else W[:, a + k * n:a + (k + 1) * n]

        def wp(name, k=0):
            return WP[:, P_AT[name][0] + k:P_AT[name][0] + k + 1]

        def wr(name):
            return WR[:, R_AT[name][0]:R_AT[name][1]]

        def over_g(row, n=128):
            return row.unsqueeze(1).broadcast_to([128, G, n])

        X = sb("X", [128, G, D])
        C = sb("C", [128, G, DC])
        MT = sb("MT", [128, G])
        LT = sb("LT", [128, G], I32)
        MB = sb("MB", [128, G, 128])
        negrow = sb("negrow", [128, GT], BF16)
        xb = sb("xb", [128, G, D])
        XN = sb("XN", [128, G, D])
        XT = sb("XT", [128, GT])
        QT = sb("QT", [128, 4, GT])
        KT = sb("KT", [128, 4, GT])
        V0 = sb("V0", [128, G, H0, D0 + 1])
        V1 = sb("V1", [128, G, H1, D1 + 1])
        mx = sb("mx", [128, 16, 4])
        SM = sb("SM", [128, 2, 4, 128])
        PT = sb("PT", [128, 2, 4, 128])
        base = PT[:, 0, 0, :]
        ones = PT[:, 0, 1, :]
        rs = sb("rs", [128, G, 8])
        AO = sb("AO", [128, G, D])
        AT = sb("AT", [128, GT])
        CT = sb("CT", [128, 2, GT])
        bm = sb("bm", [128, G, 128])
        vtmp = sb("vtmp", [128, G, 128])
        cu = vtmp
        X1 = sb("X1", [128, G, D])
        X1b = sb("X1b", [128, G, D])
        X2 = X1
        lg = sb("lg", [128, G, E])
        top = sb("top", [128, G, 8])
        topi = sb("topi", [128, G, 8], U32)
        topf = sb("topf", [128, G, 8])
        lsh = sb("lsh", [128, G, E])
        lex = sb("lex", [128, G, E])
        lsum = sb("lsum", [128, G])
        l2 = sb("l2", [128, G])
        oh = sb("oh", [128, 2, G, E])
        lf = sb("lf", [128, G])
        bi = sb("bi", [128, G])
        bw = sb("bw", [128, G])
        OH = sb("OH", [128, G, 128], BF16)
        bnd = sb("bnd", [128, G, 128], BF16)
        csq = SM[:].rearrange("p a b c -> p (a b) c").rearrange("p (b k) c -> p b (k c)", k=2)
        css = sb("css", [128, G])
        cr = sb("cr", [128, G])
        XL = sb("XL", [128, G, D])
        XLT = sb("XLT", [128, GT])
        X2b = sb("X2b", [128, G, D])
        gv = sb("gv", [128, 2, G])
        ohT = sb("ohT", [E, 2, GT])
        ohM = sb("ohM", [E, 2, GT], BF16)
        sel = sb("sel", [128, G, 128])
        dp = sb("dp", [128, G, 128])
        HS = sb("HS", [128, 3, GT])
        boostT = sb("boostT", [128, GT])
        eoT = sb("eoT", [128, GT])
        f1 = sb("f1", [128, G, D])
        YN = sb("YN", [128, G, D])
        YNT = sb("YNT", [128, GT])
        X3 = sb("X3", [128, G, D])
        xp = sb("xp", [128, 3, G, S + TAPS - 1])
        u = sb("u", [128, 3, G, S])
        th = sb("th", [128, 3, G, S])
        xs = sb("xs", [128, 2, G, S])
        Bm = sb("Bm", [NS, G, S])
        Cm = sb("Cm", [NS, G, S])
        xh = sb("xh", [128, G, 2, 128])
        xd = sb("xd", [128, G, 2, 128])
        tz = sb("tz", [128, G, DI])
        sz = sb("sz", [128, G, DI])
        dtr, dta, dte, dtw, dtl, dtd, dtz, dtm, dt, dA = (
            sb(n, [128, G, HM]) for n in ("dtr", "dta", "dte", "dtw", "dtl", "dtd", "dtz", "dtm", "dt", "dA"))
        RE = sb("RE", [128, 4, GT])
        R = RE[:, 0:2, :].rearrange("p b (h t) -> p b h t", h=HM)
        EX = RE[:, 2:4, :].rearrange("p b (h t) -> p b h t", h=HM)
        HF = RE
        Gm = sb("Gm", [128, G, 128])
        M = sb("M", [128, 2, HM, 128])
        Y = u[:, 0:2, :, :].rearrange("p k b t -> p (k b t)").rearrange("p (b c) -> p b c", c=DI)
        Yz = tz
        ysq = Y
        yss = sb("yss", [128, G])
        yr = sb("yr", [128, G])
        YT = th[:, 0:2, :, :].rearrange("p k b t -> p k (b t)")
        X4 = f1
        X4b = sb("X4b", [128, G, D])
        q6 = sb("q6", [128, G])
        X5 = X3
        X5b = X4b
        Pt = YNT[0:RANK, :]
        Qt = boostT[0:RANK, :]
        X6 = sb("X6", [128, G, D])

        once = stack.enter_context(nc.semaphore("weights_loaded"))
        const_pool = stack.enter_context(nc.semaphore("pool_constants"))
        const_vec = stack.enter_context(nc.semaphore("vector_constants"))
        const_act = stack.enter_context(nc.semaphore("scalar_constants"))
        x_loaded, c_loaded, m_loaded, l_loaded, mt_loaded, stored = (
            sem(n, 16) for n in ("x_loaded", "c_loaded", "m_loaded", "l_loaded", "mt_loaded", "stored"))

        class Norms:

            def __init__(self, part, n):
                self.bst = sb(part + "_bst", [128, G, 6])
                self.mv = sb(part + "_mv", [128, G, 2])
                self.vs = sb(part + "_vs", [128, G])
                self.rstd = sb(part + "_rstd", [128, G])
                self.bn_done = sem(part + "_bn_done", n * G)
                self.mv_ready = sem(part + "_mv_ready", n * G)
                self.ve_ready = sem(part + "_ve_ready", n)
                self.rstd_ready = sem(part + "_rstd_ready", n)
                self.xn_ready = sem(part + "_xn_ready", n)
                self.xt_psum = sem(part + "_xt_psum", 3)
                self.xt_ready = sem(part + "_xt_ready", 3)

        NF, NB = Norms("front", 3), Norms("back", 4)
        xb_ready, xbb_ready = sem("xb_ready", 3), sem("xbb_ready", 2)
        q_psum, k_psum, q_ready, k_ready = (sem(n, 4) for n in ("q_psum", "k_psum", "q_ready", "k_ready"))
        v_psum, v_ready = sem("v_psum"), sem("v_ready")
        NJ = H0 + H1
        s_psum, max_ready, sm_ready, pt_psum, pt_ready, pv_done = (
            sem(n, NJ) for n in ("s_psum", "max_ready", "sm_ready", "pt_psum", "pt_ready", "pv_done"))
        rs_ready, ao_ready = sem("rs_ready", 4), sem("ao_ready", 4)
        at_psum, at_ready, att_psum = sem("at_psum", 2), sem("at_ready", 2), sem("att_psum", 2)
        x1_ready, x2_ready = sem("x1_ready"), sem("x2_ready")
        ct_psum, ct_ready = sem("ct_psum", 2), sem("ct_ready", 2)
        neg_ready, bm_ready = sem("neg_ready"), sem("bm_ready")
        k1_psum, k1_ready, q1_psum, q1_ready = (sem(n, 2) for n in ("k1_psum", "k1_ready", "q1_psum", "q1_ready"))
        v1_psum, v1_part, v1_ready = sem("v1_psum"), sem("v1_part"), sem("v1_ready")
        gate_psum, lsh_ready, lex_ready, oh_ready = (
            sem(n) for n in ("gate_psum", "lsh_ready", "lex_ready", "oh_ready"))
        oh_psum, ohm_ready = sem("oh_psum", 2), sem("ohm_ready", 2)
        lf_copied, bi_step, ohj_ready, cs_psum, nb_psum, bnd_ready, plug_psum, sel_ready = (
            sem(n, k) for n, k in (("lf_copied", 1), ("bi_step", 3), ("ohj_ready", 1), ("cs_psum", 1),
                                   ("nb_psum", 1), ("bnd_ready", 1), ("plug_psum", 1), ("sel_ready", 1)))
        css_ready, cr_ready, cu_ready, dp_psum, dp_ready = (
            sem(n, k) for n, k in (("css_ready", G), ("cr_ready", 2), ("cu_ready", 1), ("dp_psum", 1), ("dp_ready", 1)))
        LINKS = 9
        link_sem = sem("gate_link", LINKS)

        NH = 2 * E * EC
        h_psum, h_act, h_vec, hs_used = sem("h_psum", NH), sem("h_act", NH // 2), sem("h_vec", NH // 2), sem("hs_used", NH)
        eo_ready, boost_ready, et_psum, f_ready = sem("eo_ready", 2), sem("boost_ready"), sem("et_psum", 2), sem("f_ready", 2)
        gamma_done, x3_ready = sem("gamma_done"), sem("x3_ready")
        z_psum, xp_psum, xp_ready, dt_psum = sem("z_psum", 2), sem("xp_psum", 3), sem("xp_ready", 3), sem("dt_psum")
        tz_ready, sz_ready = sem("tz_ready", 2), sem("sz_ready", 2)
        conv_step, th_ready, bc_ready, xs_ready = sem("conv_step", 12), sem("th_ready", 3), sem("bc_ready", 2), sem("xs_ready", 2)
        xh_psum, xh_ready, xd_ready = sem("xh_psum", 2), sem("xh_ready", 2), sem("xd_ready")
        dt_step, dte_ready, dtw_ready, dtl_ready, dt_ready = (
            sem("dt_step", 8), sem("dte_ready"), sem("dtw_ready"), sem("dtl_ready"), sem("dt_ready"))
        dA_ready, r_ready, seg_psum, ex_ready = sem("dA_ready"), sem("r_ready", G), sem("seg_psum", G), sem("ex_ready", G)
        g_psum, gm_ready, m_ready, y_done = sem("g_psum"), sem("gm_ready"), sem("m_ready", G), sem("y_done", G)
        y_step, yss_ready, yr_ready, yt_psum, yt_ready = (
            sem("y_step", 4), sem("yss_ready", G), sem("yr_ready", 2), sem("yt_psum", 2), sem("yt_ready", 2))
        mo_psum, x4_ready = sem("mo_psum"), sem("x4_ready")
        r6_step = sem("r6_step", 5)
        x5_psum, x5_ready = sem("x5_psum"), sem("x5_ready")
        p_psum, p_ready, hf_psum, hf_ready = sem("p_psum"), sem("p_ready"), sem("hf_psum", 4), sem("hf_ready", 4)
        qf_psum, qf_ready, x6_psum, x6_ready = sem("qf_psum"), sem("qf_ready"), sem("x6_psum"), sem("x6_ready")

        def woven(front, back, g):
            order = sorted([((i + 0.5) / FRONT_STAGES, 0) for i in range(FRONT_STAGES)] +
                           [((i + 0.5) / BACK_STAGES, 1) for i in range(BACK_STAGES)])
            parts = front(g, False), back(g - 1)
            for _, part in order:
                next(parts[part])
            assert all(next(p, None) is None for p in parts)

        def alone(stages, n):
            m = sum(1 for _ in stages)
            assert m == n, (m, n)

        def run(engine, front, back):
            alone(front(0, True), FRONT_STAGES)
            with engine.Fori(1, NG) as g:
                woven(front, back, g)
            alone(back(NG - 1), BACK_STAGES)

        block = stack.enter_context(nc.Block())

        @block.sync
        def _(sp):
            for dst, src in ((W, w_in), (WP, w_p), (WR, w_r), (B2, w_b2), (V1w, w_v1), (V2w, w_v2)):
                sp.dma_start(dst[:], src).then_inc(once, 16)
            sp.sem_inc(stored, 1)

            def load_x(g):
                sp.dma_start(X[:], x_t[:, bass.ds(g * G, G), :]).then_inc(x_loaded, 16)

            def load_rest(g):
                sp.dma_start(C[:], c_t[:, bass.ds(g * G, G), :]).then_inc(c_loaded, 16)
                sp.dma_start(MT[:], m_t[:, bass.ds(g * G, G)]).then_inc(mt_loaded, 16)
                sp.dma_start(MB[:], mask[bass.ds(g * G, G), :].unsqueeze(0).broadcast_to([128, G, S])
                             ).then_inc(m_loaded, 16)
                sp.dma_start(LT[:], l_t[:, bass.ds(g * G, G)]).then_inc(l_loaded, 16)

            def load_next(g):
                at = counter(g)
                sp.wait_ge(NF.xn_ready, at(NF.xn_ready, 1))
                sp.wait_ge(xb_ready, at(xb_ready, 1))
                load_x(g + 1)
                sp.wait_ge(cu_ready, at(cu_ready, 1))
                load_rest(g + 1)

            def store(g):
                sp.wait_ge(x6_ready, counter(g)(x6_ready, 1))
                sp.dma_start(o_t[:, bass.ds(g * G, G), :], X6[:]).then_inc(stored, 16)

            load_x(0)
            load_rest(0)
            load_next(0)
            with sp.Fori(1, NG - 1) as g:
                load_next(g)
                store(g - 1)
            store(NG - 2)
            store(NG - 1)
            sp.wait_ge(stored, 16 * NG + 1)

        @block.gpsimd
        def _(pool):
            pg = nc.gpsimd
            nconst = [0]

            def const(ins):
                nconst[0] += 1
                ins.then_inc(const_pool, 1)
                pool.wait_ge(const_pool, nconst[0])

            const(pg.memset(ones, 1.0))
            const(pg.memset(ones_bf[:], 1.0))
            const(pg.memset(halfneg[:], -0.5))
            const(pg.memset(eps[:], LN_EPS))
            for out_, step, sign, op in ((ident, 1, -1, ALU.is_equal), (tri, 1, -1, ALU.is_ge),
                                         (tri_bf, 1, -1, ALU.is_ge), (after, -1, 1, ALU.is_gt)):
                const(pg.affine_select(out=out_[:], in_=ones, pattern=[[step, 128]], compare_op=op,
                                       fill=0.0, base=0, channel_multiplier=sign))
            const(pg.iota(iota_row[:], pattern=[[1, 128]], base=0, channel_multiplier=0,
                          allow_small_or_imprecise_dtypes=True))
            const(pg.iota(iota_part1[:], pattern=[[0, 1]], base=1, channel_multiplier=1,
                          allow_small_or_imprecise_dtypes=True))
            const(pg.iota(base, pattern=[[1, 128]], base=0, channel_multiplier=-1,
                          allow_small_or_imprecise_dtypes=True))
            const(pg.tensor_scalar(base, base, 0.0, None, ALU.max))
            const(pg.memset(decay[:], float(-np.expm1(-PATCH_EPS))))
            const(pg.tensor_tensor(base, decay[:], base, ALU.pow))
            const(pg.affine_select(out=decay[:], in_=base, pattern=[[1, 128]], compare_op=ALU.is_ge,
                                   fill=0.0, base=0, channel_multiplier=-1))
            const(pg.memset(big_e[:], BIG))
            const(pg.affine_select(out=big_e[:], in_=big_e[:], pattern=[[1, E], [0, 128]], compare_op=ALU.is_equal,
                                   fill=0.0, base=0, channel_multiplier=-1))
            pg.memset(V0[:], 1.0)
            pg.memset(V1[:], 1.0)
            const(pg.memset(xp[:], 0.0))
            assert nconst[0] == N_CONST
            pool.wait_ge(once, 96)

            def inverse_std(at, N, k):
                pool.wait_ge(N.mv_ready, at(N.mv_ready, G * (k + 1)))
                pg.tensor_tensor(N.vs[:], N.mv[:, :, 1], eps[:, 0:G], ALU.add).then_inc(N.ve_ready, 1)
                pool.wait_ge(N.ve_ready, at(N.ve_ready, k + 1))
                return pg.tensor_tensor(N.rstd[:], N.vs[:], halfneg[:, 0:G], ALU.pow)

            def front(g, first):
                at, prev = counter(g), counter(g - 1)
                pool.wait_ge(x_loaded, at(x_loaded, 16))
                pg.tensor_tensor(xb[:], X[:], over_g(wr("bproj")), ALU.add).then_inc(xb_ready, 1)
                inverse_std(at, NF, 0).then_inc(NF.rstd_ready, 1)
                yield
                pool.wait_ge(mt_loaded, at(mt_loaded, 16))
                pg.tensor_tensor(bm[:], over_g(wr("bv1")), MT[:].unsqueeze(2).broadcast_to([128, G, 128]), ALU.mult
                                 ).then_inc(bm_ready, 1)
                pool.wait_ge(css_ready, at(css_ready, G))
                pg.tensor_tensor(cr[:], css[:], eps[:, 0:G], ALU.add).then_inc(cr_ready, 1)
                pool.wait_ge(cr_ready, at(cr_ready, 1))
                pg.tensor_tensor(cr[:], cr[:], halfneg[:, 0:G], ALU.pow).then_inc(cr_ready, 1)
                for _ in range(30):
                    yield
                pool.wait_ge(x1_ready, at(x1_ready, 1))
                pg.tensor_tensor(X1b[:], X1[:], over_g(wr("bout")), ALU.add).then_inc(xb_ready, 1)
                inverse_std(at, NF, 1).then_inc(NF.rstd_ready, 1)
                for _ in range(17):
                    yield
                pool.wait_ge(x2_ready, at(x2_ready, 1))
                if not first:
                    pool.wait_ge(x3_ready, prev(x3_ready, 1))
                pg.tensor_tensor(X2b[:], X2[:], over_g(wr("beta")), ALU.add).then_inc(xb_ready, 1)
                inverse_std(at, NF, 2).then_inc(NF.rstd_ready, 1)
                for _ in range(FRONT_STAGES - 48):
                    yield

            def back(g):
                at = counter(g)
                for _ in range(39):
                    yield
                inverse_std(at, NB, 0).then_inc(NB.rstd_ready, 1)
                yield
                yield
                inverse_std(at, NB, 1).then_inc(NB.rstd_ready, 1)
                for _ in range(6):
                    yield
                pool.wait_ge(dA_ready, at(dA_ready, 1))
                for b in range(G):
                    if b >= 2:
                        pool.wait_ge(seg_psum, at(seg_psum, b - 1))
                    pg.tensor_tensor(R[:, b % 2, :, :], tri[:, :].unsqueeze(1).broadcast_to([128, HM, 128]),
                                     dA[:, b, :].unsqueeze(2).broadcast_to([128, HM, 128]),
                                     ALU.mult).then_inc(r_ready, 1)
                    if b == 1:
                        pool.wait_ge(xh_ready, at(xh_ready, 2))
                        for c in range(G):
                            ins = pg.tensor_tensor(xd[:, c, :, :].rearrange("t k (h p) -> t (k h) p", p=HP),
                                                   xh[:, c, :, :].rearrange("t k (h p) -> t (k h) p", p=HP),
                                                   wr("dskip").unsqueeze(2).broadcast_to([128, HM, HP]), ALU.mult)
                        ins.then_inc(xd_ready, 1)
                    yield
                for _ in range(4):
                    yield
                pool.wait_ge(yss_ready, at(yss_ready, G))
                pg.tensor_tensor(yr[:], yss[:], eps[:, 0:G], ALU.add).then_inc(yr_ready, 1)
                pool.wait_ge(yr_ready, at(yr_ready, 1))
                pg.tensor_tensor(yr[:], yr[:], halfneg[:, 0:G], ALU.pow).then_inc(yr_ready, 1)
                yield
                yield
                pool.wait_ge(x4_ready, at(x4_ready, 1))
                pg.tensor_tensor(X4b[:], X4[:], over_g(wr("bin")), ALU.add).then_inc(xbb_ready, 1)
                inverse_std(at, NB, 2).then_inc(r6_step, 1)
                pool.wait_ge(r6_step, at(r6_step, 1))
                pg.tensor_tensor(q6[:], NB.rstd[:], NB.rstd[:], ALU.mult).then_inc(r6_step, 1)
                pool.wait_ge(r6_step, at(r6_step, 2))
                pg.tensor_tensor(NB.vs[:], q6[:], NB.mv[:, :, 1], ALU.mult).then_inc(r6_step, 1)
                pool.wait_ge(r6_step, at(r6_step, 3))
                pg.tensor_tensor(q6[:], NB.vs[:], eps[:, 0:G], ALU.add).then_inc(r6_step, 1)
                pool.wait_ge(r6_step, at(r6_step, 4))
                pg.tensor_tensor(q6[:], q6[:], halfneg[:, 0:G], ALU.pow).then_inc(r6_step, 1)
                pool.wait_ge(r6_step, at(r6_step, 5))
                pg.tensor_tensor(NB.rstd[:], NB.rstd[:], q6[:], ALU.mult).then_inc(NB.rstd_ready, 1)
                for _ in range(4):
                    yield
                pool.wait_ge(x5_ready, at(x5_ready, 1))
                pg.tensor_tensor(X5b[:], X5[:], over_g(wr("bff2")), ALU.add).then_inc(xbb_ready, 1)
                inverse_std(at, NB, 3).then_inc(NB.rstd_ready, 1)
                for _ in range(BACK_STAGES - 61):
                    yield

            run(pool, front, back)

        @block.scalar
        def _(act):
            ac = nc.scalar
            act.wait_ge(once, 96)
            ac.activation(neg_a[:], wr("alog"), ACT.Exp).then_inc(const_act, 1)

            def front(g, first):
                at, prev = counter(g), counter(g - 1)

                def copy_xt(k, src, dst=XT):
                    act.wait_ge(NF.xt_psum, at(NF.xt_psum, k + 1))
                    ac.copy(dst[:], src[:, :]).then_inc(NF.xt_ready, 1)

                def exps(j0, n, scale):
                    for t in range(n + 3):
                        j = t - 2
                        if 0 <= j < n:
                            act.wait_ge(pt_psum, at(pt_psum, j0 + j + 1))
                            if j >= 2:
                                act.wait_ge(pv_done, at(pv_done, j0 + j - 1))
                            ac.activation(PT[:, j % 2, :, :], FB[2][:, :], ACT.Exp, scale=scale).then_inc(pt_ready, 1)
                        yield

                act.wait_ge(c_loaded, at(c_loaded, 16))
                for b in range(G):
                    ac.activation(csq[:, b, :], C[:, b, :], ACT.Square, scale=DC ** -0.5, accum_out=css[:, b:b + 1]
                                  ).then_inc(css_ready, 1)
                yield
                for k in range(2):
                    act.wait_ge(ct_psum, at(ct_psum, k + 1))
                    ac.copy(CT[:, k, :], FB[k][:, :]).then_inc(ct_ready, 1)
                yield
                copy_xt(0, FB[2])
                yield
                for i in range(4):
                    act.wait_ge(q_psum, at(q_psum, i + 1))
                    ac.copy(QT[:, i, :], FB[2 * (i % 2)][:, :]).then_inc(q_ready, 1)
                    yield
                yield
                yield from exps(0, H0, D0 ** -0.5)
                yield
                act.wait_ge(at_psum, at(at_psum, 1))
                ac.copy(AT[:], FB[2][:, :]).then_inc(at_ready, 1)
                yield
                yield
                yield
                yield
                copy_xt(1, FB[2])
                yield
                yield
                yield from exps(H0, H1, D1 ** -0.5)
                yield
                act.wait_ge(at_psum, at(at_psum, 2))
                ac.copy(AT[:], FB[0][:, :]).then_inc(at_ready, 1)
                yield
                yield
                yield
                yield
                if not first:
                    act.wait_ge(boost_ready, prev(boost_ready, 1))
                copy_xt(2, FB[2], XLT)
                yield
                act.wait_ge(lsh_ready, at(lsh_ready, 1))
                ac.activation(lex[:], lsh[:], ACT.Exp).then_inc(lex_ready, 1)
                yield
                yield
                yield
                yield
                yield
                act.wait_ge(dp_psum, at(dp_psum, 1))
                if not first:
                    act.wait_ge(x5_psum, prev(x5_psum, 1))
                ac.copy(dp[:], seqs(FB[1])).then_inc(dp_ready, 1)
                yield

            def back(g):
                at = counter(g)

                def copy_xt(k, src):
                    act.wait_ge(NB.xt_psum, at(NB.xt_psum, k + 1))
                    ac.copy(YNT[:], src[:, :]).then_inc(NB.xt_ready, 1)

                for r in range(2):
                    for n in range(E * EC + 2):
                        m = r * E * EC + n
                        if n < E * EC and n % 2 == 0:
                            act.wait_ge(h_psum, at(h_psum, m + 1))
                            if m >= 3:
                                act.wait_ge(hs_used, at(hs_used, m - 2))
                            ac.activation(HS[:, m % 3, :], BB[m % 2][:, :], ACT.Relu,
                                          bias=wp("b1", n)).then_inc(h_act, 1)
                        yield
                    act.wait_ge(hs_used, at(hs_used, (r + 1) * E * EC))
                    if r == 1:
                        act.wait_ge(et_psum, at(et_psum, 1))
                    ac.copy(eoT[:], BB[2][:, :]).then_inc(eo_ready, 1)
                    yield
                yield
                yield
                yield
                yield
                yield
                copy_xt(0, BB[3])
                yield
                act.wait_ge(xp_psum, at(xp_psum, 1))
                ac.copy(xp[0:64, 2, :, TAPS - 1:], seqs(BB[2])[0:64]).then_inc(xp_ready, 1)
                yield
                for k in range(2):
                    act.wait_ge(xp_psum, at(xp_psum, k + 2))
                    ac.copy(xp[:, k, :, TAPS - 1:], seqs(BB[k])).then_inc(xp_ready, 1)
                act.wait_ge(dt_step, at(dt_step, 2))
                ac.activation(dte[:], dta[:], ACT.Exp).then_inc(dte_ready, 1)
                act.wait_ge(dtw_ready, at(dtw_ready, 1))
                ac.activation(dtl[:], dtw[:], ACT.Ln).then_inc(dtl_ready, 1)
                yield
                for k in range(2):
                    act.wait_ge(z_psum, at(z_psum, k + 1))
                    ac.activation(tz[:, 2 * k:2 * k + 2, :], BB[2 + k][:, :], ACT.Tanh, scale=0.5).then_inc(tz_ready, 1)
                act.wait_ge(conv_step, at(conv_step, 4))
                ac.activation(th[0:64, 2, :, :], u[0:64, 2, :, :], ACT.Tanh, scale=0.5).then_inc(th_ready, 1)
                yield
                for k in range(2):
                    act.wait_ge(conv_step, at(conv_step, 4 * k + 8))
                    ac.activation(th[:, k, :, :], u[:, k, :, :], ACT.Tanh, scale=0.5).then_inc(th_ready, 1)
                yield
                for k in range(2):
                    act.wait_ge(xh_psum, at(xh_psum, k + 1))
                    ac.mul(xh[:, :, k, :], seqs(BB[1 + k]), 0.5).then_inc(xh_ready, 1)
                yield
                for b in range(G):
                    act.wait_ge(seg_psum, at(seg_psum, b + 1))
                    if b >= 2:
                        act.wait_ge(m_ready, at(m_ready, b - 1))
                    ac.activation(EX[:, b % 2, :, :], BB[1 + b % 2][:, :], ACT.Exp).then_inc(ex_ready, 1)
                    yield
                yield
                yield
                act.wait_ge(y_step, at(y_step, 4))
                for b in range(G):
                    ac.activation(ysq[:, b, :], Yz[:, b, :], ACT.Square, scale=DI ** -0.5, accum_out=yss[:, b:b + 1]
                                  ).then_inc(yss_ready, 1)
                for k in range(2):
                    act.wait_ge(yt_psum, at(yt_psum, k + 1))
                    ac.copy(YT[:, k, :], BB[1 + k][:, :]).then_inc(yt_ready, 1)
                yield
                yield
                yield
                yield
                copy_xt(1, BB[0])
                yield
                yield
                yield
                yield
                copy_xt(2, BB[2])
                yield
                yield
                for k in range(4):
                    act.wait_ge(hf_psum, at(hf_psum, k + 1))
                    ac.activation(HF[:, k, :], BB[k % 3][:, :], ACT.Gelu_apprx_tanh,
                                  bias=wp("bff1", k)).then_inc(hf_ready, 1)
                    if k % 2:
                        yield
                yield
                yield

            run(act, front, back)

        @block.vector
        def _(dve):
            v = nc.vector
            dve.wait_ge(once, 96)
            for k in range(2):
                v.tensor_scalar(woutn[:, k, :], w("mout", k), wp("normw", k), None, ALU.mult).then_inc(const_vec, 1)
            v.tensor_scalar(winn[:], w("win"), wp("gres"), None, ALU.mult).then_inc(const_vec, 1)
            v.tensor_scalar(gb[:], wr("ginit"), float(np.exp(-PATCH_EPS)), None, ALU.mult).then_inc(const_vec, 1)
            dve.wait_ge(const_act, 1)
            v.tensor_scalar(neg_a[:], neg_a[:], -1.0, None, ALU.mult).then_inc(const_vec, 1)
            dve.wait_ge(const_vec, 5)
            dve.wait_ge(const_pool, N_CONST)
            carried = [0]

            def carry():
                k = carried[0] % 32
                carried[0] += 1
                v.memset(mark[:, k:k + 1], 0.0)

            def statistics(at, N, k, src):
                for b in range(G):
                    v.bn_stats(N.bst[:, b, :], src[:, b, :]).then_inc(N.bn_done, 1)
                dve.wait_ge(N.bn_done, at(N.bn_done, G * (k + 1)))
                carry()
                for b in range(G):
                    v.bn_aggr(N.mv[:, b, :], N.bst[:, b, :]).then_inc(N.mv_ready, 1)

            def normed(at, N, k, src, dst):
                dve.wait_ge(N.mv_ready, at(N.mv_ready, G * (k + 1)))
                dve.wait_ge(N.rstd_ready, at(N.rstd_ready, k + 1))
                for b in range(G):
                    ins = v.tensor_scalar(dst[:, b, :], src[:, b, :], N.mv[:, b, 0:1], N.rstd[:, b:b + 1],
                                          ALU.subtract, ALU.mult)
                ins.then_inc(N.xn_ready, 1)

            def front(g, first):
                at, prev = counter(g), counter(g - 1)
                links = [0]

                def link(ins):
                    links[0] += 1
                    ins.then_inc(link_sem, 1)
                    dve.wait_ge(link_sem, at(link_sem, links[0]))

                def attended(n, h0, heads, width, last):
                    o = FB[3][:, 0:G * heads * (width + 1)].rearrange("t (b h e) -> t b h e", b=G, h=heads)
                    dve.wait_ge(pv_done, at(pv_done, last))
                    v.reciprocal(rs[:, :, 0:heads], o[:, :, :, width]).then_inc(rs_ready, 1)
                    dve.wait_ge(rs_ready, at(rs_ready, n + 1))
                    for b in range(G):
                        ins = v.tensor_tensor(
                            AO[:, b, h0 * width:(h0 + heads) * width].rearrange("t (h e) -> t h e", h=heads),
                            o[:, b, :, 0:width], rs[:, b, 0:heads].unsqueeze(2).broadcast_to([128, heads, width]),
                            ALU.mult)
                    ins.then_inc(ao_ready, 1)

                def maxima(j0, n):
                    for t in range(n + 3):
                        if t < n:
                            j = j0 + t
                            sc = seqs(FB[t % 2])
                            m = mx[:, t, :]
                            dve.wait_ge(s_psum, at(s_psum, j + 1))
                            v.tensor_reduce(m, sc, AX.X, ALU.max).then_inc(max_ready, 1)
                            dve.wait_ge(max_ready, at(max_ready, j + 1))
                            if t >= 2:
                                dve.wait_ge(pt_psum, at(pt_psum, j - 1))
                            v.tensor_tensor(SM[:, t % 2, :, :], sc, m.unsqueeze(2).broadcast_to([128, 4, 128]),
                                            ALU.subtract).then_inc(sm_ready, 1)
                        if t == n // 2 + 2:
                            attended(0 if n == H0 else 2, 0, n // 2, D // n, j0 + n // 2)
                        yield

                dve.wait_ge(x_loaded, at(x_loaded, 16))
                statistics(at, NF, 0, X)
                dve.wait_ge(m_loaded, at(m_loaded, 16))
                v.tensor_scalar(negrow[:], MB[:].rearrange("p b t -> p (b t)"), 0.0, -BIG, ALU.is_equal, ALU.mult
                                ).then_inc(neg_ready, 1)
                yield
                normed(at, NF, 0, X, XN)
                yield
                yield
                for i in range(4):
                    dve.wait_ge(k_psum, at(k_psum, i + 1))
                    v.tensor_copy(KT[:, i, :], FB[2 * (i % 2) + 1][:, :]).then_inc(k_ready, 1)
                    yield
                dve.wait_ge(v_psum, at(v_psum, 1))
                v.tensor_copy(V0[:, :, :, 0:D0].rearrange("t b h e -> t (b h) e"),
                              FB[0][:, :].rearrange("t (n e) -> t n e", e=D0)).then_inc(v_ready, 1)
                yield
                yield from maxima(0, H0)
                attended(1, H0 // 2, H0 // 2, D0, H0)
                for i in range(2):
                    dve.wait_ge(k1_psum, at(k1_psum, i + 1))
                    v.scalar_tensor_tensor(KT[:, i, :], FB[i][:, :], wp("bk1", i),
                                           MB[:].rearrange("p b t -> p (b t)"), ALU.add, ALU.mult).then_inc(k1_ready, 1)
                yield
                dve.wait_ge(v1_psum, at(v1_psum, 1))
                dve.wait_ge(mt_loaded, at(mt_loaded, 16))
                v.tensor_tensor(vtmp[:], seqs(FB[0]), MT[:].unsqueeze(2).broadcast_to([128, G, 128]), ALU.mult
                                ).then_inc(v1_part, 1)
                dve.wait_ge(v1_part, at(v1_part, 1))
                dve.wait_ge(bm_ready, at(bm_ready, 1))
                v.tensor_tensor(V1[:, :, :, 0:D1].rearrange("t b h e -> t (b h) e"),
                                vtmp[:].rearrange("t b (h e) -> t (b h) e", e=D1),
                                bm[:].rearrange("t b (h e) -> t (b h) e", e=D1), ALU.add).then_inc(v1_ready, 1)
                yield
                dve.wait_ge(att_psum, at(att_psum, 1))
                dve.wait_ge(xb_ready, at(xb_ready, 1))
                v.tensor_tensor(X1[:], seqs(FB[1]), xb[:], ALU.add).then_inc(x1_ready, 1)
                yield
                dve.wait_ge(x1_ready, at(x1_ready, 1))
                statistics(at, NF, 1, X1)
                yield
                normed(at, NF, 1, X1, XN)
                yield
                yield
                for i in range(2):
                    dve.wait_ge(q1_psum, at(q1_psum, i + 1))
                    v.scalar_tensor_tensor(QT[:, i, :], FB[i][:, :], wp("bq1", i),
                                           MB[:].rearrange("p b t -> p (b t)"), ALU.add, ALU.mult).then_inc(q1_ready, 1)
                yield
                yield from maxima(H0, H1)
                attended(3, H1 // 2, H1 // 2, D1, NJ)
                yield
                yield
                dve.wait_ge(att_psum, at(att_psum, 2))
                dve.wait_ge(xb_ready, at(xb_ready, 2))
                v.tensor_tensor(X2[:], seqs(FB[1]), X1b[:], ALU.add).then_inc(x2_ready, 1)
                yield
                dve.wait_ge(x2_ready, at(x2_ready, 1))
                statistics(at, NF, 2, X2)
                yield
                normed(at, NF, 2, X2, XL)
                yield
                yield
                dve.wait_ge(gate_psum, at(gate_psum, 1))
                link(v.tensor_tensor(lg[:], FB[0][:, 0:G * E].rearrange("t (b e) -> t b e", b=G),
                                     over_g(wr("gateb"), E), ALU.add))
                carry()
                for b in range(G):
                    ins = v.max(top[:, b, :], lg[:, b, :])
                link(ins)
                carry()
                for b in range(G):
                    ins = v.max_index(topi[:, b, :], top[:, b, :], lg[:, b, :])
                v.tensor_tensor(lsh[:], lg[:], top[:, :, 0:1].broadcast_to([128, G, E]), ALU.subtract
                                ).then_inc(lsh_ready, 1)
                link(v.tensor_tensor(l2[:], top[:, :, 1], top[:, :, 0], ALU.subtract))
                link(v.tensor_copy(topf[:], topi[:]))
                for r in range(2):
                    for b in range(G):
                        ins = v.tensor_scalar(oh[:, r, b, :], iota_row[:, 0:E], topf[:, b, r:r + 1], None, ALU.is_equal)
                ins.then_inc(oh_ready, 1)
                dve.wait_ge(l_loaded, at(l_loaded, 16))
                v.tensor_copy(lf[:], LT[:]).then_inc(lf_copied, 1)
                yield
                if not first:
                    dve.wait_ge(hs_used, prev(hs_used, NH))
                for r in range(2):
                    dve.wait_ge(oh_psum, at(oh_psum, r + 1))
                    ps = FB[[1, 3][r]][0:E, :]
                    v.tensor_copy(ohT[:, r, :], ps)
                    v.tensor_scalar(ohM[:, r, :], ps, 1.0, None, ALU.subtract).then_inc(ohm_ready, 1)
                dve.wait_ge(lex_ready, at(lex_ready, 1))
                link(v.tensor_reduce(lsum[:], lex[:], AX.X, ALU.add))
                link(v.reciprocal(gv[:, 0, :], lsum[:]))
                link(v.tensor_tensor(lsh[:], lex[:], oh[:, 1, :, :], ALU.mult))
                link(v.tensor_reduce(l2[:], lsh[:], AX.X, ALU.add))
                link(v.tensor_tensor(gv[:, 1, :], l2[:], gv[:, 0, :], ALU.mult))
                yield
                dve.wait_ge(cs_psum, at(cs_psum, 1))
                v.tensor_scalar(bi[:], FB[0][:, 0:G], 1.0, None, ALU.subtract).then_inc(bi_step, 1)
                dve.wait_ge(bi_step, at(bi_step, 1))
                v.tensor_scalar(bw[:], bi[:], 0.0, float(S), ALU.is_lt, ALU.mult).then_inc(bi_step, 1)
                dve.wait_ge(bi_step, at(bi_step, 2))
                v.tensor_tensor(bi[:], bi[:], bw[:], ALU.add).then_inc(bi_step, 1)
                dve.wait_ge(bi_step, at(bi_step, 3))
                for b in range(G):
                    ins = v.tensor_scalar(OH[:, b, :], iota_row[:], bi[:, b:b + 1], None, ALU.is_equal)
                ins.then_inc(ohj_ready, 1)
                dve.wait_ge(cr_ready, at(cr_ready, 2))
                for b in range(G):
                    ins = v.scalar_tensor_tensor(cu[:, b, :], C[:, b, 0:128], cr[:, b:b + 1], gb[:], ALU.mult, ALU.mult)
                ins.then_inc(cu_ready, 1)
                yield
                dve.wait_ge(nb_psum, at(nb_psum, 1))
                v.tensor_scalar(bnd[:], FB[0][:, 0:G].unsqueeze(2).broadcast_to([128, G, 128]), 1.0, None,
                                ALU.min).then_inc(bnd_ready, 1)
                yield
                yield
                if not first:
                    dve.wait_ge(x5_psum, prev(x5_psum, 1))
                dve.wait_ge(plug_psum, at(plug_psum, 1))
                v.tensor_scalar(sel[:], seqs(FB[2]), 1.0, iota_part1[:, 0:1], ALU.max, ALU.is_equal
                                ).then_inc(sel_ready, 1)
                yield
                assert links[0] == LINKS, links

            def back(g):
                at = counter(g)

                def weighted(r):
                    dve.wait_ge(et_psum, at(et_psum, r + 1))
                    for b in range(G):
                        ins = v.scalar_tensor_tensor(f1[:, b, :], BB[3][:, cols(b)], gv[:, r, b:b + 1],
                                                     (XL if r == 0 else f1)[:, b, :], ALU.mult, ALU.add)
                    ins.then_inc(f_ready, 1)

                for r in range(2):
                    for n in range(E * EC + 2):
                        m = r * E * EC + n
                        if n < E * EC and n % 2:
                            dve.wait_ge(h_psum, at(h_psum, m + 1))
                            if m >= 3:
                                dve.wait_ge(hs_used, at(hs_used, m - 2))
                            v.tensor_scalar(HS[:, m % 3, :], BB[m % 2][:, :], wp("b1", n), 0.0, ALU.add, ALU.max
                                            ).then_inc(h_vec, 1)
                        if r == 1 and n == 3:
                            weighted(0)
                        yield
                    if r == 0:
                        dve.wait_ge(hs_used, at(hs_used, E * EC))
                        dve.wait_ge(eo_ready, at(eo_ready, 1))
                        v.scalar_tensor_tensor(boostT[:], BB[2][:, :], 0.5, XLT[:], ALU.mult, ALU.add
                                               ).then_inc(boost_ready, 1)
                    yield
                weighted(1)
                yield
                dve.wait_ge(f_ready, at(f_ready, 2))
                statistics(at, NB, 0, f1)
                yield
                normed(at, NB, 0, f1, YN)
                dve.wait_ge(NB.xn_ready, at(NB.xn_ready, 1))
                v.tensor_tensor(f1[:], YN[:], over_g(wr("gamma")), ALU.mult).then_inc(gamma_done, 1)
                dve.wait_ge(gamma_done, at(gamma_done, 1))
                dve.wait_ge(xb_ready, at(xb_ready, 3))
                v.tensor_tensor(X3[:], f1[:], X2b[:], ALU.add).then_inc(x3_ready, 1)
                yield
                dve.wait_ge(x3_ready, at(x3_ready, 1))
                statistics(at, NB, 1, X3)
                yield
                normed(at, NB, 1, X3, YN)
                yield
                yield

                def convolve(q, k):
                    n = 128 if k < 2 else 64
                    dve.wait_ge(xp_ready, at(xp_ready, q + 1))
                    uk = u[0:n, k, :, :]
                    cw = P_AT["cw"][0] + TAPS * k
                    v.tensor_scalar(uk, xp[0:n, k, :, 0:S], WP[0:n, cw:cw + 1], wp("cb", k)[0:n], ALU.mult, ALU.add
                                    ).then_inc(conv_step, 1)
                    for i in range(1, TAPS):
                        dve.wait_ge(conv_step, at(conv_step, 4 * q + i))
                        v.scalar_tensor_tensor(uk, xp[0:n, k, :, i:i + S], WP[0:n, cw + i:cw + i + 1], uk,
                                               ALU.mult, ALU.add).then_inc(conv_step, 1)

                dve.wait_ge(dt_psum, at(dt_psum, 1))
                v.tensor_tensor(dtr[:], BB[3][:, 0:G * HM].rearrange("t (b h) -> t b h", b=G),
                                over_g(wr("dtb"), HM), ALU.add).then_inc(dt_step, 1)
                dve.wait_ge(dt_step, at(dt_step, 1))
                v.scalar_tensor_tensor(dta[:], dtr[:], -1.0, dtr[:], ALU.mult, ALU.min).then_inc(dt_step, 1)
                v.tensor_scalar(dtm[:], dtr[:], 0.0, None, ALU.max)
                convolve(0, 2)
                yield
                dve.wait_ge(dte_ready, at(dte_ready, 1))
                v.tensor_scalar(dtw[:], dte[:], 1.0, None, ALU.add).then_inc(dtw_ready, 1)
                dve.wait_ge(dtw_ready, at(dtw_ready, 1))
                v.tensor_scalar(dtd[:], dtw[:], 1.0, None, ALU.subtract).then_inc(dt_step, 1)
                dve.wait_ge(dt_step, at(dt_step, 3))
                v.tensor_scalar(dtz[:], dtd[:], 0.0, None, ALU.is_equal).then_inc(dt_step, 1)
                dve.wait_ge(dt_step, at(dt_step, 4))
                v.tensor_tensor(dtd[:], dtd[:], dtz[:], ALU.add).then_inc(dt_step, 1)
                dve.wait_ge(dt_step, at(dt_step, 5))
                v.reciprocal(dtd[:], dtd[:])
                convolve(1, 0)
                dve.wait_ge(dtl_ready, at(dtl_ready, 1))
                v.tensor_tensor(dtl[:], dtl[:], dtz[:], ALU.add).then_inc(dt_step, 1)
                dve.wait_ge(dt_step, at(dt_step, 6))
                v.tensor_tensor(dtl[:], dtl[:], dtd[:], ALU.mult).then_inc(dt_step, 1)
                dve.wait_ge(dt_step, at(dt_step, 7))
                v.tensor_tensor(dtl[:], dtl[:], dte[:], ALU.mult).then_inc(dt_step, 1)
                dve.wait_ge(dt_step, at(dt_step, 8))
                v.tensor_tensor(dt[:], dtl[:], dtm[:], ALU.add).then_inc(dt_ready, 1)
                dve.wait_ge(dt_ready, at(dt_ready, 1))
                v.tensor_tensor(dA[:], dt[:], over_g(neg_a[:, :], HM), ALU.mult).then_inc(dA_ready, 1)
                yield
                convolve(2, 1)
                for k in range(2):
                    dve.wait_ge(tz_ready, at(tz_ready, k + 1))
                    v.scalar_tensor_tensor(sz[:, 2 * k:2 * k + 2, :], tz[:, 2 * k:2 * k + 2, :], 1.0,
                                           BB[2 + k][:, :].rearrange("t (b c) -> t b c", b=2), ALU.add, ALU.mult
                                           ).then_inc(sz_ready, 1)
                dve.wait_ge(th_ready, at(th_ready, 1))
                v.scalar_tensor_tensor(Bm[:], th[0:NS, 2, :, :], 1.0, u[0:NS, 2, :, :], ALU.add, ALU.mult
                                       ).then_inc(bc_ready, 1)
                v.scalar_tensor_tensor(Cm[:], th[32:32 + NS, 2, :, :], 1.0, u[32:32 + NS, 2, :, :], ALU.add, ALU.mult
                                       ).then_inc(bc_ready, 1)
                yield
                for k in range(2):
                    dve.wait_ge(th_ready, at(th_ready, k + 2))
                    v.scalar_tensor_tensor(xs[:, k, :, :], th[:, k, :, :], 1.0, u[:, k, :, :], ALU.add, ALU.mult
                                           ).then_inc(xs_ready, 1)
                dve.wait_ge(g_psum, at(g_psum, 1))
                v.scalar_tensor_tensor(Gm[:], seqs(BB[0]), 0.25, over_g(tri[:, :]), ALU.mult, ALU.mult
                                       ).then_inc(gm_ready, 1)
                yield
                yield
                dve.wait_ge(gm_ready, at(gm_ready, 1))
                for b in range(G):
                    dve.wait_ge(ex_ready, at(ex_ready, b + 1))
                    if b >= 2:
                        dve.wait_ge(y_done, at(y_done, b - 1))
                    for h in range(HM):
                        ins = v.scalar_tensor_tensor(M[:, b % 2, h, :], EX[:, b % 2, h, :], dt[:, b, h:h + 1],
                                                     Gm[:, b, :], ALU.mult, ALU.mult)
                    ins.then_inc(m_ready, 1)
                    yield
                dve.wait_ge(xd_ready, at(xd_ready, 1))
                for k in range(2):
                    dve.wait_ge(y_done, at(y_done, 2 * k + 2))
                    v.tensor_tensor(Y[:, 2 * k:2 * k + 2, :], BB[[3, 0][k]][:, :].rearrange("t (b c) -> t b c", b=2),
                                    xd[:, 2 * k:2 * k + 2, :, :].rearrange("t b k c -> t b (k c)"), ALU.add
                                    ).then_inc(y_step, 1)
                    if k == 0:
                        yield
                dve.wait_ge(sz_ready, at(sz_ready, 2))
                for k in range(2):
                    dve.wait_ge(y_step, at(y_step, k + 1))
                    v.scalar_tensor_tensor(Yz[:, 2 * k:2 * k + 2, :], Y[:, 2 * k:2 * k + 2, :], 0.5,
                                           sz[:, 2 * k:2 * k + 2, :], ALU.mult, ALU.mult).then_inc(y_step, 1)
                yield
                yield
                dve.wait_ge(mo_psum, at(mo_psum, 1))
                dve.wait_ge(yr_ready, at(yr_ready, 2))
                for b in range(G):
                    ins = v.scalar_tensor_tensor(X4[:, b, :], BB[3][:, cols(b)], yr[:, b:b + 1],
                                                 X3[:, b, :], ALU.mult, ALU.add)
                ins.then_inc(x4_ready, 1)
                yield
                dve.wait_ge(x4_ready, at(x4_ready, 1))
                statistics(at, NB, 2, X4)
                yield
                normed(at, NB, 2, X4, YN)
                yield
                yield
                dve.wait_ge(x5_psum, at(x5_psum, 1))
                dve.wait_ge(xbb_ready, at(xbb_ready, 1))
                v.tensor_tensor(X5[:], seqs(BB[1]), X4b[:], ALU.add).then_inc(x5_ready, 1)
                yield
                dve.wait_ge(x5_ready, at(x5_ready, 1))
                statistics(at, NB, 3, X5)
                yield
                normed(at, NB, 3, X5, YN)
                yield
                yield
                dve.wait_ge(p_psum, at(p_psum, 1))
                v.tensor_copy(Pt, BB[3][0:RANK, :]).then_inc(p_ready, 1)
                yield
                yield
                yield
                dve.wait_ge(qf_psum, at(qf_psum, 1))
                v.tensor_copy(Qt, BB[3][0:RANK, :]).then_inc(qf_ready, 1)
                yield
                dve.wait_ge(x6_psum, at(x6_psum, 1))
                dve.wait_ge(xbb_ready, at(xbb_ready, 2))
                dve.wait_ge(stored, at(stored, 1))
                v.tensor_tensor(X6[:], seqs(BB[3]), X5b[:], ALU.add).then_inc(x6_ready, 1)
                yield

            run(dve, front, back)

        @block.tensor
        def _(pe):
            mm = nc.tensor.matmul
            pe.wait_ge(once, 96)
            pe.wait_ge(const_vec, 5)
            pe.wait_ge(const_pool, N_CONST)

            def turn(dst, src):
                for b in range(G):
                    ins = nc.tensor.transpose(dst[:, cols(b)], src[:, b, :], ident[:])
                return ins

            def front(g, first):
                at, prev = counter(g), counter(g - 1)

                def attention(j0, n, width, values):
                    for t in range(n + 3):
                        if t < n:
                            i, q = t // 4, Q * (t % 4)
                            dst = FB[t % 2]
                            if t >= 2:
                                pe.wait_ge(sm_ready, at(sm_ready, j0 + t - 1))
                            if n == H1:
                                mm(dst[:, :], ones_bf[q:q + 1, :], negrow[q:q + 1, :], start=True, stop=False,
                                   skip_group_check=True)
                            for b in range(G):
                                ins = mm(dst[:, cols(b)], QT[q:q + Q, i, cols(b)], KT[q:q + Q, i, cols(b)],
                                         start=n == H0, stop=True, skip_group_check=True)
                            ins.then_inc(s_psum, 1)
                        j = t - 2
                        if 0 <= j < n:
                            pe.wait_ge(sm_ready, at(sm_ready, j0 + j + 1))
                            if j >= 1:
                                pe.wait_ge(pt_ready, at(pt_ready, j0 + j))
                            for b in range(G):
                                ins = nc.tensor.transpose(FB[2][:, cols(b)], SM[:, j % 2, b, :], ident[:])
                            ins.then_inc(pt_psum, 1)
                        j = t - 3
                        if j >= 0:
                            pe.wait_ge(pt_ready, at(pt_ready, j0 + j + 1))
                            if j == n // 2:
                                pe.wait_ge(ao_ready, at(ao_ready, 1 if n == H0 else 3))
                            for b in range(G):
                                c = (b * n // 2 + j % (n // 2)) * (width + 1)
                                ins = mm(FB[3][:, c:c + width + 1], PT[:, j % 2, b, :], values[:, b, j, :],
                                         start=True, stop=True)
                            ins.then_inc(pv_done, 1)
                        yield

                pe.wait_ge(c_loaded, at(c_loaded, 16))
                for k in range(2):
                    if k == 1 and not first:
                        pe.wait_ge(dp_ready, prev(dp_ready, 1))
                    for b in range(G):
                        ins = nc.tensor.transpose(FB[k][:, cols(b)], C[:, b, 128 * k:128 * k + 128], ident[:])
                    ins.then_inc(ct_psum, 1)
                yield
                yield
                pe.wait_ge(NF.xn_ready, at(NF.xn_ready, 1))
                if not first:
                    pe.wait_ge(sel_ready, prev(sel_ready, 1))
                turn(FB[2], XN).then_inc(NF.xt_psum, 1)
                yield
                pe.wait_ge(NF.xt_ready, at(NF.xt_ready, 1))
                pe.wait_ge(ct_ready, at(ct_ready, 2))
                for i in range(4):
                    if i >= 2:
                        pe.wait_ge(q_ready, at(q_ready, i - 1))
                        pe.wait_ge(k_ready, at(k_ready, i - 1))
                    mm(FB[2 * (i % 2)][:, :], w("q0", i), XT[:], start=True, stop=True).then_inc(q_psum, 1)
                    mm(FB[2 * (i % 2) + 1][:, :], w("k0", i), XT[:], start=True, stop=True).then_inc(k_psum, 1)
                    yield
                pe.wait_ge(q_ready, at(q_ready, 3))
                for b in range(G):
                    ins = mm(FB[0][:, cols(b)], XT[:, cols(b)], w("v0"), start=True, stop=True)
                ins.then_inc(v_psum, 1)
                yield
                pe.wait_ge(q_ready, at(q_ready, 4))
                pe.wait_ge(k_ready, at(k_ready, 4))
                pe.wait_ge(v_ready, at(v_ready, 1))
                yield from attention(0, H0, D0, V0)
                for i in range(2):
                    for k in range(2):
                        ins = mm(FB[i][:, :], w("k1", 2 * i + k), CT[:, k, :], start=k == 0, stop=k == 1)
                    ins.then_inc(k1_psum, 1)
                yield
                pe.wait_ge(ao_ready, at(ao_ready, 2))
                turn(FB[2], AO).then_inc(at_psum, 1)
                pe.wait_ge(k1_ready, at(k1_ready, 1))
                for b in range(G):
                    for k in range(2):
                        ins = mm(FB[0][:, cols(b)], CT[:, k, cols(b)], w("v1", k), start=k == 0, stop=k == 1)
                ins.then_inc(v1_psum, 1)
                yield
                pe.wait_ge(at_ready, at(at_ready, 1))
                pe.wait_ge(k1_ready, at(k1_ready, 2))
                for b in range(G):
                    ins = mm(FB[1][:, cols(b)], AT[:, cols(b)], w("proj"), start=True, stop=True)
                ins.then_inc(att_psum, 1)
                yield
                yield
                yield
                pe.wait_ge(NF.xn_ready, at(NF.xn_ready, 2))
                turn(FB[2], XN).then_inc(NF.xt_psum, 1)
                yield
                pe.wait_ge(NF.xt_ready, at(NF.xt_ready, 2))
                pe.wait_ge(v1_ready, at(v1_ready, 1))
                for i in range(2):
                    mm(FB[i][:, :], w("q1", i), XT[:], start=True, stop=True).then_inc(q1_psum, 1)
                yield
                pe.wait_ge(q1_ready, at(q1_ready, 2))
                pe.wait_ge(neg_ready, at(neg_ready, 1))
                yield from attention(H0, H1, D1, V1)
                yield
                pe.wait_ge(ao_ready, at(ao_ready, 4))
                turn(FB[0], AO).then_inc(at_psum, 1)
                yield
                pe.wait_ge(at_ready, at(at_ready, 2))
                for b in range(G):
                    mm(FB[1][:, cols(b)], XT[:, cols(b)], w("out1", 0), start=True, stop=False)
                    ins = mm(FB[1][:, cols(b)], AT[:, cols(b)], w("out1", 1), start=False, stop=True)
                ins.then_inc(att_psum, 1)
                yield
                yield
                yield
                pe.wait_ge(NF.xn_ready, at(NF.xn_ready, 3))
                turn(FB[2], XL).then_inc(NF.xt_psum, 1)
                yield
                pe.wait_ge(NF.xt_ready, at(NF.xt_ready, 3))
                for b in range(G):
                    ins = mm(FB[0][:, E * b:E * b + E], XLT[:, cols(b)], w("gate"), start=True, stop=True)
                ins.then_inc(gate_psum, 1)
                yield
                pe.wait_ge(oh_ready, at(oh_ready, 1))
                for r in range(2):
                    for b in range(G):
                        ins = nc.tensor.transpose(FB[[1, 3][r]][0:E, cols(b)], oh[:, r, b, :], ident[:])
                    ins.then_inc(oh_psum, 1)
                pe.wait_ge(lf_copied, at(lf_copied, 1))
                mm(FB[0][:, 0:G], tri[:], lf[:], start=True, stop=True).then_inc(cs_psum, 1)
                yield
                yield
                pe.wait_ge(ohj_ready, at(ohj_ready, 1))
                for b in range(G):
                    ins = mm(FB[0][:, b:b + 1], OH[:, b, :], ones_bf[:, 0:1], start=True, stop=True)
                ins.then_inc(nb_psum, 1)
                yield
                pe.wait_ge(bnd_ready, at(bnd_ready, 1))
                for b in range(G):
                    ins = mm(FB[2][:, cols(b)], bnd[:, b, :], tri_bf[:], start=True, stop=True)
                ins.then_inc(plug_psum, 1)
                yield
                pe.wait_ge(cu_ready, at(cu_ready, 1))
                pe.wait_ge(ohm_ready, at(ohm_ready, 2))
                mm(FB[1][:, :], decay[:], cu[:].rearrange("q b c -> q (b c)"), start=True, stop=True
                   ).then_inc(dp_psum, 1)
                yield

            def back(g):
                at = counter(g)

                def relu_done(m):
                    s = h_vec if m % 2 else h_act
                    pe.wait_ge(s, at(s, m // 2 + 1))

                pe.wait_ge(ohm_ready, at(ohm_ready, 2))
                for r in range(2):
                    src = XLT if r == 0 else boostT
                    acc = BB[2]
                    for t in range(E * EC + 2):
                        m = r * E * EC + t
                        if t == 0:
                            if r == 1:
                                pe.wait_ge(boost_ready, at(boost_ready, 1))
                            mm(acc[:, :], B2[:], ohT[:, r, :], start=True, stop=False, skip_group_check=True)
                        if t < E * EC:
                            if m >= 2:
                                relu_done(m - 2)
                            mm(BB[m % 2][:, :], w("w1", t), src[:], start=True, stop=False, skip_group_check=True)
                            mm(BB[m % 2][:, :], big_e[:, t // EC, :], ohM[:, r, :], start=False, stop=True,
                               skip_group_check=True).then_inc(h_psum, 1)
                        if t >= 2:
                            n = t - 2
                            relu_done(m - 2)
                            mm(acc[:, :], w("w2", n), HS[:, (m - 2) % 3, :], start=False, stop=n == E * EC - 1,
                               skip_group_check=True).then_inc(hs_used, 1)
                        if r == 1 and t == 2:
                            pe.wait_ge(eo_ready, at(eo_ready, 1))
                            for b in range(G):
                                ins = nc.tensor.transpose(BB[3][:, cols(b)], eoT[:, cols(b)], ident[:])
                            ins.then_inc(et_psum, 1)
                        yield
                    yield
                pe.wait_ge(eo_ready, at(eo_ready, 2))
                pe.wait_ge(f_ready, at(f_ready, 1))
                for b in range(G):
                    ins = nc.tensor.transpose(BB[3][:, cols(b)], eoT[:, cols(b)], ident[:])
                ins.then_inc(et_psum, 1)
                yield
                yield
                yield
                yield
                yield
                pe.wait_ge(NB.xn_ready, at(NB.xn_ready, 2))
                turn(BB[3], YN).then_inc(NB.xt_psum, 1)
                yield
                pe.wait_ge(NB.xt_ready, at(NB.xt_ready, 1))
                for b in range(G):
                    ins = mm(BB[3][:, HM * b:HM * b + HM], YNT[:, cols(b)], w("dt"), start=True, stop=True)
                ins.then_inc(dt_psum, 1)
                mm(BB[2][:, :], w("bc"), YNT[:], start=True, stop=True).then_inc(xp_psum, 1)
                yield
                for k in range(2):
                    mm(BB[k][:, :], w("xs", k), YNT[:], start=True, stop=True).then_inc(xp_psum, 1)
                yield
                pe.wait_ge(xp_ready, at(xp_ready, 1))
                pe.wait_ge(dt_step, at(dt_step, 1))
                for k in range(2):
                    for b in range(2):
                        ins = mm(BB[2 + k][:, DI * b:DI * b + DI], YNT[:, cols(2 * k + b)], w("z"),
                                 start=True, stop=True)
                    ins.then_inc(z_psum, 1)
                yield
                pe.wait_ge(bc_ready, at(bc_ready, 2))
                pe.wait_ge(xp_ready, at(xp_ready, 2))
                for b in range(G):
                    ins = mm(BB[0][:, cols(b)], Bm[:, b, :], Cm[:, b, :], start=True, stop=True)
                ins.then_inc(g_psum, 1)
                yield
                pe.wait_ge(sz_ready, at(sz_ready, 1))
                pe.wait_ge(xp_ready, at(xp_ready, 3))
                for k in range(2):
                    pe.wait_ge(xs_ready, at(xs_ready, 1 + k))
                    turn(BB[1 + k], xs[:, k, :, :]).then_inc(xh_psum, 1)
                yield
                pe.wait_ge(xh_ready, at(xh_ready, 2))
                pe.wait_ge(sz_ready, at(sz_ready, 2))
                pe.wait_ge(gm_ready, at(gm_ready, 1))
                for t in range(G + 2):
                    if t < G:
                        pe.wait_ge(r_ready, at(r_ready, t + 1))
                        if t >= 2:
                            pe.wait_ge(ex_ready, at(ex_ready, t - 1))
                        mm(BB[1 + t % 2][:, :], after[:], R[:, t % 2, :, :].rearrange("u h t -> u (h t)"), start=True,
                           stop=True).then_inc(seg_psum, 1)
                    b = t - 1
                    if 0 <= b < G:
                        pe.wait_ge(m_ready, at(m_ready, b + 1))
                        for h in range(HM):
                            c = 256 * (b % 2) + HP * h
                            ins = mm(BB[[3, 0][b // 2]][:, c:c + HP], M[:, b % 2, h, :],
                                     xh[:, b, h // 2, HP * (h % 2):HP * (h % 2) + HP], start=True, stop=True)
                        ins.then_inc(y_done, 1)
                    yield
                pe.wait_ge(y_step, at(y_step, 4))
                for k in range(2):
                    turn(BB[1 + k], Yz[:, :, 128 * k:128 * k + 128]).then_inc(yt_psum, 1)
                yield
                pe.wait_ge(yt_ready, at(yt_ready, 2))
                for b in range(G):
                    for k in range(2):
                        ins = mm(BB[3][:, cols(b)], YT[:, k, cols(b)], woutn[:, k, :], start=k == 0, stop=k == 1)
                ins.then_inc(mo_psum, 1)
                yield
                yield
                yield
                pe.wait_ge(NB.xn_ready, at(NB.xn_ready, 3))
                turn(BB[0], YN).then_inc(NB.xt_psum, 1)
                yield
                pe.wait_ge(NB.xt_ready, at(NB.xt_ready, 2))
                pe.wait_ge(dp_ready, at(dp_ready, 1))
                pe.wait_ge(sel_ready, at(sel_ready, 1))
                for b in range(G):
                    mm(BB[1][:, cols(b)], YNT[:, cols(b)], winn[:], start=True, stop=False)
                    ins = mm(BB[1][:, cols(b)], sel[:, b, :], dp[:, b, :], start=False, stop=True)
                ins.then_inc(x5_psum, 1)
                yield
                yield
                yield
                pe.wait_ge(NB.xn_ready, at(NB.xn_ready, 4))
                turn(BB[2], YN).then_inc(NB.xt_psum, 1)
                yield
                pe.wait_ge(NB.xt_ready, at(NB.xt_ready, 3))
                mm(BB[3][0:RANK, :], w("u1"), YNT[:], start=True, stop=True).then_inc(p_psum, 1)
                yield
                pe.wait_ge(p_ready, at(p_ready, 1))
                for k in range(4):
                    if k == 3:
                        pe.wait_ge(hf_ready, at(hf_ready, 1))
                    mm(BB[k % 3][:, :], V1w[:, 128 * k:128 * k + 128], Pt, start=True, stop=True
                       ).then_inc(hf_psum, 1)
                    if k % 2:
                        yield
                for k in range(4):
                    pe.wait_ge(hf_ready, at(hf_ready, k + 1))
                    ins = mm(BB[3][0:RANK, :], w("u2", k, RANK), HF[:, k, :], start=k == 0, stop=k == 3)
                ins.then_inc(qf_psum, 1)
                yield
                pe.wait_ge(qf_ready, at(qf_ready, 1))
                for b in range(G):
                    ins = mm(BB[3][:, cols(b)], Qt[:, cols(b)], V2w[:], start=True, stop=True)
                ins.then_inc(x6_psum, 1)
                yield

            run(pe, front, back)


def layout(i):
    f = np.float32
    Wt = np.zeros((128, W_N), f)
    Pc = np.zeros((128, P_N), f)

    def put(name, a, k=0):
        at = W_AT[name][0] + k
        Wt[:a.shape[0], at:at + a.shape[1]] = a

    def col(name, a, k=0):
        Pc[:a.shape[0], P_AT[name][0] + k] = a

    qkv = np.zeros((128, 384), f)
    proj = np.zeros((128, 128), f)
    for n in range(8):
        qkv[16 * n:16 * n + 16, 48 * n:48 * n + 48] = i["L0_attn_w_qkv"][n]
        proj[16 * n:16 * n + 16, 16 * n:16 * n + 16] = i["L0_attn_w_proj"][n]
    for h in range(H0):
        at = 128 * (h // 4) + Q * (h % 4)
        put("q0", qkv[:, D0 * h:D0 * h + D0], at)
        put("k0", qkv[:, 128 + D0 * h:128 + D0 * h + D0], at)
    put("v0", qkv[:, 256:384])
    put("proj", proj)
    src, tgt = i["L0_xattn_W_src"].T, i["L0_xattn_W_tgt"].T
    for h in range(H1):
        n, r = h // 4, Q * (h % 4)
        mine = slice(D1 * h, D1 * h + D1)
        for k in range(2):
            put("k1", src[128 * k:128 * k + 128, mine], 128 * (2 * n + k) + r)
        put("q1", tgt[:, mine], 128 * n + r)
        Pc[r:r + D1, P_AT["bk1"][0] + n] = i["L0_xattn_b_src"][mine]
        Pc[r:r + D1, P_AT["bq1"][0] + n] = i["L0_xattn_b_tgt"][mine]
    w_out = i["L0_xattn_W_out"].T
    for k in range(2):
        put("v1", src[128 * k:128 * k + 128, 128:], 128 * k)
        put("out1", w_out[128 * k:128 * k + 128], 128 * k)
    put("gate", i["L0_ffn_gate_W"])
    for e in range(E):
        put("w1", i["L0_ffn_W1"][e], HID * e)
        for c in range(EC):
            put("w2", i["L0_ffn_W2"][e, 128 * c:128 * c + 128], 128 * (EC * e + c))
            col("b1", i["L0_ffn_b1"][e, 128 * c:128 * c + 128], EC * e + c)
    m_in = i["L1_attn_W_in"].T
    put("z", m_in[:, 0:DI])
    put("xs", m_in[:, DI:2 * DI])
    put("bc", m_in[:, 2 * DI:2 * DI + NS], 0)
    put("bc", m_in[:, 2 * DI + NS:2 * DI + 2 * NS], 32)
    put("dt", m_in[:, 2 * DI + 2 * NS:])
    cw, cb = i["L1_attn_conv_w"], i["L1_attn_conv_b"]
    for k, (rows, at) in enumerate([(slice(0, 128), 0), (slice(128, 256), 0), (slice(256, 272), 0)]):
        n = rows.stop - rows.start
        c = P_AT["cw"][0] + TAPS * k
        Pc[at:at + n, c:c + TAPS] = cw[rows]
        Pc[at:at + n, P_AT["cb"][0] + k] = cb[rows]
    c = P_AT["cw"][0] + TAPS * 2
    Pc[32:32 + NS, c:c + TAPS] = cw[272:288]
    Pc[32:32 + NS, P_AT["cb"][0] + 2] = cb[272:288]
    m_out = i["L1_attn_W_out"].T
    for k in range(2):
        put("mout", m_out[128 * k:128 * k + 128], 128 * k)
        col("normw", i["L1_attn_norm_w"][128 * k:128 * k + 128], k)
    put("win", i["L1_xattn_W_in"].T)
    col("gres", i["L1_xattn_g_res"])
    put("u1", i["L1_ffn_U1"])
    for k in range(4):
        put("u2", i["L1_ffn_U2"][128 * k:128 * k + 128], RANK * k)
        col("bff1", i["L1_ffn_b1"][128 * k:128 * k + 128], k)
    rows = [i["L0_attn_b_proj"], i["L0_xattn_b_src"][128:], i["L0_xattn_b_out"], i["L0_ffn_gate_b"],
            i["L0_ffn_ln_gamma"], i["L0_ffn_ln_beta"], i["L1_attn_dt_bias"], i["L1_attn_A_log"], i["L1_attn_D"],
            i["L1_xattn_b_in"], i["L1_xattn_g_init"][:128], i["L1_ffn_b2"]]
    Rr = np.ascontiguousarray(np.broadcast_to(np.concatenate(rows), (128, R_N)))
    return Wt, Pc, Rr, i["L0_ffn_b2"], i["L1_ffn_V1"], i["L1_ffn_V2"]


def kernel(**inputs):
    import concourse.bacc as bacc
    from concourse.bass_utils import run_bass_kernel_spmd

    i = {k: np.asarray(a) for k, a in inputs.items()}
    arrays = [i["x"], i["ctx_2048"], i["mask_BxS2_fk1"], i["mask_BxS2_fk1"].T, i["mask_BxS2_if0"].T, *layout(i)]
    names = ["x", "ctx", "mask", "mask_t", "lens_t", "w", "wp", "wr", "b2", "v1", "v2"]
    nc = bacc.Bacc("TRN2", target_bir_lowering=False, num_devices=1)
    feed, args = {}, []
    for name, a in zip(names, arrays):
        a = np.ascontiguousarray(a)
        feed[f"in_{name}"] = a
        args.append(nc.dram_tensor(f"in_{name}", a.shape, mybir.dt.from_np(a.dtype), kind="ExternalInput").ap())
    args.append(nc.dram_tensor("out", (B, S, D), F32, kind="ExternalOutput").ap())
    build(nc, *args)
    r = run_bass_kernel_spmd(nc, [feed], core_ids=[0])
    return r.results[0]["out"]
```

```python
from contextlib import ExitStack

import numpy as np

import concourse.bass as bass
from concourse import mybir

F32 = mybir.dt.float32
BF16 = mybir.dt.bfloat16
I32 = mybir.dt.int32
U32 = mybir.dt.uint32
ACT = mybir.ActivationFunctionType
ALU = mybir.AluOpType
AX = mybir.AxisListType

B, S, D, DC = 32, 128, 128, 256
G = 4
NG = B // G
GT = G * S
TERMS = [(0, 0), (0, 1), (1, 0), (1, 1), (0, 2), (2, 0)]
NT = len(TERMS)
H0, D0 = 16, 8
H1, D1 = 8, 16
E, HID = 8, 256
EC = HID // 128
DI, NS, HM, HP = 256, 16, 4, 64
TAPS = 4
FF, RANK = 512, 32
LN_EPS = 1e-5
PATCH_EPS = 1e-3
N_EARLY, N_FRONT, N_CONST = 4, 16, 21
FRONT_STAGES, BACK_STAGES = 56, 71
BACK_BEFORE = {
    "PE": [0, 1, 1, 1, 3, 0, 10, 4, 0, 0, 2, 0, 0, 0, 0, 0, 0, 3, 1, 0, 2, 3, 0, 2, 0, 0, 1, 1, 1, 3, 1, 0, 0, 0,
           0, 0, 3, 5, 0, 1, 0, 7, 2, 1, 1, 0, 2, 0, 2, 0, 2, 1, 0, 2, 0, 0, 2],
    "ACT": [0, 2, 1, 0, 5, 9, 0, 0, 0, 1, 0, 0, 2, 0, 2, 0, 0, 3, 2, 0, 1, 2, 0, 1, 0, 3, 1, 3, 0, 0, 1, 1, 0, 0,
            4, 0, 1, 3, 0, 1, 7, 1, 1, 1, 1, 0, 3, 0, 1, 0, 2, 0, 0, 2, 2, 0, 1],
    "DVE": [2, 0, 0, 1, 0, 8, 0, 6, 1, 0, 0, 1, 1, 0, 0, 0, 2, 0, 4, 0, 2, 3, 0, 2, 0, 0, 1, 1, 1, 3, 0, 1, 0, 0,
            2, 1, 2, 3, 0, 1, 0, 3, 4, 2, 2, 1, 1, 0, 2, 0, 2, 3, 0, 0, 2, 0, 0],
    "Pool": [1, 1, 1, 0, 0, 2, 10, 4, 0, 0, 2, 0, 0, 0, 1, 0, 0, 4, 4, 0, 0, 0, 1, 0, 2, 0, 1, 1, 1, 0, 0, 0, 0, 4,
             2, 1, 0, 1, 1, 5, 0, 10, 0, 0, 0, 0, 0, 1, 2, 1, 0, 2, 5, 0, 0, 0, 0],
}
assert all(len(n) == FRONT_STAGES + 1 and sum(n) == BACK_STAGES for n in BACK_BEFORE.values())
SB = 128
NBLK = GT // SB + E - 1
RING = 5
PIECES = [(0, 4), (4, 8), (8, NBLK)]
BIG = 1e30
T_W1, T_B1, T_B2 = 0, HID, HID + EC
T_N = T_B2 + 128

W_COLS = [("q0", 128), ("k0", 128), ("v0", 128), ("proj", 128),
          ("k1", 2 * 2 * 128), ("v1", 2 * 128), ("q1", 128), ("out1", 2 * 128), ("gate", E),
          ("w2", E * EC * 128), ("z", DI), ("xs", DI), ("bc", 128), ("dt", HM),
          ("mout", 2 * 128), ("win", 128), ("u1", RANK), ("u2", 4 * RANK)]
P_COLS = [("bk1", 2), ("bq1", 1), ("cw", 3 * TAPS), ("cb", 3), ("bff1", 4),
          ("normw", 2), ("gres", 1)]
R_COLS = [("bproj", 128), ("bv1", 128), ("bout", 128), ("gateb", E), ("gamma", 128), ("beta", 128),
          ("dtb", HM), ("alog", HM), ("dskip", HM), ("bin", 128), ("ginit", 128), ("bff2", 128)]


def places(cols):
    at, out = 0, {}
    for name, n in cols:
        out[name] = (at, at + n)
        at += n
    return out, at


W_AT, W_N = places(W_COLS)
P_AT, P_N = places(P_COLS)
R_AT, R_N = places(R_COLS)


def build(nc, x, ctx_in, mask, m_t, l_t, w_in, w_p, w_r, w_experts, w_v1, w_v2, out):
    x_t = x.rearrange("b t d -> t b d")
    c_t = ctx_in.rearrange("b t d -> t b d")
    o_t = out.rearrange("b t d -> t b d")

    slots_x = nc.dram_tensor("slots_x", (NBLK * SB, D), F32).ap()
    slots_y = nc.dram_tensor("slots_y", (NBLK * SB, D), F32).ap()

    parts_out = nc.dram_tensor("parts_out", (2, 3, 128, GT), BF16).ap()

    stack = ExitStack()
    with stack:
        def sb(name, shape, dt=F32):
            return stack.enter_context(nc.sbuf_tensor(name, shape, dt))

        by_sem = []

        def sem(name, n=1):
            s = stack.enter_context(nc.semaphore(name))
            by_sem.append((s, n))
            return s

        def counter(g):
            def at(s, c):
                n = [k for t, k in by_sem if t is s][0]
                return g * n + c
            return at

        bank = [stack.enter_context(nc.psum_tensor(f"bank{i}", [128, 512], F32)) for i in range(8)]
        FB, BB = bank[0:4], bank[4:8]

        def seqs(b):
            return b[:, :].rearrange("p (b c) -> p b c", b=G)

        def cols(b):
            return slice(128 * b, 128 * b + 128)

        W = sb("W", [128, W_N])
        WP = sb("WP", [128, P_N])
        WR = sb("WR", [128, R_N])
        V1w = sb("V1w", [RANK, FF])
        V2w = sb("V2w", [RANK, 128])
        ident = sb("ident", [128, 128])
        tri = sb("tri", [128, 128])
        after = sb("after", [128, 128])
        tri_bf = sb("tri_bf", [128, 128], BF16)
        decay = sb("decay", [128, 128])
        ones_bf = sb("ones_bf", [128, 128], BF16)
        iota_row = sb("iota_row", [128, 128])
        iota_part1 = sb("iota_part1", [128, 1])
        ones_f = sb("ones_f", [128, 128])
        below = sb("below", [128, E, E])
        filled = sb("filled", [128, GT // SB])
        carry_at = sb("carry_at", [1, 32])
        halfneg = sb("halfneg", [128, 16])
        eps = sb("eps", [128, 16])
        mark = sb("mark", [1, 32])
        neg_a = sb("neg_a", [128, HM])
        gb = sb("gb", [128, 128])
        woutn = sb("woutn", [128, 2, 128])
        winn = sb("winn", [128, 128])

        def w(name, k=None, n=128):
            a, b = W_AT[name]
            return W[:, a:b] if k is None else W[:, a + k * n:a + (k + 1) * n]

        def wp(name, k=0):
            return WP[:, P_AT[name][0] + k:P_AT[name][0] + k + 1]

        def wr(name):
            return WR[:, R_AT[name][0]:R_AT[name][1]]

        def over_g(row, n=128):
            return row.unsqueeze(1).broadcast_to([128, G, n])

        X = sb("X", [128, G, D])
        C = sb("C", [128, G, DC])
        MT = sb("MT", [128, G])
        LT = sb("LT", [128, G], I32)
        MB = sb("MB", [128, G, 128])
        negrow = sb("negrow", [128, GT], BF16)
        xb = sb("xb", [128, G, D])
        XN = sb("XN", [128, G, D])
        XT = sb("XT", [128, GT])
        PA = sb("PA", [128, 3, GT])
        parts = PA[:].bitcast(BF16).rearrange("p a (u n) -> p (a u) n", u=2).rearrange("p (o k) n -> p o k n", k=3)
        qf = sb("qf", [128, 4, GT])
        kf = sb("kf", [128, 4, GT])
        QP, KP = (a[:].bitcast(BF16).rearrange("p a (u n) -> p (a u) n", u=2) for a in (qf, kf))
        QT, KT = qf[:, 0, :], kf[:, 0:2, :]
        PT = PA[:, 0:2, :].rearrange("p j (b t) -> p j b t", b=G)
        AO = PA[:, 2, :].rearrange("p (b c) -> p b c", b=G)
        V0 = sb("V0", [128, G, H0, D0 + 1])
        V1 = sb("V1", [128, G, H1, D1 + 1])
        mx = sb("mx", [128, 16, 4])
        SM = sb("SM", [128, 2, 4, 128])
        rest = SM[:].rearrange("p a b c -> p (a b c)").rearrange("p (k n) -> p k n", k=2)
        rs = sb("rs", [128, G, 8])
        AT = sb("AT", [128, GT])
        CT = sb("CT", [128, 2, GT])
        bm = sb("bm", [128, G, 128])
        vtmp = sb("vtmp", [128, G, 128])
        cu = vtmp
        X1 = sb("X1", [128, G, D])
        X1b = sb("X1b", [128, G, D])
        X2 = X1
        lg = sb("lg", [128, G, E])
        top = sb("top", [128, G, 8])
        topi = sb("topi", [128, G, 8], U32)
        topf = sb("topf", [128, G, 8])
        lsh = sb("lsh", [128, G, E])
        lex = sb("lex", [128, G, E])
        lsum = sb("lsum", [128, G])
        l2 = sb("l2", [128, G])
        oh = sb("oh", [128, 2, G, E])
        ne = sb("ne", [128, 2, E])
        full = sb("full", [128, 2, E, GT // SB])
        nblk = sb("nblk", [128, 2, E])
        endm = sb("endm", [128, 2, E, E])
        endb = sb("endb", [128, 2, E])
        start = sb("start", [128, 2, G, E])
        at_e = sb("at_e", [128, 2, G, E])
        slot = sb("slot", [128, 2, G])
        le = sb("le", [128, 2, NBLK, E])
        eb = sb("eb", [128, 2, NBLK])
        lf = sb("lf", [128, G])
        bi = sb("bi", [128, G])
        bw = sb("bw", [128, G])
        OH = sb("OH", [128, G, 128], BF16)
        bnd = sb("bnd", [128, G, 128], BF16)
        csq = SM[:].rearrange("p a b c -> p (a b) c").rearrange("p (b k) c -> p b (k c)", k=2)
        css = sb("css", [128, G])
        cr = sb("cr", [128, G])
        XL = sb("XL", [128, G, D])
        XLT = XT
        X2b = sb("X2b", [128, G, D])
        gv = sb("gv", [128, 2, G])
        pos = sb("pos", [128, 2, G], U32)
        rows = sb("rows", [128, 2, NBLK], U32)
        place = sb("place", [128, 2, NBLK], U32)
        sel = sb("sel", [128, G, 128])
        dp = sb("dp", [128, G, 128])
        wt = sb("wt", [128, RING, T_N])
        xg = sb("xg", [128, NBLK, D])
        xgT = sb("xgT", [128, NBLK, SB])
        HS = sb("HS", [128, 3, EC, SB])
        yo = xg
        eo = sb("eo", [128, G, D])
        boost = sb("boost", [128, G, D])
        f1 = sb("f1", [128, G, D])
        YN = sb("YN", [128, G, D])
        YNT = sb("YNT", [128, GT])
        X3 = sb("X3", [128, G, D])
        xp = sb("xp", [128, 3, G, S + TAPS - 1])
        u = sb("u", [128, 3, G, S])
        th = sb("th", [128, 3, G, S])
        xs = sb("xs", [128, 2, G, S])
        Bm = sb("Bm", [NS, G, S])
        Cm = sb("Cm", [NS, G, S])
        xh = sb("xh", [128, G, 2, 128])
        xd = sb("xd", [128, G, 2, 128])
        tz = sb("tz", [128, G, DI])
        sz = sb("sz", [128, G, DI])
        dtr, dta, dte, dtw, dtl, dtd, dtz, dtm, dt, dA = (
            sb(n, [128, G, HM]) for n in ("dtr", "dta", "dte", "dtw", "dtl", "dtd", "dtz", "dtm", "dt", "dA"))
        RE = sb("RE", [128, 4, GT])
        R = RE[:, 0:2, :].rearrange("p b (h t) -> p b h t", h=HM)
        EX = RE[:, 2:4, :].rearrange("p b (h t) -> p b h t", h=HM)
        HF = RE
        Gm = sb("Gm", [128, G, 128])
        M = sb("M", [128, 2, HM, 128])
        ones, base = M[:, 0, 0, :], M[:, 0, 1, :]
        Y = u[:, 0:2, :, :].rearrange("p k b t -> p (k b t)").rearrange("p (b c) -> p b c", c=DI)
        Yz = tz
        ysq = Y
        yss = sb("yss", [128, G])
        yr = sb("yr", [128, G])
        YT = th[:, 0:2, :, :].rearrange("p k b t -> p k (b t)")
        X4 = f1
        X4b = sb("X4b", [128, G, D])
        q6 = sb("q6", [128, G])
        X5 = X3
        X5b = X4b
        Pt = YNT[0:RANK, :]
        Qt = boost[0:RANK, :, :].rearrange("r b t -> r (b t)")
        X6 = sb("X6", [128, G, D])

        early = stack.enter_context(nc.semaphore("first_weights_loaded"))
        once = stack.enter_context(nc.semaphore("weights_loaded"))
        slots_zeroed = stack.enter_context(nc.semaphore("slots_zeroed"))
        const_pool = stack.enter_context(nc.semaphore("pool_constants"))
        const_vec = stack.enter_context(nc.semaphore("vector_constants"))
        const_act = stack.enter_context(nc.semaphore("scalar_constants"))
        x_loaded, c_loaded, m_loaded, l_loaded, mt_loaded, stored = (
            sem(n, 16) for n in ("x_loaded", "c_loaded", "m_loaded", "l_loaded", "mt_loaded", "stored"))

        class Norms:

            def __init__(self, part, n):
                self.bst = sb(part + "_bst", [128, G, 6])
                self.mv = sb(part + "_mv", [128, G, 2])
                self.ve = sb(part + "_ve", [128, G])
                self.rstd = sb(part + "_rstd", [128, G])
                self.bn_done = sem(part + "_bn_done", n * G)
                self.mv_ready = sem(part + "_mv_ready", n * G)
                self.ve_ready = sem(part + "_ve_ready", n)
                self.rstd_ready = sem(part + "_rstd_ready", n)
                self.xn_ready = sem(part + "_xn_ready", n)
                self.xt_psum = sem(part + "_xt_psum", 3)
                self.xt_ready = sem(part + "_xt_ready", 3)

        NF, NB = Norms("front", 3), Norms("back", 4)
        xb_ready, xbb_ready = sem("xb_ready", 3), sem("xbb_ready", 2)
        q_psum = sem("q_psum", 2)
        part0_ready, rest_ready, part1_ready, parts_ready = (
            sem(n, 2) for n in ("part0_ready", "rest_ready", "part1_ready", "parts_ready"))
        parts_stored = [sem(f"parts_stored{k}", 16) for k in range(2)]
        terms_loaded = sem("terms_loaded", 2 * 2 * NT * 16)
        v_psum, v_ready = sem("v_psum"), sem("v_ready")
        NJ = H0 + H1
        s_psum, max_ready, sm_ready, pt_psum, pt_ready, pv_done = (
            sem(n, NJ) for n in ("s_psum", "max_ready", "sm_ready", "pt_psum", "pt_ready", "pv_done"))
        rs_ready, ao_ready = sem("rs_ready", 4), sem("ao_ready", 4)
        at_psum, at_ready, att_psum = sem("at_psum", 2), sem("at_ready", 2), sem("att_psum", 2)
        x1_ready, x2_ready = sem("x1_ready"), sem("x2_ready")
        ct_psum, ct_ready = sem("ct_psum", 2), sem("ct_ready", 2)
        neg_ready, bm_ready = sem("neg_ready"), sem("bm_ready")
        k1_psum, k1_ready, q1_psum, q1_ready = sem("k1_psum", 2), sem("k1_ready", 2), sem("q1_psum"), sem("q1_ready")
        v1_psum, v1_part, v1_ready = sem("v1_psum"), sem("v1_part"), sem("v1_ready")
        gate_psum, lsh_ready, lex_ready, oh_ready = (
            sem(n) for n in ("gate_psum", "lsh_ready", "lex_ready", "oh_ready"))
        pos_ready, rows_ready, place_ready = sem("pos_ready"), sem("rows_ready"), sem("place_ready")
        lf_copied, bi_step, ohj_ready, cs_psum, nb_psum, bnd_ready, plug_psum, sel_ready = (
            sem(n, k) for n, k in (("lf_copied", 1), ("bi_step", 3), ("ohj_ready", 1), ("cs_psum", 1),
                                   ("nb_psum", 1), ("bnd_ready", 1), ("plug_psum", 1), ("sel_ready", 1)))
        css_ready, cr_ready, cu_ready, dp_psum, dp_ready = (
            sem(n, k) for n, k in (("css_ready", G), ("cr_ready", 2), ("cu_ready", 1), ("dp_psum", 1), ("dp_ready", 1)))
        LINKS = 25
        link_sem = sem("gate_link", LINKS)

        x_scattered, y_stored, eo_loaded = sem("x_scattered", 2 * G * 16), sem("y_stored", 2 * 3 * 16), sem("eo_loaded", 2 * G * 16)
        xg_loaded = [sem(f"xg_loaded{k}", 2 * 16) for k in range(3)]
        w_loaded = [sem(f"w_loaded{k}", 16 * len(range(k, 2 * NBLK, RING))) for k in range(RING)]
        xg_psum, xg_ready = sem("xg_psum", 6), sem("xg_ready", 6)
        NE, NO = 2 * ((NBLK + 1) // 2), 2 * (NBLK // 2)
        h_psum, h_act, h_vec, y_psum, yo_ready = (
            sem("h_psum", 2 * NBLK), sem("h_act", NE), sem("h_vec", NO), sem("y_psum", 2 * NBLK), sem("yo_ready", 2 * NBLK))
        boost_ready, f_ready = sem("boost_ready"), sem("f_ready", 2)
        gamma_done, x3_ready = sem("gamma_done"), sem("x3_ready")
        z_psum, xp_psum, xp_ready, dt_psum = sem("z_psum", 2), sem("xp_psum", 3), sem("xp_ready", 3), sem("dt_psum")
        tz_ready, sz_ready = sem("tz_ready", 2), sem("sz_ready", 2)
        conv_step, th_ready, bc_ready, xs_ready = sem("conv_step", 12), sem("th_ready", 3), sem("bc_ready", 2), sem("xs_ready", 2)
        xh_psum, xh_ready, xd_ready = sem("xh_psum", 2), sem("xh_ready", 2), sem("xd_ready")
        dt_step, dte_ready, dtw_ready, dtl_ready, dt_ready = (
            sem("dt_step", 8), sem("dte_ready"), sem("dtw_ready"), sem("dtl_ready"), sem("dt_ready"))
        dA_ready, r_ready, seg_psum, ex_ready = sem("dA_ready"), sem("r_ready", G), sem("seg_psum", G), sem("ex_ready", G)
        g_psum, gm_ready, m_ready, y_done = sem("g_psum"), sem("gm_ready"), sem("m_ready", G), sem("y_done", G)
        y_step, yss_ready, yr_ready, yt_psum, yt_ready = (
            sem("y_step", 4), sem("yss_ready", G), sem("yr_ready", 2), sem("yt_psum", 2), sem("yt_ready", 2))
        mo_psum, x4_ready = sem("mo_psum"), sem("x4_ready")
        r6_step = sem("r6_step", 3)
        x5_psum, x5_ready = sem("x5_psum"), sem("x5_ready")
        p_psum, p_ready, hf_psum, hf_ready = sem("p_psum"), sem("p_ready"), sem("hf_psum", 4), sem("hf_ready", 4)
        qf_psum, qf_ready, x6_psum, x6_ready = sem("qf_psum"), sem("qf_ready"), sem("x6_psum"), sem("x6_ready")

        def woven(front, back, g, back_before):
            ahead, behind = front(g, False), back(g - 1)
            for n in range(FRONT_STAGES + 1):
                for _ in range(back_before[n]):
                    next(behind)
                if n < FRONT_STAGES:
                    next(ahead)
            assert next(ahead, None) is None and next(behind, None) is None

        def alone(stages, n):
            m = sum(1 for _ in stages)
            assert m == n, (m, n)

        def run(engine, name, front, back):
            alone(front(0, True), FRONT_STAGES)
            with engine.Fori(1, NG) as g:
                woven(front, back, g, BACK_BEFORE[name])
            alone(back(NG - 1), BACK_STAGES)

        block = stack.enter_context(nc.Block())

        @block.sync
        def _(sp):
            sp.sem_inc(stored, 1)

            def load_x(g):
                sp.dma_start(X[:], x_t[:, bass.ds(g * G, G), :]).then_inc(x_loaded, 16)

            def load_rest(g):
                sp.dma_start(C[:], c_t[:, bass.ds(g * G, G), :]).then_inc(c_loaded, 16)
                sp.dma_start(MT[:], m_t[:, bass.ds(g * G, G)]).then_inc(mt_loaded, 16)
                sp.dma_start(MB[:], mask[bass.ds(g * G, G), :].unsqueeze(0).broadcast_to([128, G, S])
                             ).then_inc(m_loaded, 16)
                sp.dma_start(LT[:], l_t[:, bass.ds(g * G, G)]).then_inc(l_loaded, 16)

            def spread(g):
                at = counter(g)
                for operand in range(2):
                    sp.wait_ge(parts_ready, at(parts_ready, operand + 1))
                    sp.dma_start(parts_out[operand].rearrange("k p n -> p k n"), parts[:, operand, :, :]
                                 ).then_inc(parts_stored[operand], 16)
                for operand in range(2):
                    sp.wait_ge(parts_stored[operand], at(parts_stored[operand], 16))
                    for i, term in enumerate(TERMS):
                        src = parts_out[operand, term[operand]].rearrange("(c a d) n -> a d c n", a=2, d=D0)
                        for a in range(2):
                            row = 64 * a + D0 * i
                            sp.dma_start([QP, KP][operand][row:row + D0, :, :], src[a]).then_inc(terms_loaded, 16)

            def load_slots(g, r):
                sp.wait_ge(x_scattered, counter(g)(x_scattered, G * 16 * (r + 1)))
                for k, (a, b) in enumerate(PIECES):
                    sp.dma_start(xg[:, a:b, :], slots_x[SB * a:SB * b, :].rearrange("(j p) d -> p j d", p=SB)
                                 ).then_inc(xg_loaded[k], 16)

            def store_slots(g, r):
                for a, b in PIECES:
                    sp.wait_ge(yo_ready, counter(g)(yo_ready, r * NBLK + b))
                    sp.dma_start(slots_y[SB * a:SB * b, :].rearrange("(j p) d -> p j d", p=SB), yo[:, a:b, :]
                                 ).then_inc(y_stored, 16)

            def group(g, last, first=False):
                at = counter(g)
                if not first:
                    load_slots(g - 1, 0)
                if not last:
                    sp.wait_ge(NF.xn_ready, at(NF.xn_ready, 1))
                    sp.wait_ge(xb_ready, at(xb_ready, 1))
                    load_x(g + 1)
                spread(g)
                if not first:
                    store_slots(g - 1, 0)
                    load_slots(g - 1, 1)
                    store_slots(g - 1, 1)
                if not last:
                    sp.wait_ge(cu_ready, at(cu_ready, 1))
                    load_rest(g + 1)
                if not first:
                    store(g - 1)

            def store(g):
                sp.wait_ge(x6_ready, counter(g)(x6_ready, 1))
                sp.dma_start(o_t[:, bass.ds(g * G, G), :], X6[:]).then_inc(stored, 16)

            load_x(0)
            first = W_AT["k1"][0]
            for dst, src in ((W[:, 0:first], w_in[:, 0:first]), (WP[:], w_p), (WR[:], w_r)):
                sp.dma_start(dst, src).then_inc(early, 16)
            load_rest(0)
            for dst, src in ((W[:, first:], w_in[:, first:]), (V1w[:], w_v1), (V2w[:], w_v2)):
                sp.dma_start(dst, src).then_inc(once, 16)
            group(0, False, first=True)
            with sp.Fori(1, NG - 1) as g:
                group(g, False)
            group(NG - 1, True)
            for r in range(2):
                load_slots(NG - 1, r)
                store_slots(NG - 1, r)
            store(NG - 1)
            sp.wait_ge(stored, 16 * NG + 1)

        @block.gpsimd
        def _(pool):
            pg = nc.gpsimd
            nconst = [0]

            def const(ins):
                nconst[0] += 1
                ins.then_inc(const_pool, 1)
                pool.wait_ge(const_pool, nconst[0])

            const(pg.memset(ones, 1.0))
            const(pg.affine_select(out=ident[:], in_=ones, pattern=[[1, 128]], compare_op=ALU.is_equal,
                                   fill=0.0, base=0, channel_multiplier=-1))
            const(pg.memset(halfneg[:], -0.5))
            const(pg.memset(eps[:], LN_EPS))
            assert nconst[0] == N_EARLY
            pool.wait_ge(early, 48)

            def constants():
                const(pg.memset(ones_bf[:], 1.0))
                const(pg.memset(ones_f[:], 1.0))
                for out_, step, sign, op in ((tri, 1, -1, ALU.is_ge), (tri_bf, 1, -1, ALU.is_ge), (after, -1, 1, ALU.is_gt)):
                    const(pg.affine_select(out=out_[:], in_=ones_f[:], pattern=[[step, 128]], compare_op=op,
                                           fill=0.0, base=0, channel_multiplier=sign))
                const(pg.iota(iota_row[:], pattern=[[1, 128]], base=0, channel_multiplier=0,
                              allow_small_or_imprecise_dtypes=True))
                const(pg.iota(iota_part1[:], pattern=[[0, 1]], base=1, channel_multiplier=1,
                              allow_small_or_imprecise_dtypes=True))
                const(pg.memset(below[:], 1.0))
                const(pg.affine_select(out=below[:], in_=below[:], pattern=[[1, E], [-1, E]], compare_op=ALU.is_ge,
                                       fill=0.0, base=0, channel_multiplier=0))
                const(pg.iota(filled[:], pattern=[[SB, GT // SB]], base=0, channel_multiplier=0,
                              allow_small_or_imprecise_dtypes=True))
                const(pg.memset(xg[:], 0.0))
                pg.dma_start(slots_x.rearrange("(j p) d -> p j d", p=SB), xg[:]).then_inc(slots_zeroed, 16)
                pg.memset(V0[:], 1.0)
                pg.memset(V1[:], 1.0)
                const(pg.memset(xp[:], 0.0))
                assert nconst[0] == N_FRONT
                const(pg.iota(base, pattern=[[1, 128]], base=0, channel_multiplier=-1,
                              allow_small_or_imprecise_dtypes=True))
                const(pg.tensor_scalar(base, base, 0.0, None, ALU.max))
                const(pg.memset(decay[:], float(-np.expm1(-PATCH_EPS))))
                const(pg.tensor_tensor(base, decay[:], base, ALU.pow))
                const(pg.affine_select(out=decay[:], in_=base, pattern=[[1, 128]], compare_op=ALU.is_ge,
                                       fill=0.0, base=0, channel_multiplier=-1))
                assert nconst[0] == N_CONST
                pool.wait_ge(slots_zeroed, 16)

            carried = [0]

            def carry():
                k = carried[0] % 32
                carried[0] += 1
                pg.tensor_tensor(carry_at[:, k:k + 1], eps[0:1, 0:1], eps[0:1, 0:1], ALU.add)

            def weights(at, m):
                r, j = m // NBLK, m % NBLK
                pg.indirect_dma_start(wt[:, m % RING, :], None, w_experts,
                                      bass.IndirectOffsetOnAxis(ap=rows[:, r, j:j + 1], axis=0)
                                      ).then_inc(w_loaded[m % RING], 16)

            def scatter(r, src):
                for b in range(G):
                    pg.indirect_dma_start(slots_x, bass.IndirectOffsetOnAxis(ap=pos[:, r, b:b + 1], axis=0),
                                          src[:, b, :], None).then_inc(x_scattered, 16)

            def inverse_std(at, N, k):
                pool.wait_ge(N.ve_ready, at(N.ve_ready, k + 1))
                pg.tensor_tensor(N.rstd[:], N.ve[:], halfneg[:, 0:G], ALU.pow).then_inc(N.rstd_ready, 1)

            def front(g, first):
                at, prev = counter(g), counter(g - 1)
                pool.wait_ge(x_loaded, at(x_loaded, 16))
                pg.tensor_tensor(xb[:], X[:], over_g(wr("bproj")), ALU.add).then_inc(xb_ready, 1)
                inverse_std(at, NF, 0)
                if first:
                    constants()
                yield
                pool.wait_ge(mt_loaded, at(mt_loaded, 16))
                pg.tensor_tensor(bm[:], over_g(wr("bv1")), MT[:].unsqueeze(2).broadcast_to([128, G, 128]), ALU.mult
                                 ).then_inc(bm_ready, 1)
                pool.wait_ge(css_ready, at(css_ready, G))
                pg.tensor_tensor(cr[:], css[:], eps[:, 0:G], ALU.add).then_inc(cr_ready, 1)
                pool.wait_ge(cr_ready, at(cr_ready, 1))
                pg.tensor_tensor(cr[:], cr[:], halfneg[:, 0:G], ALU.pow).then_inc(cr_ready, 1)
                for _ in range(29):
                    yield
                pool.wait_ge(x1_ready, at(x1_ready, 1))
                inverse_std(at, NF, 1)
                pg.tensor_tensor(X1b[:], X1[:], over_g(wr("bout")), ALU.add).then_inc(xb_ready, 1)
                for _ in range(17):
                    yield
                pool.wait_ge(x2_ready, at(x2_ready, 1))
                inverse_std(at, NF, 2)
                if not first:
                    pool.wait_ge(x3_ready, prev(x3_ready, 1))
                pg.tensor_tensor(X2b[:], X2[:], over_g(wr("beta")), ALU.add).then_inc(xb_ready, 1)
                for _ in range(6):
                    yield
                pool.wait_ge(NF.xn_ready, at(NF.xn_ready, 3))
                carry()
                pool.wait_ge(pos_ready, at(pos_ready, 1))
                carry()
                if not first:
                    for k in range(3):
                        pool.wait_ge(xg_loaded[k], prev(xg_loaded[k], 32))
                        carry()
                    pool.wait_ge(yo_ready, prev(yo_ready, 2 * NBLK))
                    carry()
                scatter(0, XL)
                pool.wait_ge(rows_ready, at(rows_ready, 1))
                carry()
                for m in range(RING):
                    weights(at, m)
                for _ in range(FRONT_STAGES - 53):
                    yield

            def back(g):
                at = counter(g)
                for r in range(2):
                    for _ in range(6):
                        yield
                    for j in range(NBLK):
                        m = r * NBLK + j + RING
                        if m < 2 * NBLK:
                            pool.wait_ge(yo_ready, at(yo_ready, m - RING + 1))
                            carry()
                            weights(at, m)
                        if j < NBLK - 1:
                            yield
                    pool.wait_ge(y_stored, at(y_stored, 48 * (r + 1)))
                    carry()
                    if r == 1:
                        pool.wait_ge(f_ready, at(f_ready, 1))
                        carry()
                    for b in range(G):
                        pg.indirect_dma_start(eo[:, b, :], None, slots_y,
                                              bass.IndirectOffsetOnAxis(ap=pos[:, r, b:b + 1], axis=0)
                                              ).then_inc(eo_loaded, 16)
                    yield
                    yield
                    if r == 0:
                        pool.wait_ge(boost_ready, at(boost_ready, 1))
                        carry()
                        scatter(1, boost)
                        yield
                        yield
                        yield
                    yield
                inverse_std(at, NB, 0)
                yield
                yield
                inverse_std(at, NB, 1)
                for _ in range(6):
                    yield
                pool.wait_ge(dA_ready, at(dA_ready, 1))
                for b in range(G):
                    if b >= 2:
                        pool.wait_ge(seg_psum, at(seg_psum, b - 1))
                    pg.tensor_tensor(R[:, b % 2, :, :], tri[:, :].unsqueeze(1).broadcast_to([128, HM, 128]),
                                     dA[:, b, :].unsqueeze(2).broadcast_to([128, HM, 128]),
                                     ALU.mult).then_inc(r_ready, 1)
                    if b == 1:
                        pool.wait_ge(xh_ready, at(xh_ready, 2))
                        for c in range(G):
                            ins = pg.tensor_tensor(xd[:, c, :, :].rearrange("t k (h p) -> t (k h) p", p=HP),
                                                   xh[:, c, :, :].rearrange("t k (h p) -> t (k h) p", p=HP),
                                                   wr("dskip").unsqueeze(2).broadcast_to([128, HM, HP]), ALU.mult)
                        ins.then_inc(xd_ready, 1)
                    yield
                for _ in range(4):
                    yield
                pool.wait_ge(yss_ready, at(yss_ready, G))
                pg.tensor_tensor(yr[:], yss[:], eps[:, 0:G], ALU.add).then_inc(yr_ready, 1)
                pool.wait_ge(yr_ready, at(yr_ready, 1))
                pg.tensor_tensor(yr[:], yr[:], halfneg[:, 0:G], ALU.pow).then_inc(yr_ready, 1)
                yield
                yield
                pool.wait_ge(r6_step, at(r6_step, 3))
                pg.tensor_tensor(NB.rstd[:], q6[:], halfneg[:, 0:G], ALU.pow).then_inc(NB.rstd_ready, 1)
                pool.wait_ge(x4_ready, at(x4_ready, 1))
                pg.tensor_tensor(X4b[:], X4[:], over_g(wr("bin")), ALU.add).then_inc(xbb_ready, 1)
                for _ in range(4):
                    yield
                inverse_std(at, NB, 3)
                pool.wait_ge(x5_ready, at(x5_ready, 1))
                pg.tensor_tensor(X5b[:], X5[:], over_g(wr("bff2")), ALU.add).then_inc(xbb_ready, 1)
                for _ in range(BACK_STAGES - 63):
                    yield

            run(pool, "Pool", front, back)

        @block.scalar
        def _(act):
            ac = nc.scalar
            act.wait_ge(early, 48)
            ac.activation(neg_a[:], wr("alog"), ACT.Exp).then_inc(const_act, 1)

            def front(g, first):
                at, prev = counter(g), counter(g - 1)

                def copy_xt(k, src, dst=XT):
                    act.wait_ge(NF.xt_psum, at(NF.xt_psum, k + 1))
                    ac.copy(dst[:], src[:, :]).then_inc(NF.xt_ready, 1)

                def part0(n, operand, src):
                    ac.copy(parts[:, operand, 0, :], src).then_inc(part0_ready, 1)

                def part1(n, operand):
                    act.wait_ge(rest_ready, at(rest_ready, n + 1))
                    ac.copy(parts[:, operand, 1, :], rest[:, operand, :]).then_inc(part1_ready, 1)

                def exps(j0, n, scale):
                    for t in range(n + 3):
                        j = t - 2
                        if 0 <= j < n:
                            act.wait_ge(pt_psum, at(pt_psum, j0 + j + 1))
                            if j >= 2:
                                act.wait_ge(pv_done, at(pv_done, j0 + j - 1))
                            ac.activation(PT[:, j % 2, :, :], FB[2][:, :], ACT.Exp, scale=scale).then_inc(pt_ready, 1)
                        yield

                act.wait_ge(c_loaded, at(c_loaded, 16))
                for b in range(G):
                    ac.activation(csq[:, b, :], C[:, b, :], ACT.Square, scale=DC ** -0.5, accum_out=css[:, b:b + 1]
                                  ).then_inc(css_ready, 1)
                yield
                for k in range(2):
                    act.wait_ge(ct_psum, at(ct_psum, k + 1))
                    ac.copy(CT[:, k, :], FB[k][:, :]).then_inc(ct_ready, 1)
                yield
                copy_xt(0, FB[2])
                yield
                act.wait_ge(q_psum, at(q_psum, 1))
                part0(0, 0, FB[3][:, :])
                act.wait_ge(q_psum, at(q_psum, 2))
                part0(1, 1, FB[0][:, :])
                part1(0, 0)
                part1(1, 1)
                yield
                yield
                yield
                yield
                yield from exps(0, H0, D0 ** -0.5)
                yield
                act.wait_ge(at_psum, at(at_psum, 1))
                ac.copy(AT[:], FB[2][:, :]).then_inc(at_ready, 1)
                yield
                yield
                yield
                yield
                copy_xt(1, FB[2])
                yield
                yield
                yield from exps(H0, H1, D1 ** -0.5)
                yield
                act.wait_ge(at_psum, at(at_psum, 2))
                ac.copy(AT[:], FB[0][:, :]).then_inc(at_ready, 1)
                yield
                yield
                yield
                yield
                copy_xt(2, FB[2], XLT)
                yield
                act.wait_ge(lsh_ready, at(lsh_ready, 1))
                ac.activation(lex[:], lsh[:], ACT.Exp).then_inc(lex_ready, 1)
                yield
                yield
                yield
                yield
                yield
                act.wait_ge(dp_psum, at(dp_psum, 1))
                if not first:
                    act.wait_ge(x5_psum, prev(x5_psum, 1))
                ac.copy(dp[:], seqs(FB[1])).then_inc(dp_ready, 1)
                yield

            def back(g):
                at = counter(g)

                def copy_xt(k, src):
                    act.wait_ge(NB.xt_psum, at(NB.xt_psum, k + 1))
                    ac.copy(YNT[:], src[:, :]).then_inc(NB.xt_ready, 1)

                for r in range(2):
                    for k, (a, b) in enumerate(PIECES):
                        act.wait_ge(xg_psum, at(xg_psum, 3 * r + k + 1))
                        ac.copy(xgT[:, a:b, :].rearrange("d j s -> d (j s)"), BB[k][:, 0:SB * (b - a)]
                                ).then_inc(xg_ready, 1)
                        yield
                    for t in range(NBLK + 2):
                        m = r * NBLK + t
                        if t < NBLK and t % 2 == 0:
                            act.wait_ge(h_psum, at(h_psum, m + 1))
                            if m >= 3:
                                act.wait_ge(y_psum, at(y_psum, m - 2))
                            for c in range(EC):
                                b1 = T_B1 + c
                                ins = ac.activation(HS[:, m % 3, c, :], BB[t % 2][:, SB * c:SB * c + SB], ACT.Relu,
                                                    bias=wt[:, m % RING, b1:b1 + 1])
                            ins.then_inc(h_act, 1)
                        yield
                    yield
                    yield
                    if r == 0:
                        yield
                        yield
                        yield
                        yield
                yield
                yield
                yield
                yield
                yield
                copy_xt(0, BB[3])
                yield
                act.wait_ge(xp_psum, at(xp_psum, 1))
                ac.copy(xp[0:64, 2, :, TAPS - 1:], seqs(BB[2])[0:64]).then_inc(xp_ready, 1)
                yield
                for k in range(2):
                    act.wait_ge(xp_psum, at(xp_psum, k + 2))
                    ac.copy(xp[:, k, :, TAPS - 1:], seqs(BB[k])).then_inc(xp_ready, 1)
                act.wait_ge(dt_step, at(dt_step, 2))
                ac.activation(dte[:], dta[:], ACT.Exp).then_inc(dte_ready, 1)
                act.wait_ge(dtw_ready, at(dtw_ready, 1))
                ac.activation(dtl[:], dtw[:], ACT.Ln).then_inc(dtl_ready, 1)
                yield
                for k in range(2):
                    act.wait_ge(z_psum, at(z_psum, k + 1))
                    ac.activation(tz[:, 2 * k:2 * k + 2, :], BB[2 + k][:, :], ACT.Tanh, scale=0.5).then_inc(tz_ready, 1)
                act.wait_ge(conv_step, at(conv_step, 4))
                ac.activation(th[0:64, 2, :, :], u[0:64, 2, :, :], ACT.Tanh, scale=0.5).then_inc(th_ready, 1)
                yield
                for k in range(2):
                    act.wait_ge(conv_step, at(conv_step, 4 * k + 8))
                    ac.activation(th[:, k, :, :], u[:, k, :, :], ACT.Tanh, scale=0.5).then_inc(th_ready, 1)
                yield
                for k in range(2):
                    act.wait_ge(xh_psum, at(xh_psum, k + 1))
                    ac.mul(xh[:, :, k, :], seqs(BB[1 + k]), 0.5).then_inc(xh_ready, 1)
                yield
                for b in range(G):
                    act.wait_ge(seg_psum, at(seg_psum, b + 1))
                    if b >= 2:
                        act.wait_ge(m_ready, at(m_ready, b - 1))
                    ac.activation(EX[:, b % 2, :, :], BB[1 + b % 2][:, :], ACT.Exp).then_inc(ex_ready, 1)
                    yield
                yield
                yield
                act.wait_ge(y_step, at(y_step, 4))
                for b in range(G):
                    ac.activation(ysq[:, b, :], Yz[:, b, :], ACT.Square, scale=DI ** -0.5, accum_out=yss[:, b:b + 1]
                                  ).then_inc(yss_ready, 1)
                for k in range(2):
                    act.wait_ge(yt_psum, at(yt_psum, k + 1))
                    ac.copy(YT[:, k, :], BB[1 + k][:, :]).then_inc(yt_ready, 1)
                yield
                yield
                yield
                yield
                copy_xt(1, BB[0])
                yield
                yield
                yield
                yield
                copy_xt(2, BB[2])
                yield
                yield
                for k in range(4):
                    act.wait_ge(hf_psum, at(hf_psum, k + 1))
                    ac.activation(HF[:, k, :], BB[k % 3][:, :], ACT.Gelu_apprx_tanh,
                                  bias=wp("bff1", k)).then_inc(hf_ready, 1)
                    if k % 2:
                        yield
                yield
                yield

            run(act, "ACT", front, back)

        @block.vector
        def _(dve):
            v = nc.vector
            dve.wait_ge(early, 48)

            def constants():
                dve.wait_ge(once, 48)
                for k in range(2):
                    v.tensor_scalar(woutn[:, k, :], w("mout", k), wp("normw", k), None, ALU.mult).then_inc(const_vec, 1)
                v.tensor_scalar(winn[:], w("win"), wp("gres"), None, ALU.mult).then_inc(const_vec, 1)
                v.tensor_scalar(gb[:], wr("ginit"), float(np.exp(-PATCH_EPS)), None, ALU.mult).then_inc(const_vec, 1)
                dve.wait_ge(const_act, 1)
                v.tensor_scalar(neg_a[:], neg_a[:], -1.0, None, ALU.mult).then_inc(const_vec, 1)
                dve.wait_ge(const_vec, 5)
                dve.wait_ge(const_pool, N_FRONT)

            carried = [0]

            def carry():
                k = carried[0] % 32
                carried[0] += 1
                v.memset(mark[:, k:k + 1], 0.0)

            def statistics(at, N, k, src):
                for b in range(G):
                    v.bn_stats(N.bst[:, b, :], src[:, b, :]).then_inc(N.bn_done, 1)
                dve.wait_ge(N.bn_done, at(N.bn_done, G * (k + 1)))
                carry()
                for b in range(G):
                    v.bn_aggr(N.mv[:, b, :], N.bst[:, b, :]).then_inc(N.mv_ready, 1)
                dve.wait_ge(N.mv_ready, at(N.mv_ready, G * (k + 1)))
                v.tensor_scalar(N.ve[:], N.mv[:, :, 1], LN_EPS, None, ALU.add).then_inc(N.ve_ready, 1)

            def normed(at, N, k, src, dst):
                dve.wait_ge(N.rstd_ready, at(N.rstd_ready, k + 1))
                for b in range(G):
                    ins = v.tensor_scalar(dst[:, b, :], src[:, b, :], N.mv[:, b, 0:1], N.rstd[:, b:b + 1],
                                          ALU.subtract, ALU.mult)
                ins.then_inc(N.xn_ready, 1)

            def front(g, first):
                at, prev = counter(g), counter(g - 1)
                links = [0]

                def link(ins):
                    links[0] += 1
                    ins.then_inc(link_sem, 1)
                    dve.wait_ge(link_sem, at(link_sem, links[0]))

                def attended(n, half, heads, width, last):
                    o = FB[3][:, 0:G * heads * (width + 1)].rearrange("t (b h e) -> t b h e", b=G, h=heads)
                    dve.wait_ge(pv_done, at(pv_done, last))
                    v.reciprocal(rs[:, :, 0:heads], o[:, :, :, width]).then_inc(rs_ready, 1)
                    dve.wait_ge(rs_ready, at(rs_ready, n + 1))
                    c = half * heads * width
                    for b in range(G):
                        ins = v.tensor_tensor(
                            AO[:, b, c:c + heads * width].rearrange("t (h e) -> t h e", h=heads),
                            o[:, b, :, 0:width], rs[:, b, 0:heads].unsqueeze(2).broadcast_to([128, heads, width]),
                            ALU.mult)
                    ins.then_inc(ao_ready, 1)

                def after_part0(n, operand, src):
                    dve.wait_ge(part0_ready, at(part0_ready, n + 1))
                    v.tensor_tensor(rest[:, operand, :], src, parts[:, operand, 0, :], ALU.subtract
                                    ).then_inc(rest_ready, 1)

                def part2(n, operand):
                    dve.wait_ge(part1_ready, at(part1_ready, n + 1))
                    v.tensor_tensor(parts[:, operand, 2, :], rest[:, operand, :], parts[:, operand, 1, :], ALU.subtract
                                    ).then_inc(parts_ready, 1)

                def maxima(j0, n):
                    for t in range(n + 3):
                        if t < n:
                            j = j0 + t
                            sc = seqs(FB[t % 2])
                            m = mx[:, t, :]
                            dve.wait_ge(s_psum, at(s_psum, j + 1))
                            v.tensor_reduce(m, sc, AX.X, ALU.max).then_inc(max_ready, 1)
                            dve.wait_ge(max_ready, at(max_ready, j + 1))
                            if t >= 2:
                                dve.wait_ge(pt_psum, at(pt_psum, j - 1))
                            v.tensor_tensor(SM[:, t % 2, :, :], sc, m.unsqueeze(2).broadcast_to([128, 4, 128]),
                                            ALU.subtract).then_inc(sm_ready, 1)
                        if t == n // 2 + 2:
                            attended(0 if n == H0 else 2, 0, n // 2, D // n, j0 + n // 2)
                        yield

                def slots(upto, total):
                    dims = [128, 2, E, E]
                    link(v.tensor_reduce(ne[:], total.rearrange("p r b e -> p r e b"), AX.X, ALU.add))
                    link(v.tensor_tensor(full[:], ne[:].unsqueeze(3).broadcast_to([128, 2, E, GT // SB]),
                                         filled[:].unsqueeze(1).unsqueeze(1).broadcast_to([128, 2, E, GT // SB]),
                                         ALU.is_gt))
                    link(v.tensor_reduce(nblk[:], full[:], AX.X, ALU.add))
                    link(v.tensor_tensor(endm[:], nblk[:].unsqueeze(2).broadcast_to(dims),
                                         below[:].unsqueeze(1).broadcast_to(dims), ALU.mult))
                    link(v.tensor_reduce(endb[:], endm[:], AX.X, ALU.add))
                    dims = [128, 2, NBLK, E]
                    link(v.tensor_tensor(le[:], endb[:].unsqueeze(2).broadcast_to(dims),
                                         iota_row[:, 0:NBLK].unsqueeze(1).unsqueeze(3).broadcast_to(dims), ALU.is_le))
                    link(v.tensor_reduce(eb[:], le[:], AX.X, ALU.add))
                    link(v.tensor_scalar(eb[:], eb[:], float(E - 1), 128.0, ALU.min, ALU.mult))
                    if not first:
                        dve.wait_ge(eo_loaded, prev(eo_loaded, 2 * G * 16))
                    v.tensor_scalar(rows[:], eb[:], iota_part1[:, 0:1], 1.0, ALU.add, ALU.subtract
                                    ).then_inc(rows_ready, 1)
                    v.tensor_scalar(place[:], eb[:], HID / 128.0, None, ALU.mult).then_inc(place_ready, 1)
                    link(v.tensor_tensor(nblk[:], endb[:], nblk[:], ALU.subtract))
                    link(v.tensor_scalar(start[:, :, 0, :], nblk[:], float(SB), -1.0, ALU.mult, ALU.add))
                    for b in range(1, G):
                        link(v.tensor_tensor(start[:, :, b, :], total[:, :, b - 1, :], start[:, :, b - 1, :], ALU.add))
                    link(v.tensor_tensor(at_e[:], upto, start[:], ALU.add))
                    link(v.tensor_tensor(at_e[:], at_e[:], oh[:], ALU.mult))
                    link(v.tensor_reduce(slot[:], at_e[:], AX.X, ALU.add))
                    v.tensor_copy(pos[:], slot[:]).then_inc(pos_ready, 1)

                dve.wait_ge(x_loaded, at(x_loaded, 16))
                statistics(at, NF, 0, X)
                dve.wait_ge(m_loaded, at(m_loaded, 16))
                v.tensor_scalar(negrow[:], MB[:].rearrange("p b t -> p (b t)"), 0.0, -BIG, ALU.is_equal, ALU.mult
                                ).then_inc(neg_ready, 1)
                yield
                normed(at, NF, 0, X, XN)
                yield
                yield
                dve.wait_ge(css_ready, at(css_ready, G))
                after_part0(0, 0, FB[3][:, :])
                after_part0(1, 1, FB[0][:, :])
                part2(0, 0)
                part2(1, 1)
                yield
                yield
                yield
                if first:
                    constants()
                dve.wait_ge(v_psum, at(v_psum, 1))
                v.tensor_copy(V0[:, :, :, 0:D0].rearrange("t b h e -> t (b h) e"),
                              FB[1][:, :].rearrange("t (n e) -> t n e", e=D0)).then_inc(v_ready, 1)
                yield
                yield from maxima(0, H0)
                attended(1, 1, H0 // 2, D0, H0)
                for i in range(2):
                    dve.wait_ge(k1_psum, at(k1_psum, i + 1))
                    v.scalar_tensor_tensor(KT[:, i, :], FB[i][:, :], wp("bk1", i),
                                           MB[:].rearrange("p b t -> p (b t)"), ALU.add, ALU.mult).then_inc(k1_ready, 1)
                yield
                dve.wait_ge(v1_psum, at(v1_psum, 1))
                dve.wait_ge(mt_loaded, at(mt_loaded, 16))
                v.tensor_tensor(vtmp[:], seqs(FB[0]), MT[:].unsqueeze(2).broadcast_to([128, G, 128]), ALU.mult
                                ).then_inc(v1_part, 1)
                dve.wait_ge(v1_part, at(v1_part, 1))
                dve.wait_ge(bm_ready, at(bm_ready, 1))
                v.tensor_tensor(V1[:, :, :, 0:D1].rearrange("t b h e -> t (b h) e"),
                                vtmp[:].rearrange("t b (h e) -> t (b h) e", e=D1),
                                bm[:].rearrange("t b (h e) -> t (b h) e", e=D1), ALU.add).then_inc(v1_ready, 1)
                yield
                dve.wait_ge(att_psum, at(att_psum, 1))
                dve.wait_ge(xb_ready, at(xb_ready, 1))
                v.tensor_tensor(X1[:], seqs(FB[3]), xb[:], ALU.add).then_inc(x1_ready, 1)
                yield
                dve.wait_ge(x1_ready, at(x1_ready, 1))
                statistics(at, NF, 1, X1)
                yield
                normed(at, NF, 1, X1, XN)
                yield
                yield
                dve.wait_ge(q1_psum, at(q1_psum, 1))
                v.scalar_tensor_tensor(QT, FB[0][:, :], wp("bq1"), MB[:].rearrange("p b t -> p (b t)"),
                                       ALU.add, ALU.mult).then_inc(q1_ready, 1)
                yield
                yield from maxima(H0, H1)
                attended(3, 1, H1 // 2, D1, NJ)
                yield
                yield
                dve.wait_ge(att_psum, at(att_psum, 2))
                dve.wait_ge(xb_ready, at(xb_ready, 2))
                v.tensor_tensor(X2[:], seqs(FB[1]), X1b[:], ALU.add).then_inc(x2_ready, 1)
                yield
                dve.wait_ge(x2_ready, at(x2_ready, 1))
                statistics(at, NF, 2, X2)
                yield
                normed(at, NF, 2, X2, XL)
                yield
                yield
                dve.wait_ge(gate_psum, at(gate_psum, 1))
                link(v.tensor_tensor(lg[:], FB[0][:, 0:G * E].rearrange("t (b e) -> t b e", b=G),
                                     over_g(wr("gateb"), E), ALU.add))
                carry()
                for b in range(G):
                    ins = v.max(top[:, b, :], lg[:, b, :])
                link(ins)
                carry()
                for b in range(G):
                    ins = v.max_index(topi[:, b, :], top[:, b, :], lg[:, b, :])
                v.tensor_tensor(lsh[:], lg[:], top[:, :, 0:1].broadcast_to([128, G, E]), ALU.subtract
                                ).then_inc(lsh_ready, 1)
                link(v.tensor_tensor(l2[:], top[:, :, 1], top[:, :, 0], ALU.subtract))
                link(v.tensor_copy(topf[:], topi[:]))
                for r in range(2):
                    for b in range(G):
                        ins = v.tensor_scalar(oh[:, r, b, :], iota_row[:, 0:E], topf[:, b, r:r + 1], None, ALU.is_equal)
                ins.then_inc(oh_ready, 1)
                dve.wait_ge(l_loaded, at(l_loaded, 16))
                v.tensor_copy(lf[:], LT[:]).then_inc(lf_copied, 1)
                yield
                dve.wait_ge(lex_ready, at(lex_ready, 1))
                link(v.tensor_reduce(lsum[:], lex[:], AX.X, ALU.add))
                link(v.reciprocal(gv[:, 0, :], lsum[:]))
                link(v.tensor_tensor(lsh[:], lex[:], oh[:, 1, :, :], ALU.mult))
                link(v.tensor_reduce(l2[:], lsh[:], AX.X, ALU.add))
                link(v.tensor_tensor(gv[:, 1, :], l2[:], gv[:, 0, :], ALU.mult))
                yield
                dve.wait_ge(cs_psum, at(cs_psum, 1))
                v.tensor_scalar(bi[:], FB[0][:, 0:G], 1.0, None, ALU.subtract).then_inc(bi_step, 1)
                slots(FB[0][:, 64:128].rearrange("p (r b e) -> p r b e", r=2, b=G),
                      FB[0][:, 128:192].rearrange("p (r b e) -> p r b e", r=2, b=G))
                dve.wait_ge(bi_step, at(bi_step, 1))
                v.tensor_scalar(bw[:], bi[:], 0.0, float(S), ALU.is_lt, ALU.mult).then_inc(bi_step, 1)
                dve.wait_ge(bi_step, at(bi_step, 2))
                v.tensor_tensor(bi[:], bi[:], bw[:], ALU.add).then_inc(bi_step, 1)
                dve.wait_ge(bi_step, at(bi_step, 3))
                for b in range(G):
                    ins = v.tensor_scalar(OH[:, b, :], iota_row[:], bi[:, b:b + 1], None, ALU.is_equal)
                ins.then_inc(ohj_ready, 1)
                dve.wait_ge(cr_ready, at(cr_ready, 2))
                for b in range(G):
                    ins = v.scalar_tensor_tensor(cu[:, b, :], C[:, b, 0:128], cr[:, b:b + 1], gb[:], ALU.mult, ALU.mult)
                ins.then_inc(cu_ready, 1)
                yield
                dve.wait_ge(nb_psum, at(nb_psum, 1))
                v.tensor_scalar(bnd[:], FB[0][:, 0:G].unsqueeze(2).broadcast_to([128, G, 128]), 1.0, None,
                                ALU.min).then_inc(bnd_ready, 1)
                yield
                yield
                if not first:
                    dve.wait_ge(x5_psum, prev(x5_psum, 1))
                dve.wait_ge(plug_psum, at(plug_psum, 1))
                v.tensor_scalar(sel[:], seqs(FB[2]), 1.0, iota_part1[:, 0:1], ALU.max, ALU.is_equal
                                ).then_inc(sel_ready, 1)
                yield
                assert links[0] == LINKS, links

            def back(g):
                at = counter(g)

                def weighted(r):
                    for b in range(G):
                        ins = v.scalar_tensor_tensor(f1[:, b, :], eo[:, b, :], gv[:, r, b:b + 1],
                                                     (XL if r == 0 else f1)[:, b, :], ALU.mult, ALU.add)
                    ins.then_inc(f_ready, 1)

                for r in range(2):
                    yield
                    yield
                    yield
                    for t in range(NBLK + 2):
                        m = r * NBLK + t
                        if t < NBLK and t % 2:
                            dve.wait_ge(h_psum, at(h_psum, m + 1))
                            if m >= 3:
                                dve.wait_ge(y_psum, at(y_psum, m - 2))
                            for c in range(EC):
                                b1 = T_B1 + c
                                ins = v.tensor_scalar(HS[:, m % 3, c, :], BB[t % 2][:, SB * c:SB * c + SB],
                                                      wt[:, m % RING, b1:b1 + 1], 0.0, ALU.add, ALU.max)
                            ins.then_inc(h_vec, 1)
                        if t >= 2:
                            m -= 2
                            dve.wait_ge(y_psum, at(y_psum, m + 1))
                            if r == 1 and t == 2:
                                dve.wait_ge(y_stored, at(y_stored, 48))
                            v.tensor_tensor(yo[:, t - 2, :], BB[2 + t % 2][:, 0:D], wt[:, m % RING, T_B2:T_B2 + D],
                                            ALU.add).then_inc(yo_ready, 1)
                        yield
                    yield
                    yield
                    dve.wait_ge(eo_loaded, at(eo_loaded, G * 16 * (r + 1)))
                    if r == 0:
                        v.scalar_tensor_tensor(boost[:], eo[:], 0.5, XL[:], ALU.mult, ALU.add).then_inc(boost_ready, 1)
                        weighted(0)
                        yield
                        yield
                        yield
                        yield
                    else:
                        weighted(1)
                        yield
                dve.wait_ge(f_ready, at(f_ready, 2))
                statistics(at, NB, 0, f1)
                yield
                normed(at, NB, 0, f1, YN)
                dve.wait_ge(NB.xn_ready, at(NB.xn_ready, 1))
                v.tensor_tensor(f1[:], YN[:], over_g(wr("gamma")), ALU.mult).then_inc(gamma_done, 1)
                dve.wait_ge(gamma_done, at(gamma_done, 1))
                dve.wait_ge(xb_ready, at(xb_ready, 3))
                v.tensor_tensor(X3[:], f1[:], X2b[:], ALU.add).then_inc(x3_ready, 1)
                yield
                dve.wait_ge(x3_ready, at(x3_ready, 1))
                statistics(at, NB, 1, X3)
                yield
                normed(at, NB, 1, X3, YN)
                yield
                yield

                def convolve(q, k):
                    n = 128 if k < 2 else 64
                    dve.wait_ge(xp_ready, at(xp_ready, q + 1))
                    uk = u[0:n, k, :, :]
                    cw = P_AT["cw"][0] + TAPS * k
                    v.tensor_scalar(uk, xp[0:n, k, :, 0:S], WP[0:n, cw:cw + 1], wp("cb", k)[0:n], ALU.mult, ALU.add
                                    ).then_inc(conv_step, 1)
                    for i in range(1, TAPS):
                        dve.wait_ge(conv_step, at(conv_step, 4 * q + i))
                        v.scalar_tensor_tensor(uk, xp[0:n, k, :, i:i + S], WP[0:n, cw + i:cw + i + 1], uk,
                                               ALU.mult, ALU.add).then_inc(conv_step, 1)

                dve.wait_ge(dt_psum, at(dt_psum, 1))
                v.tensor_tensor(dtr[:], BB[3][:, 0:G * HM].rearrange("t (b h) -> t b h", b=G),
                                over_g(wr("dtb"), HM), ALU.add).then_inc(dt_step, 1)
                dve.wait_ge(dt_step, at(dt_step, 1))
                v.scalar_tensor_tensor(dta[:], dtr[:], -1.0, dtr[:], ALU.mult, ALU.min).then_inc(dt_step, 1)
                v.tensor_scalar(dtm[:], dtr[:], 0.0, None, ALU.max)
                convolve(0, 2)
                yield
                dve.wait_ge(dte_ready, at(dte_ready, 1))
                v.tensor_scalar(dtw[:], dte[:], 1.0, None, ALU.add).then_inc(dtw_ready, 1)
                dve.wait_ge(dtw_ready, at(dtw_ready, 1))
                v.tensor_scalar(dtd[:], dtw[:], 1.0, None, ALU.subtract).then_inc(dt_step, 1)
                dve.wait_ge(dt_step, at(dt_step, 3))
                v.tensor_scalar(dtz[:], dtd[:], 0.0, None, ALU.is_equal).then_inc(dt_step, 1)
                dve.wait_ge(dt_step, at(dt_step, 4))
                v.tensor_tensor(dtd[:], dtd[:], dtz[:], ALU.add).then_inc(dt_step, 1)
                dve.wait_ge(dt_step, at(dt_step, 5))
                v.reciprocal(dtd[:], dtd[:])
                convolve(1, 0)
                dve.wait_ge(dtl_ready, at(dtl_ready, 1))
                v.tensor_tensor(dtl[:], dtl[:], dtz[:], ALU.add).then_inc(dt_step, 1)
                dve.wait_ge(dt_step, at(dt_step, 6))
                v.tensor_tensor(dtl[:], dtl[:], dtd[:], ALU.mult).then_inc(dt_step, 1)
                dve.wait_ge(dt_step, at(dt_step, 7))
                v.tensor_tensor(dtl[:], dtl[:], dte[:], ALU.mult).then_inc(dt_step, 1)
                dve.wait_ge(dt_step, at(dt_step, 8))
                v.tensor_tensor(dt[:], dtl[:], dtm[:], ALU.add).then_inc(dt_ready, 1)
                dve.wait_ge(dt_ready, at(dt_ready, 1))
                v.tensor_tensor(dA[:], dt[:], over_g(neg_a[:, :], HM), ALU.mult).then_inc(dA_ready, 1)
                yield
                convolve(2, 1)
                for k in range(2):
                    dve.wait_ge(tz_ready, at(tz_ready, k + 1))
                    v.scalar_tensor_tensor(sz[:, 2 * k:2 * k + 2, :], tz[:, 2 * k:2 * k + 2, :], 1.0,
                                           BB[2 + k][:, :].rearrange("t (b c) -> t b c", b=2), ALU.add, ALU.mult
                                           ).then_inc(sz_ready, 1)
                dve.wait_ge(th_ready, at(th_ready, 1))
                v.scalar_tensor_tensor(Bm[:], th[0:NS, 2, :, :], 1.0, u[0:NS, 2, :, :], ALU.add, ALU.mult
                                       ).then_inc(bc_ready, 1)
                v.scalar_tensor_tensor(Cm[:], th[32:32 + NS, 2, :, :], 1.0, u[32:32 + NS, 2, :, :], ALU.add, ALU.mult
                                       ).then_inc(bc_ready, 1)
                yield
                for k in range(2):
                    dve.wait_ge(th_ready, at(th_ready, k + 2))
                    v.scalar_tensor_tensor(xs[:, k, :, :], th[:, k, :, :], 1.0, u[:, k, :, :], ALU.add, ALU.mult
                                           ).then_inc(xs_ready, 1)
                dve.wait_ge(g_psum, at(g_psum, 1))
                v.scalar_tensor_tensor(Gm[:], seqs(BB[0]), 0.25, over_g(tri[:, :]), ALU.mult, ALU.mult
                                       ).then_inc(gm_ready, 1)
                yield
                yield
                dve.wait_ge(gm_ready, at(gm_ready, 1))
                for b in range(G):
                    dve.wait_ge(ex_ready, at(ex_ready, b + 1))
                    if b >= 2:
                        dve.wait_ge(y_done, at(y_done, b - 1))
                    for h in range(HM):
                        ins = v.scalar_tensor_tensor(M[:, b % 2, h, :], EX[:, b % 2, h, :], dt[:, b, h:h + 1],
                                                     Gm[:, b, :], ALU.mult, ALU.mult)
                    ins.then_inc(m_ready, 1)
                    yield
                dve.wait_ge(xd_ready, at(xd_ready, 1))
                for k in range(2):
                    dve.wait_ge(y_done, at(y_done, 2 * k + 2))
                    v.tensor_tensor(Y[:, 2 * k:2 * k + 2, :], BB[[3, 0][k]][:, :].rearrange("t (b c) -> t b c", b=2),
                                    xd[:, 2 * k:2 * k + 2, :, :].rearrange("t b k c -> t b (k c)"), ALU.add
                                    ).then_inc(y_step, 1)
                    if k == 0:
                        yield
                dve.wait_ge(sz_ready, at(sz_ready, 2))
                for k in range(2):
                    dve.wait_ge(y_step, at(y_step, k + 1))
                    v.scalar_tensor_tensor(Yz[:, 2 * k:2 * k + 2, :], Y[:, 2 * k:2 * k + 2, :], 0.5,
                                           sz[:, 2 * k:2 * k + 2, :], ALU.mult, ALU.mult).then_inc(y_step, 1)
                yield
                yield
                dve.wait_ge(mo_psum, at(mo_psum, 1))
                dve.wait_ge(yr_ready, at(yr_ready, 2))
                for b in range(G):
                    ins = v.scalar_tensor_tensor(X4[:, b, :], BB[3][:, cols(b)], yr[:, b:b + 1],
                                                 X3[:, b, :], ALU.mult, ALU.add)
                ins.then_inc(x4_ready, 1)
                yield
                dve.wait_ge(x4_ready, at(x4_ready, 1))
                statistics(at, NB, 2, X4)
                dve.wait_ge(NB.ve_ready, at(NB.ve_ready, 3))
                v.reciprocal(q6[:], NB.ve[:]).then_inc(r6_step, 1)
                dve.wait_ge(r6_step, at(r6_step, 1))
                v.tensor_tensor(q6[:], q6[:], NB.mv[:, :, 1], ALU.mult).then_inc(r6_step, 1)
                dve.wait_ge(r6_step, at(r6_step, 2))
                v.scalar_tensor_tensor(q6[:], q6[:], LN_EPS, NB.ve[:], ALU.add, ALU.mult).then_inc(r6_step, 1)
                yield
                normed(at, NB, 2, X4, YN)
                yield
                yield
                dve.wait_ge(x5_psum, at(x5_psum, 1))
                dve.wait_ge(xbb_ready, at(xbb_ready, 1))
                v.tensor_tensor(X5[:], seqs(BB[1]), X4b[:], ALU.add).then_inc(x5_ready, 1)
                yield
                dve.wait_ge(x5_ready, at(x5_ready, 1))
                statistics(at, NB, 3, X5)
                yield
                normed(at, NB, 3, X5, YN)
                yield
                yield
                dve.wait_ge(p_psum, at(p_psum, 1))
                v.tensor_copy(Pt, BB[3][0:RANK, :]).then_inc(p_ready, 1)
                yield
                yield
                yield
                dve.wait_ge(qf_psum, at(qf_psum, 1))
                v.tensor_copy(Qt, BB[3][0:RANK, :]).then_inc(qf_ready, 1)
                yield
                dve.wait_ge(x6_psum, at(x6_psum, 1))
                dve.wait_ge(xbb_ready, at(xbb_ready, 2))
                dve.wait_ge(stored, at(stored, 1))
                v.tensor_tensor(X6[:], seqs(BB[3]), X5b[:], ALU.add).then_inc(x6_ready, 1)
                yield

            run(dve, "DVE", front, back)

        @block.tensor
        def _(pe):
            mm = nc.tensor.matmul
            pe.wait_ge(early, 48)
            pe.wait_ge(const_pool, N_EARLY)

            def turn(dst, src):
                for b in range(G):
                    ins = nc.tensor.transpose(dst[:, cols(b)], src[:, b, :], ident[:])
                return ins

            def front(g, first):
                at, prev = counter(g), counter(g - 1)

                def attention(j0, n, width, values):
                    for t in range(n + 3):
                        if t < n:
                            dst = FB[t % 2]
                            if n == H0:
                                row = 64 * (t % 2)
                                rows, queries, keys = slice(row, row + NT * D0), QP[:, t // 2, :], KP[:, t // 2, :]
                            else:
                                row = 2 * D1 * (t // 2)
                                rows, queries, keys = slice(row, row + 2 * D1), QT, KT[:, t % 2, :]
                            if t >= 2:
                                pe.wait_ge(sm_ready, at(sm_ready, j0 + t - 1))
                            if n == H1:
                                mm(dst[:, :], ones_bf[row:row + 1, :], negrow[row:row + 1, :], start=True, stop=False,
                                   skip_group_check=True)
                            for b in range(G):
                                ins = mm(dst[:, cols(b)], queries[rows, cols(b)], keys[rows, cols(b)],
                                         start=n == H0, stop=True, skip_group_check=True)
                            ins.then_inc(s_psum, 1)
                        j = t - 2
                        if 0 <= j < n:
                            pe.wait_ge(sm_ready, at(sm_ready, j0 + j + 1))
                            if j >= 1:
                                pe.wait_ge(pt_ready, at(pt_ready, j0 + j))
                            for b in range(G):
                                ins = nc.tensor.transpose(FB[2][:, cols(b)], SM[:, j % 2, b, :], ident[:])
                            ins.then_inc(pt_psum, 1)
                        j = t - 3
                        if j >= 0:
                            pe.wait_ge(pt_ready, at(pt_ready, j0 + j + 1))
                            if j == n // 2:
                                pe.wait_ge(ao_ready, at(ao_ready, 1 if n == H0 else 3))
                            for b in range(G):
                                c = (b * n // 2 + j % (n // 2)) * (width + 1)
                                ins = mm(FB[3][:, c:c + width + 1], PT[:, j % 2, b, :], values[:, b, j, :],
                                         start=True, stop=True)
                            ins.then_inc(pv_done, 1)
                        yield

                pe.wait_ge(c_loaded, at(c_loaded, 16))
                for k in range(2):
                    if k == 1 and not first:
                        pe.wait_ge(dp_ready, prev(dp_ready, 1))
                    for b in range(G):
                        ins = nc.tensor.transpose(FB[k][:, cols(b)], C[:, b, 128 * k:128 * k + 128], ident[:])
                    ins.then_inc(ct_psum, 1)
                yield
                yield
                pe.wait_ge(NF.xn_ready, at(NF.xn_ready, 1))
                if not first:
                    pe.wait_ge(sel_ready, prev(sel_ready, 1))
                turn(FB[2], XN).then_inc(NF.xt_psum, 1)
                yield
                pe.wait_ge(NF.xt_ready, at(NF.xt_ready, 1))
                pe.wait_ge(ct_ready, at(ct_ready, 2))
                mm(FB[3][:, :], w("q0"), XT[:], start=True, stop=True).then_inc(q_psum, 1)
                mm(FB[0][:, :], w("k0"), XT[:], start=True, stop=True).then_inc(q_psum, 1)
                for b in range(G):
                    ins = mm(FB[1][:, cols(b)], XT[:, cols(b)], w("v0"), start=True, stop=True)
                ins.then_inc(v_psum, 1)
                yield
                yield
                yield
                yield
                pe.wait_ge(terms_loaded, at(terms_loaded, 4 * NT * 16))
                pe.wait_ge(v_ready, at(v_ready, 1))
                if first:
                    pe.wait_ge(once, 48)
                    pe.wait_ge(const_vec, 5)
                    pe.wait_ge(const_pool, N_FRONT)
                yield from attention(0, H0, D0, V0)
                for i in range(2):
                    for k in range(2):
                        ins = mm(FB[i][:, :], w("k1", 2 * i + k), CT[:, k, :], start=k == 0, stop=k == 1)
                    ins.then_inc(k1_psum, 1)
                yield
                pe.wait_ge(ao_ready, at(ao_ready, 2))
                turn(FB[2], AO).then_inc(at_psum, 1)
                pe.wait_ge(k1_ready, at(k1_ready, 1))
                for b in range(G):
                    for k in range(2):
                        ins = mm(FB[0][:, cols(b)], CT[:, k, cols(b)], w("v1", k), start=k == 0, stop=k == 1)
                ins.then_inc(v1_psum, 1)
                yield
                pe.wait_ge(at_ready, at(at_ready, 1))
                for b in range(G):
                    ins = mm(FB[3][:, cols(b)], AT[:, cols(b)], w("proj"), start=True, stop=True)
                ins.then_inc(att_psum, 1)
                yield
                yield
                yield
                pe.wait_ge(NF.xn_ready, at(NF.xn_ready, 2))
                turn(FB[2], XN).then_inc(NF.xt_psum, 1)
                yield
                pe.wait_ge(NF.xt_ready, at(NF.xt_ready, 2))
                pe.wait_ge(v1_ready, at(v1_ready, 1))
                mm(FB[0][:, :], w("q1"), XT[:], start=True, stop=True).then_inc(q1_psum, 1)
                yield
                pe.wait_ge(q1_ready, at(q1_ready, 1))
                pe.wait_ge(neg_ready, at(neg_ready, 1))
                yield from attention(H0, H1, D1, V1)
                yield
                pe.wait_ge(ao_ready, at(ao_ready, 4))
                turn(FB[0], AO).then_inc(at_psum, 1)
                yield
                pe.wait_ge(at_ready, at(at_ready, 2))
                for b in range(G):
                    mm(FB[1][:, cols(b)], XT[:, cols(b)], w("out1", 0), start=True, stop=False)
                    ins = mm(FB[1][:, cols(b)], AT[:, cols(b)], w("out1", 1), start=False, stop=True)
                ins.then_inc(att_psum, 1)
                yield
                yield
                yield
                pe.wait_ge(NF.xn_ready, at(NF.xn_ready, 3))
                turn(FB[2], XL).then_inc(NF.xt_psum, 1)
                yield
                pe.wait_ge(NF.xt_ready, at(NF.xt_ready, 3))
                for b in range(G):
                    ins = mm(FB[0][:, E * b:E * b + E], XLT[:, cols(b)], w("gate"), start=True, stop=True)
                ins.then_inc(gate_psum, 1)
                yield
                pe.wait_ge(oh_ready, at(oh_ready, 1))
                mm(FB[0][:, 64:128], tri[:], oh[:].rearrange("t r b e -> t (r b e)"), start=True, stop=True)
                mm(FB[0][:, 128:192], ones_f[:], oh[:].rearrange("t r b e -> t (r b e)"), start=True, stop=True)
                pe.wait_ge(lf_copied, at(lf_copied, 1))
                mm(FB[0][:, 0:G], tri[:], lf[:], start=True, stop=True).then_inc(cs_psum, 1)
                yield
                yield
                pe.wait_ge(ohj_ready, at(ohj_ready, 1))
                for b in range(G):
                    ins = mm(FB[0][:, b:b + 1], OH[:, b, :], ones_bf[:, 0:1], start=True, stop=True)
                ins.then_inc(nb_psum, 1)
                yield
                pe.wait_ge(bnd_ready, at(bnd_ready, 1))
                for b in range(G):
                    ins = mm(FB[2][:, cols(b)], bnd[:, b, :], tri_bf[:], start=True, stop=True)
                ins.then_inc(plug_psum, 1)
                yield
                pe.wait_ge(cu_ready, at(cu_ready, 1))
                if first:
                    pe.wait_ge(const_pool, N_CONST)
                mm(FB[1][:, :], decay[:], cu[:].rearrange("q b c -> q (b c)"), start=True, stop=True
                   ).then_inc(dp_psum, 1)
                yield

            def back(g):
                at = counter(g)

                def relu_done(m):
                    r, j = m // NBLK, m % NBLK
                    if j % 2:
                        pe.wait_ge(h_vec, at(h_vec, r * NO // 2 + j // 2 + 1))
                    else:
                        pe.wait_ge(h_act, at(h_act, r * NE // 2 + j // 2 + 1))

                pe.wait_ge(place_ready, at(place_ready, 1))
                at_expert = [None] * 3
                for r in range(2):
                    for k, (a, b) in enumerate(PIECES):
                        pe.wait_ge(xg_loaded[k], at(xg_loaded[k], 16 * (r + 1)))
                        for j in range(a, b):
                            ins = nc.tensor.transpose(BB[k][:, cols(j - a)], xg[:, j, :], ident[:])
                        ins.then_inc(xg_psum, 1)
                        yield
                    for t in range(NBLK + 2):
                        m = r * NBLK + t
                        if t < NBLK:
                            at_expert[t % 3] = pe.value_load(place[0:1, r, t:t + 1], min_val=0, max_val=(E - 1) * HID)
                            if t == 0:
                                pe.wait_ge(xg_ready, at(xg_ready, 3 * r + 3))
                            if t >= 2:
                                relu_done(m - 2)
                            pe.wait_ge(w_loaded[m % RING], at(w_loaded[m % RING], 16 * (m // RING + 1)))
                            for c in range(EC):
                                ins = mm(BB[t % 2][:, SB * c:SB * c + SB],
                                         wt[:, m % RING, T_W1 + 128 * c:T_W1 + 128 * c + 128], xgT[:, t, :],
                                         start=True, stop=True)
                            ins.then_inc(h_psum, 1)
                        if t >= 2:
                            m -= 2
                            if t >= NBLK:
                                relu_done(m)
                            if t >= 4:
                                pe.wait_ge(yo_ready, at(yo_ready, m - 1))
                            for c in range(EC):
                                ins = mm(BB[2 + t % 2][:, 0:D], HS[:, m % 3, c, :],
                                         w("w2")[:, bass.ds(at_expert[(t - 2) % 3] + 128 * c, 128)],
                                         start=c == 0, stop=c == EC - 1)
                            ins.then_inc(y_psum, 1)
                        yield
                    for _ in range(6 if r == 0 else 3):
                        yield
                yield
                yield
                yield
                yield
                pe.wait_ge(NB.xn_ready, at(NB.xn_ready, 2))
                turn(BB[3], YN).then_inc(NB.xt_psum, 1)
                yield
                pe.wait_ge(NB.xt_ready, at(NB.xt_ready, 1))
                for b in range(G):
                    ins = mm(BB[3][:, HM * b:HM * b + HM], YNT[:, cols(b)], w("dt"), start=True, stop=True)
                ins.then_inc(dt_psum, 1)
                mm(BB[2][:, :], w("bc"), YNT[:], start=True, stop=True).then_inc(xp_psum, 1)
                yield
                for k in range(2):
                    mm(BB[k][:, :], w("xs", k), YNT[:], start=True, stop=True).then_inc(xp_psum, 1)
                yield
                pe.wait_ge(xp_ready, at(xp_ready, 1))
                pe.wait_ge(dt_step, at(dt_step, 1))
                for k in range(2):
                    for b in range(2):
                        ins = mm(BB[2 + k][:, DI * b:DI * b + DI], YNT[:, cols(2 * k + b)], w("z"),
                                 start=True, stop=True)
                    ins.then_inc(z_psum, 1)
                yield
                pe.wait_ge(bc_ready, at(bc_ready, 2))
                pe.wait_ge(xp_ready, at(xp_ready, 2))
                for b in range(G):
                    ins = mm(BB[0][:, cols(b)], Bm[:, b, :], Cm[:, b, :], start=True, stop=True)
                ins.then_inc(g_psum, 1)
                yield
                pe.wait_ge(sz_ready, at(sz_ready, 1))
                pe.wait_ge(xp_ready, at(xp_ready, 3))
                for k in range(2):
                    pe.wait_ge(xs_ready, at(xs_ready, 1 + k))
                    turn(BB[1 + k], xs[:, k, :, :]).then_inc(xh_psum, 1)
                yield
                pe.wait_ge(xh_ready, at(xh_ready, 2))
                pe.wait_ge(sz_ready, at(sz_ready, 2))
                pe.wait_ge(gm_ready, at(gm_ready, 1))
                for t in range(G + 2):
                    if t < G:
                        pe.wait_ge(r_ready, at(r_ready, t + 1))
                        if t >= 2:
                            pe.wait_ge(ex_ready, at(ex_ready, t - 1))
                        mm(BB[1 + t % 2][:, :], after[:], R[:, t % 2, :, :].rearrange("u h t -> u (h t)"), start=True,
                           stop=True).then_inc(seg_psum, 1)
                    b = t - 1
                    if 0 <= b < G:
                        pe.wait_ge(m_ready, at(m_ready, b + 1))
                        for h in range(HM):
                            c = 256 * (b % 2) + HP * h
                            ins = mm(BB[[3, 0][b // 2]][:, c:c + HP], M[:, b % 2, h, :],
                                     xh[:, b, h // 2, HP * (h % 2):HP * (h % 2) + HP], start=True, stop=True)
                        ins.then_inc(y_done, 1)
                    yield
                pe.wait_ge(y_step, at(y_step, 4))
                for k in range(2):
                    turn(BB[1 + k], Yz[:, :, 128 * k:128 * k + 128]).then_inc(yt_psum, 1)
                yield
                pe.wait_ge(yt_ready, at(yt_ready, 2))
                for b in range(G):
                    for k in range(2):
                        ins = mm(BB[3][:, cols(b)], YT[:, k, cols(b)], woutn[:, k, :], start=k == 0, stop=k == 1)
                ins.then_inc(mo_psum, 1)
                yield
                yield
                yield
                pe.wait_ge(NB.xn_ready, at(NB.xn_ready, 3))
                turn(BB[0], YN).then_inc(NB.xt_psum, 1)
                yield
                pe.wait_ge(NB.xt_ready, at(NB.xt_ready, 2))
                pe.wait_ge(dp_ready, at(dp_ready, 1))
                pe.wait_ge(sel_ready, at(sel_ready, 1))
                for b in range(G):
                    mm(BB[1][:, cols(b)], YNT[:, cols(b)], winn[:], start=True, stop=False)
                    ins = mm(BB[1][:, cols(b)], sel[:, b, :], dp[:, b, :], start=False, stop=True)
                ins.then_inc(x5_psum, 1)
                yield
                yield
                yield
                pe.wait_ge(NB.xn_ready, at(NB.xn_ready, 4))
                turn(BB[2], YN).then_inc(NB.xt_psum, 1)
                yield
                pe.wait_ge(NB.xt_ready, at(NB.xt_ready, 3))
                mm(BB[3][0:RANK, :], w("u1"), YNT[:], start=True, stop=True).then_inc(p_psum, 1)
                yield
                pe.wait_ge(p_ready, at(p_ready, 1))
                for k in range(4):
                    if k == 3:
                        pe.wait_ge(hf_ready, at(hf_ready, 1))
                    mm(BB[k % 3][:, :], V1w[:, 128 * k:128 * k + 128], Pt, start=True, stop=True
                       ).then_inc(hf_psum, 1)
                    if k % 2:
                        yield
                for k in range(4):
                    pe.wait_ge(hf_ready, at(hf_ready, k + 1))
                    ins = mm(BB[3][0:RANK, :], w("u2", k, RANK), HF[:, k, :], start=k == 0, stop=k == 3)
                ins.then_inc(qf_psum, 1)
                yield
                pe.wait_ge(qf_ready, at(qf_ready, 1))
                for b in range(G):
                    ins = mm(BB[3][:, cols(b)], Qt[:, cols(b)], V2w[:], start=True, stop=True)
                ins.then_inc(x6_psum, 1)
                yield

            run(pe, "PE", front, back)


def layout(i):
    f = np.float32
    Wt = np.zeros((128, W_N), f)
    Pc = np.zeros((128, P_N), f)

    def put(name, a, k=0):
        at = W_AT[name][0] + k
        Wt[:a.shape[0], at:at + a.shape[1]] = a

    def col(name, a, k=0):
        Pc[:a.shape[0], P_AT[name][0] + k] = a

    qkv = np.zeros((128, 384), f)
    proj = np.zeros((128, 128), f)
    for n in range(8):
        qkv[16 * n:16 * n + 16, 48 * n:48 * n + 48] = i["L0_attn_w_qkv"][n]
        proj[16 * n:16 * n + 16, 16 * n:16 * n + 16] = i["L0_attn_w_proj"][n]
    put("q0", qkv[:, 0:128])
    put("k0", qkv[:, 128:256])
    put("v0", qkv[:, 256:384])
    put("proj", proj)
    src, tgt = i["L0_xattn_W_src"].T, i["L0_xattn_W_tgt"].T
    for h in range(H1):
        mine = slice(D1 * h, D1 * h + D1)
        for k in range(2):
            put("k1", src[128 * k:128 * k + 128, mine], 128 * (2 * (h % 2) + k) + D1 * h)
        Pc[mine, P_AT["bk1"][0] + h % 2] = i["L0_xattn_b_src"][mine]
    put("q1", tgt)
    col("bq1", i["L0_xattn_b_tgt"])
    w_out = i["L0_xattn_W_out"].T
    for k in range(2):
        put("v1", src[128 * k:128 * k + 128, 128:], 128 * k)
        put("out1", w_out[128 * k:128 * k + 128], 128 * k)
    put("gate", i["L0_ffn_gate_W"])
    for e in range(E):
        for c in range(EC):
            put("w2", i["L0_ffn_W2"][e, 128 * c:128 * c + 128], 128 * (EC * e + c))
    table = np.concatenate([
        i["L0_ffn_W1"],
        i["L0_ffn_b1"].reshape(E, EC, 128).transpose(0, 2, 1),
        np.broadcast_to(i["L0_ffn_b2"][:, None, :], (E, 128, 128))], axis=2).reshape(E * 128, T_N)
    m_in = i["L1_attn_W_in"].T
    put("z", m_in[:, 0:DI])
    put("xs", m_in[:, DI:2 * DI])
    put("bc", m_in[:, 2 * DI:2 * DI + NS], 0)
    put("bc", m_in[:, 2 * DI + NS:2 * DI + 2 * NS], 32)
    put("dt", m_in[:, 2 * DI + 2 * NS:])
    cw, cb = i["L1_attn_conv_w"], i["L1_attn_conv_b"]
    for k, (rows, at) in enumerate([(slice(0, 128), 0), (slice(128, 256), 0), (slice(256, 272), 0)]):
        n = rows.stop - rows.start
        c = P_AT["cw"][0] + TAPS * k
        Pc[at:at + n, c:c + TAPS] = cw[rows]
        Pc[at:at + n, P_AT["cb"][0] + k] = cb[rows]
    c = P_AT["cw"][0] + TAPS * 2
    Pc[32:32 + NS, c:c + TAPS] = cw[272:288]
    Pc[32:32 + NS, P_AT["cb"][0] + 2] = cb[272:288]
    m_out = i["L1_attn_W_out"].T
    for k in range(2):
        put("mout", m_out[128 * k:128 * k + 128], 128 * k)
        col("normw", i["L1_attn_norm_w"][128 * k:128 * k + 128], k)
    put("win", i["L1_xattn_W_in"].T)
    col("gres", i["L1_xattn_g_res"])
    put("u1", i["L1_ffn_U1"])
    for k in range(4):
        put("u2", i["L1_ffn_U2"][128 * k:128 * k + 128], RANK * k)
        col("bff1", i["L1_ffn_b1"][128 * k:128 * k + 128], k)
    rows = [i["L0_attn_b_proj"], i["L0_xattn_b_src"][128:], i["L0_xattn_b_out"], i["L0_ffn_gate_b"],
            i["L0_ffn_ln_gamma"], i["L0_ffn_ln_beta"], i["L1_attn_dt_bias"], i["L1_attn_A_log"], i["L1_attn_D"],
            i["L1_xattn_b_in"], i["L1_xattn_g_init"][:128], i["L1_ffn_b2"]]
    Rr = np.ascontiguousarray(np.broadcast_to(np.concatenate(rows), (128, R_N)))
    return Wt, Pc, Rr, table, i["L1_ffn_V1"], i["L1_ffn_V2"]


def kernel(**inputs):
    import concourse.bacc as bacc
    from concourse.bass_utils import run_bass_kernel_spmd

    i = {k: np.asarray(a) for k, a in inputs.items()}
    arrays = [i["x"], i["ctx_2048"], i["mask_BxS2_fk1"], i["mask_BxS2_fk1"].T, i["mask_BxS2_if0"].T, *layout(i)]
    names = ["x", "ctx", "mask", "mask_t", "lens_t", "w", "wp", "wr", "experts", "v1", "v2"]
    nc = bacc.Bacc("TRN2", target_bir_lowering=False, num_devices=1)
    feed, args = {}, []
    for name, a in zip(names, arrays):
        a = np.ascontiguousarray(a)
        feed[f"in_{name}"] = a
        args.append(nc.dram_tensor(f"in_{name}", a.shape, mybir.dt.from_np(a.dtype), kind="ExternalInput").ap())
    args.append(nc.dram_tensor("out", (B, S, D), F32, kind="ExternalOutput").ap())
    build(nc, *args)
    r = run_bass_kernel_spmd(nc, [feed], core_ids=[0])
    return r.results[0]["out"]
```
